# Optimizing a Trainium2 kernel written in Bass

```python
import numpy as np
import jax
import jax.numpy as jnp

def _softmax(x, axis=-1):
    return jax.nn.softmax(x, axis=axis)

def _gelu(x):
    return jax.nn.gelu(x, approximate=True)

def _silu(x):
    return jax.nn.silu(x)

def _sigmoid(x):
    return jax.nn.sigmoid(x)

def _layernorm(x, axis=-1, eps=1e-05):
    m = jnp.mean(x, axis=axis, keepdims=True)
    v = jnp.var(x, axis=axis, keepdims=True)
    return (x - m) / jnp.sqrt(v + eps)

def _scatter_add(tgt, idx, src, axis=0):
    return tgt.at[idx].add(src)

def _segment_sum(src, seg, n):
    return jax.ops.segment_sum(src, seg, n)
kernel_name = 'mk_flamingo_gated_d2_seqx_r4_77de40'

def setup_inputs(seed: int=0):
    np.random.seed(seed)
    _w = jnp.asarray

    def _rec_inputs():
        import jax
        import jax.numpy as jnp
        _rk = jax.random.key(seed)
        x = 7.22e-05 + 1 * jax.random.normal(jax.random.fold_in(_rk, 1), (128, 128, 256), jnp.float32)
        _lenS = 128 - jax.random.randint(jax.random.fold_in(_rk, 7), (128,), 0, max(1, 128 // 4) + 1, jnp.int32)
        _lenS2 = 128 - jax.random.randint(jax.random.fold_in(_rk, 8), (128,), 0, max(1, 128 // 4) + 1, jnp.int32)
        _ctx_1024P = jax.random.normal(jax.random.fold_in(_rk, 11), (128, 16, 256), jnp.float32)
        _ctx_1024c = jax.random.dirichlet(jax.random.fold_in(_rk, 511), 0.3 * jnp.ones((16,), jnp.float32), (128, 128))
        _ctx_1024t = jnp.einsum('bsk,bkd->bsd', _ctx_1024c, _ctx_1024P)
        _ctx_1024t = _ctx_1024t * jax.lax.rsqrt(jnp.mean(jnp.square(_ctx_1024t)) + 1e-12) * 0.953939
        ctx_1024 = 4.13588e-05 + 0.999923 * (_ctx_1024t + 0.3 * jax.random.normal(jax.random.fold_in(_rk, 611), (128, 128, 256), jnp.float32))
        _validS = jnp.arange(128)[None, :] < _lenS[:, None]
        _validS2 = jnp.arange(128)[None, :] < _lenS2[:, None]
        _causal = jnp.tril(jnp.ones((128, 128), dtype=bool))
        mask_Bx1x1xS2_ik0 = jnp.where(jnp.broadcast_to(_validS2[:, None, None, :], (128, 1, 1, 128)), 0, 1).astype(jnp.int32)
        _g = jax.random.normal(jax.random.fold_in(_rk, 9001), (2, 2), jnp.float32)
        _g = jnp.sign(_g) * jnp.maximum(jnp.abs(_g), 1.0) + (_g == 0) * 1.0
        g_xattn = _g[0]
        g_ffn = _g[1]
        return (x, ctx_1024, mask_Bx1x1xS2_ik0, g_xattn, g_ffn)
    x, ctx_1024, mask_Bx1x1xS2_ik0, g_xattn, g_ffn = _rec_inputs()

    def _L0_xattn_setup():
        import jax, jax.numpy as jnp
        import numpy as np
        BS, SEQ, D_MODEL, N_HEADS = (4, 512, 256, 16)
        D_HEAD = D_MODEL // N_HEADS

        def _split_heads(x):
            b, s, _ = x.shape
            return x.reshape(b, s, N_HEADS, D_HEAD).transpose(0, 2, 1, 3)
        key = jax.random.key(seed)
        ks = jax.random.split(key, 12)
        s = 1.0 / np.sqrt(D_MODEL)
        return {'Q': jax.random.normal(ks[0], (BS, SEQ, D_MODEL), jnp.float32), 'K': jax.random.normal(ks[1], (BS, SEQ, D_MODEL), jnp.float32), 'V': jax.random.normal(ks[2], (BS, SEQ, D_MODEL), jnp.float32), 'mask': jax.random.randint(ks[3], (BS, 1, 1, SEQ), 0, 2, jnp.int32), 'Wq': jax.random.normal(ks[4], (D_MODEL, D_MODEL), jnp.float32) * s, 'bq': jnp.zeros((D_MODEL,), jnp.float32), 'Wk': jax.random.normal(ks[5], (D_MODEL, D_MODEL), jnp.float32) * s, 'bk': jnp.zeros((D_MODEL,), jnp.float32), 'Wv': jax.random.normal(ks[6], (D_MODEL, D_MODEL), jnp.float32) * s, 'bv': jnp.zeros((D_MODEL,), jnp.float32), 'Wo': jax.random.normal(ks[7], (D_MODEL, D_MODEL), jnp.float32) * s, 'bo': jnp.zeros((D_MODEL,), jnp.float32)}
    _L0_xattn_all = _L0_xattn_setup()
    _L0_xattn_in = {k: v for k, v in _L0_xattn_all.items() if k in ('Wq', 'bq', 'Wk', 'bk', 'Wv', 'bv', 'Wo', 'bo')}
    del _L0_xattn_all

    def _L0_ffn_setup():
        import jax, jax.numpy as jnp
        import numpy as np
        N_EXPERTS = 8
        CAP_FACTOR = 1.25
        BATCH, SEQ, DMODEL, DFF = (4, 512, 256, 1024)
        key = jax.random.key(seed)
        k0, k1, k2, k3 = jax.random.split(key, 4)
        x = jax.random.normal(k0, (BATCH, SEQ, DMODEL), dtype=jnp.float32)
        Wr = jax.random.normal(k1, (DMODEL, N_EXPERTS), dtype=jnp.float32) * 0.02
        W1 = jax.random.normal(k2, (N_EXPERTS, DMODEL, DFF), dtype=jnp.float32) * 0.02
        W2 = jax.random.normal(k3, (N_EXPERTS, DFF, DMODEL), dtype=jnp.float32) * 0.02
        return {'x': x, 'Wr': Wr, 'W1': W1, 'W2': W2}
    _L0_ffn_all = _L0_ffn_setup()
    _L0_ffn_in = {k: v for k, v in _L0_ffn_all.items() if k in ('Wr', 'W1', 'W2')}
    del _L0_ffn_all

    def _L1_xattn_setup():
        import math
        import jax, jax.numpy as jnp
        import numpy as np
        H = 16
        D_MODEL = 256
        DK = D_MODEL // H
        K_FACTOR = 2

        def _time_delay_agg_inference(v, corr):
            B, _, _, L = v.shape
            top_k = min(int(K_FACTOR * math.log(L)), L)
            mean_value = jnp.mean(corr, axis=(1, 2))
            weights, delay = jax.lax.top_k(mean_value, top_k)
            tmp_corr = jax.nn.softmax(weights, axis=-1)
            idx = (delay[:, :, None] + jnp.arange(L)) % L
            gathered = jnp.take_along_axis(v[:, None], idx[:, :, None, None, :], axis=-1)
            return jnp.einsum('bk,bkhdl->bhdl', tmp_corr, gathered)
        key = jax.random.key(seed)
        ks = jax.random.split(key, 11)
        B, L, D = (4, 512, D_MODEL)
        s = 1.0 / math.sqrt(D)
        return {'queries': jax.random.normal(ks[0], (B, L, D), jnp.float32), 'keys': jax.random.normal(ks[1], (B, L, D), jnp.float32), 'values': jax.random.normal(ks[2], (B, L, D), jnp.float32), 'Wq': jax.random.normal(ks[3], (D, H * DK), jnp.float32) * s, 'bq': jnp.zeros((H * DK,), jnp.float32), 'Wk': jax.random.normal(ks[4], (D, H * DK), jnp.float32) * s, 'bk': jnp.zeros((H * DK,), jnp.float32), 'Wv': jax.random.normal(ks[5], (D, H * DK), jnp.float32) * s, 'bv': jnp.zeros((H * DK,), jnp.float32), 'Wo': jax.random.normal(ks[6], (H * DK, D), jnp.float32) * s, 'bo': jnp.zeros((D,), jnp.float32)}
    _L1_xattn_all = _L1_xattn_setup()
    _L1_xattn_in = {k: v for k, v in _L1_xattn_all.items() if k in ('Wq', 'bq', 'Wk', 'bk', 'Wv', 'bv', 'Wo', 'bo')}
    del _L1_xattn_all

    def _L1_ffn_setup():
        import jax, jax.numpy as jnp
        import numpy as np
        EPS = 1e-06
        LN_EPS = 1e-05

        def _absmean_core(W):
            gamma = jnp.mean(jnp.abs(W)) + EPS
            Ws = W / gamma
            Wq = jnp.sign(Ws) * jnp.minimum(jnp.round(jnp.abs(Ws)), 1.0)
            return (Wq, gamma)

        @jax.custom_vjp
        def absmean(W):
            return _absmean_core(W)[0]

        def _absmean_fwd(W):
            Wq, gamma = _absmean_core(W)
            return (Wq, gamma)

        def _absmean_bwd(gamma, g):
            return (g / gamma,)
        absmean.defvjp(_absmean_fwd, _absmean_bwd)

        def layernorm(x, w, b, eps=LN_EPS):
            mu = jnp.mean(x, axis=-1, keepdims=True)
            var = jnp.mean((x - mu) ** 2, axis=-1, keepdims=True)
            return (x - mu) * jax.lax.rsqrt(var + eps) * w + b
        key = jax.random.key(seed)
        k1, k2, k3 = jax.random.split(key, 3)
        d, h = (256, 1024)
        B, T = (8, 512)
        return {'x': jax.random.normal(k1, (B, T, d), jnp.float32), 'W_fc': jax.random.normal(k2, (h, d), jnp.float32), 'ln_w': jnp.ones((h,), jnp.float32), 'ln_b': jnp.zeros((h,), jnp.float32), 'W_proj': jax.random.normal(k3, (d, h), jnp.float32)}
    _L1_ffn_all = _L1_ffn_setup()
    _L1_ffn_in = {k: v for k, v in _L1_ffn_all.items() if k in ('W_fc', 'ln_w', 'ln_b', 'W_proj')}
    del _L1_ffn_all
    return {'x': x, 'ctx_1024': ctx_1024, 'mask_Bx1x1xS2_ik0': mask_Bx1x1xS2_ik0, 'g_xattn': g_xattn, 'g_ffn': g_ffn, 'L0_xattn_Wq': _L0_xattn_in['Wq'], 'L0_xattn_bq': _L0_xattn_in['bq'], 'L0_xattn_Wk': _L0_xattn_in['Wk'], 'L0_xattn_bk': _L0_xattn_in['bk'], 'L0_xattn_Wv': _L0_xattn_in['Wv'], 'L0_xattn_bv': _L0_xattn_in['bv'], 'L0_xattn_Wo': _L0_xattn_in['Wo'], 'L0_xattn_bo': _L0_xattn_in['bo'], 'L0_ffn_Wr': _L0_ffn_in['Wr'], 'L0_ffn_W1': _L0_ffn_in['W1'], 'L0_ffn_W2': _L0_ffn_in['W2'], 'L1_xattn_Wq': _L1_xattn_in['Wq'], 'L1_xattn_bq': _L1_xattn_in['bq'], 'L1_xattn_Wk': _L1_xattn_in['Wk'], 'L1_xattn_bk': _L1_xattn_in['bk'], 'L1_xattn_Wv': _L1_xattn_in['Wv'], 'L1_xattn_bv': _L1_xattn_in['bv'], 'L1_xattn_Wo': _L1_xattn_in['Wo'], 'L1_xattn_bo': _L1_xattn_in['bo'], 'L1_ffn_W_fc': _L1_ffn_in['W_fc'], 'L1_ffn_ln_w': _L1_ffn_in['ln_w'], 'L1_ffn_ln_b': _L1_ffn_in['ln_b'], 'L1_ffn_W_proj': _L1_ffn_in['W_proj']}

def reference(x, ctx_1024, mask_Bx1x1xS2_ik0, g_xattn, g_ffn, L0_xattn_Wq, L0_xattn_bq, L0_xattn_Wk, L0_xattn_bk, L0_xattn_Wv, L0_xattn_bv, L0_xattn_Wo, L0_xattn_bo, L0_ffn_Wr, L0_ffn_W1, L0_ffn_W2, L1_xattn_Wq, L1_xattn_bq, L1_xattn_Wk, L1_xattn_bk, L1_xattn_Wv, L1_xattn_bv, L1_xattn_Wo, L1_xattn_bo, L1_ffn_W_fc, L1_ffn_ln_w, L1_ffn_ln_b, L1_ffn_W_proj):
    import jax
    import jax.numpy as jnp

    def _L0_xattn_ref(Q, K, V, mask, Wq, bq, Wk, bk, Wv, bv, Wo, bo):
        import jax, jax.numpy as jnp
        import numpy as np
        BS, SEQ, D_MODEL, N_HEADS = (4, 512, 256, 16)
        D_HEAD = D_MODEL // N_HEADS

        def _split_heads(x):
            b, s, _ = x.shape
            return x.reshape(b, s, N_HEADS, D_HEAD).transpose(0, 2, 1, 3)
        q = _split_heads(Q @ Wq.T + bq)
        k = _split_heads(K @ Wk.T + bk)
        v = _split_heads(V @ Wv.T + bv)
        scores = jnp.einsum('bhqd,bhkd->bhqk', q, k) / np.sqrt(D_HEAD).astype(np.float32)
        scores = jnp.where(mask == 0, jnp.float32(-1000000000.0), scores)
        attn = jax.nn.softmax(scores, axis=-1)
        ctx = jnp.einsum('bhqk,bhkd->bhqd', attn, v)
        b, h, s, d = ctx.shape
        ctx = ctx.transpose(0, 2, 1, 3).reshape(b, s, h * d)
        return ctx @ Wo.T + bo

    def _L0_ffn_ref(x, Wr, W1, W2):
        import jax, jax.numpy as jnp
        import numpy as np
        N_EXPERTS = 8
        CAP_FACTOR = 1.25
        BATCH, SEQ, DMODEL, DFF = (4, 512, 256, 1024)
        B, S, D = x.shape
        E = W1.shape[0]
        cap = int(CAP_FACTOR * B * S / E)
        t = x.reshape(-1, D)
        probs = jax.nn.softmax(t @ Wr, axis=-1)
        idx = jnp.argmax(probs, axis=-1)
        pmax = jnp.max(probs, axis=-1)
        onehot = jax.nn.one_hot(idx, E, dtype=jnp.int32)
        pos = jnp.sum(jnp.cumsum(onehot, axis=0) * onehot, axis=-1) - 1
        kept = pos < cap
        flat = idx * cap + jnp.minimum(pos, cap - 1)
        disp = jnp.zeros((E * cap, D), t.dtype).at[flat].add(t * kept[:, None].astype(t.dtype))
        ein = disp.reshape(E, cap, D)
        h = jax.nn.relu(jnp.einsum('ecd,edf->ecf', ein, W1))
        eout = jnp.einsum('ecf,efd->ecd', h, W2).reshape(E * cap, D)
        comb = jnp.where(kept[:, None], eout[flat], t)
        factor = jnp.where(kept, pmax, jnp.ones_like(pmax))
        out = (comb * factor[:, None]).reshape(B, S, D)
        return out

    def _L1_xattn_ref(queries, keys, values, Wq, bq, Wk, bk, Wv, bv, Wo, bo):
        import math
        import jax, jax.numpy as jnp
        import numpy as np
        H = 16
        D_MODEL = 256
        DK = D_MODEL // H
        K_FACTOR = 2

        def _time_delay_agg_inference(v, corr):
            B, _, _, L = v.shape
            top_k = min(int(K_FACTOR * math.log(L)), L)
            mean_value = jnp.mean(corr, axis=(1, 2))
            weights, delay = jax.lax.top_k(mean_value, top_k)
            tmp_corr = jax.nn.softmax(weights, axis=-1)
            idx = (delay[:, :, None] + jnp.arange(L)) % L
            gathered = jnp.take_along_axis(v[:, None], idx[:, :, None, None, :], axis=-1)
            return jnp.einsum('bk,bkhdl->bhdl', tmp_corr, gathered)
        B, Lq, _ = queries.shape
        Lk = keys.shape[1]
        q = (queries @ Wq + bq).reshape(B, Lq, H, DK)
        k = (keys @ Wk + bk).reshape(B, Lk, H, DK)
        v = (values @ Wv + bv).reshape(B, Lk, H, DK)
        if Lq > Lk:
            pad = ((0, 0), (0, Lq - Lk), (0, 0), (0, 0))
            k = jnp.pad(k, pad)
            v = jnp.pad(v, pad)
        else:
            k = k[:, :Lq]
            v = v[:, :Lq]
        qt = jnp.transpose(q, (0, 2, 3, 1))
        kt = jnp.transpose(k, (0, 2, 3, 1))
        vt = jnp.transpose(v, (0, 2, 3, 1))
        qf = jnp.fft.rfft(qt)
        kf = jnp.fft.rfft(kt)
        c = qf.real * kf.real + 1j * -(qf.imag * kf.imag)
        corr = jnp.fft.irfft(c, n=Lq).astype(qt.dtype)
        agg = _time_delay_agg_inference(vt, corr)
        out = jnp.transpose(agg, (0, 3, 1, 2)).reshape(B, Lq, H * DK)
        return out @ Wo + bo

    def _L1_ffn_ref(x, W_fc, ln_w, ln_b, W_proj):
        import jax, jax.numpy as jnp
        import numpy as np
        EPS = 1e-06
        LN_EPS = 1e-05

        def _absmean_core(W):
            gamma = jnp.mean(jnp.abs(W)) + EPS
            Ws = W / gamma
            Wq = jnp.sign(Ws) * jnp.minimum(jnp.round(jnp.abs(Ws)), 1.0)
            return (Wq, gamma)

        @jax.custom_vjp
        def absmean(W):
            return _absmean_core(W)[0]

        def _absmean_fwd(W):
            Wq, gamma = _absmean_core(W)
            return (Wq, gamma)

        def _absmean_bwd(gamma, g):
            return (g / gamma,)
        absmean.defvjp(_absmean_fwd, _absmean_bwd)

        def layernorm(x, w, b, eps=LN_EPS):
            mu = jnp.mean(x, axis=-1, keepdims=True)
            var = jnp.mean((x - mu) ** 2, axis=-1, keepdims=True)
            return (x - mu) * jax.lax.rsqrt(var + eps) * w + b
        h = jnp.einsum('btd,hd->bth', x, absmean(W_fc))
        h = jax.nn.gelu(h, approximate=False)
        h = layernorm(h, ln_w, ln_b)
        return jnp.einsum('bth,dh->btd', h, absmean(W_proj))
    x = x + jnp.tanh(g_xattn[0]) * _L0_xattn_ref(_layernorm(x, axis=-1), ctx_1024, ctx_1024, mask_Bx1x1xS2_ik0, L0_xattn_Wq, L0_xattn_bq, L0_xattn_Wk, L0_xattn_bk, L0_xattn_Wv, L0_xattn_bv, L0_xattn_Wo, L0_xattn_bo)
    x = x + jnp.tanh(g_ffn[0]) * _L0_ffn_ref(_layernorm(x, axis=-1), L0_ffn_Wr, L0_ffn_W1, L0_ffn_W2)
    x = x + jnp.tanh(g_xattn[1]) * _L1_xattn_ref(_layernorm(x, axis=-1), ctx_1024, ctx_1024, L1_xattn_Wq, L1_xattn_bq, L1_xattn_Wk, L1_xattn_bk, L1_xattn_Wv, L1_xattn_bv, L1_xattn_Wo, L1_xattn_bo)
    x = x + jnp.tanh(g_ffn[1]) * _L1_ffn_ref(_layernorm(x, axis=-1), L1_ffn_W_fc, L1_ffn_ln_w, L1_ffn_ln_b, L1_ffn_W_proj)
    return x

_drawn_inputs = setup_inputs


def setup_inputs(seed=0):
    import zlib

    import numpy as np

    out = dict(_drawn_inputs(seed))
    spreads = {'g_ffn': (-1.0, 0.2),
     'L0_xattn_bq': (0.0, 0.1),
     'L0_xattn_bk': (0.0, 0.1),
     'L0_xattn_bv': (0.0, 0.1),
     'L0_xattn_bo': (0.0, 0.1),
     'L1_xattn_bq': (0.0, 0.1),
     'L1_xattn_bk': (0.0, 0.1),
     'L1_xattn_bv': (0.0, 0.1),
     'L1_xattn_bo': (0.0, 0.1),
     'L1_ffn_ln_w': (1.0, 0.2),
     'L1_ffn_ln_b': (0.0, 0.1)}
    factors = {}
    for name, (base, spread) in spreads.items():
        noise = np.random.default_rng([zlib.crc32(name.encode()), seed]).standard_normal(out[name].shape)
        drawn = base * np.exp(spread * noise) if base else spread * noise
        out[name] = jnp.asarray(drawn.astype(out[name].dtype))
    for name, factor in factors.items():
        out[name] = (out[name] * factor).astype(out[name].dtype)
    return out
```

```python
from contextlib import ExitStack

import numpy as np

import concourse.bass as bass
from concourse import mybir

F32 = mybir.dt.float32
BF16 = mybir.dt.bfloat16
I32 = mybir.dt.int32
U32 = mybir.dt.uint32
ALU = mybir.AluOpType
ACT = mybir.ActivationFunctionType
AX = mybir.AxisListType

P = 128
D = 256
DC = D // P
H = 16
DH = D // H
HC = H // DC
UNIT = 4
NU = H // UNIT
E = 8
FF = 1024
FC = FF // P
TOPK = 9
LN_EPS = 1e-5
MASK_PARTS = (-998244352.0, -1753088.0, -2560.0)
LOWEST = -3.0e38


def steps(eng, n):
    yield 0, 0, 0
    yield 1, 1, 0
    if n > 4:
        with eng.Fori(0, (n - 4) // 2) as j:
            yield 2 * j + 2, 0, j + 1
            yield 2 * j + 3, 1, j + 1
    yield n - 2, 0, (n - 2) // 2
    yield n - 1, 1, (n - 2) // 2


def first(b, k):
    return isinstance(b, int) and b < k


def last(b, n, k):
    return isinstance(b, int) and b >= n - k


def two_on(b, p, u):
    return (b, p, u + 2) if u + 2 < NU else (b + 1, 1 - p, u + 2 - NU)


def one_back(b, p, u):
    return (b, p, u - 1) if u else (b - 1, 1 - p, NU - 1)


def quads(eng, n):
    for r in range(4):
        yield r, r, 0
    if n > 8:
        with eng.Fori(1, n // 4 - 1) as j:
            for r in range(4):
                yield 4 * j + r, r, j
    for r in range(4):
        yield n - 4 + r, r, n // 4 - 1


class Kernel:
    pass


def new_signal(nc, K, name):
    K.signals.append(nc.alloc_semaphore(name=name))
    return K.signals[-1]


def end_stage(nc, K):
    nc.clear_and_free_semaphores(K.signals)
    nc.all_engine_barrier()
    K.signals = []


def setup(nc, ctx, K):
    def sb(name, shape, dt=F32):
        return ctx.enter_context(nc.sbuf_tensor(name, shape, dt))

    def sem(name):
        return ctx.enter_context(nc.semaphore(name))

    n = K.n
    K.xres = sb("xres", [P, n * D])
    K.ident = sb("ident", [P, P])
    K.ones = sb("ones", [P, P])
    K.gates = sb("gates", [P, 4])
    K.logits = sb("logits", [P, n, E])
    K.ln2 = sb("ln2", [P, n, 2])
    K.slot = sb("slot", [P, n], U32)
    K.read = sb("read", [P, n], U32)
    K.wexp = sb("wexp", [P, n])
    K.wself = sb("wself", [P, n])
    K.half = sb("half", [P, 1])

    made = sem("const_made")
    loaded = sem("gates_loaded")
    gated = sem("gated")
    K.passed = sem("passed")
    with nc.Block() as block:

        @block.gpsimd
        def _(pool):
            pool.memset(K.ident[:, :], 0.0).then_inc(made, 1)
            pool.wait_ge(made, 1)
            pool.memset(K.ones[:, :], 1.0).then_inc(made, 1)
            pool.memset(K.half[:, :], -0.5).then_inc(made, 1)
            pool.affine_select(out=K.ident[:, :], in_=K.ident[:, :], compare_op=ALU.not_equal, fill=1.0,
                               base=0, pattern=[[-1, P]], channel_multiplier=1).then_inc(made, 1)
            pool.wait_ge(made, 4)

        @block.sync
        def _(sp):
            sp.dma_start(K.gates[:, 0:2], K.g_xattn.partition_broadcast(P)).then_inc(loaded, 16)
            sp.dma_start(K.gates[:, 2:4], K.g_ffn.partition_broadcast(P)).then_inc(loaded, 16)

        @block.scalar
        def _(act):
            act.wait_ge(loaded, 32)
            act.activation(K.gates[:, :], K.gates[:, :], ACT.Tanh).then_inc(gated, 1)
            act.wait_ge(gated, 1)


def transpose_square(pe, bank, rows, ident):
    for ki in range(DC):
        for ko in range(DC):
            mm = pe.transpose(bank[:, ki * D + ko * P:ki * D + (ko + 1) * P],
                              rows[:, ko, ki * P:(ki + 1) * P], ident[:, :])
    return mm


def cross_attention(nc, ctx, K):

    def sb(name, shape, dt=F32):
        return ctx.enter_context(nc.sbuf_tensor(name, shape, dt))

    def psum(name):
        return ctx.enter_context(nc.psum_tensor(name, [P, 512], F32))

    def sem(name):
        return new_signal(nc, K, "a_" + name)

    n = K.n
    g = K.gates[:, 0:1]
    wq, wk, wv, wo = (sb(f"a_w{c}T", [P, DC, D]) for c in "qkvo")
    wr = sb("a_wr", [P, DC, E])
    bq = sb("a_bq", [P, DC])
    bk = sb("a_bk", [P, DC])
    bv = sb("a_bv", [P, DC])
    gbias = sb("a_gbias", [P, D])
    headmask = sb("a_headmask", [P, HC, P])
    ones3 = sb("a_ones3", [3, P], BF16)
    parts = sb("a_parts", [3, 1])
    zeros = sb("a_zeros", [P, 1024])

    banks = [psum(f"a_bank{i}") for i in range(8)]
    sbank, tbank, pvbank, fbank, qkbank, bbank = banks[0:2], banks[2:4], banks[4], banks[5], banks[6], banks[7]

    w_loaded = sem("w_loaded")
    w_turned = sem("w_turned")
    w_ready = sem("w_ready")
    bias_mm = sem("bias_mm")
    hm = sem("headmask")
    zero_made = sem("zero_made")

    with ExitStack() as prep, nc.Block() as block:
        raw = prep.enter_context(nc.sbuf_tensor("a_raw", [P, 4, DC, D], F32))
        bvb = prep.enter_context(nc.sbuf_tensor("a_bvb", [P, DC, P], F32))
        bob = prep.enter_context(nc.sbuf_tensor("a_bob", [P, D], F32))

        @block.sync
        def _(sp):
            for i, w in enumerate((K.Wq0, K.Wk0, K.Wv0, K.Wo0)):
                sp.dma_start(raw[:, i], w.rearrange("(c p) d -> p c d", p=P)).then_inc(w_loaded, 16)
            sp.dma_start(wr[:, :, :], K.Wr.rearrange("(c p) e -> p c e", p=P)).then_inc(w_loaded, 16)
            for t, v in ((bq, K.bq0), (bk, K.bk0), (bv, K.bv0)):
                sp.dma_start(t[:, :], v.rearrange("(c p) -> p c", p=P), allow_slow_non_contiguous=True).then_inc(w_loaded, 16)
            sp.dma_start(bob[:, :], K.bo0.partition_broadcast(P)).then_inc(w_loaded, 16)
            sp.dma_start(parts[:, :], K.mask_parts).then_inc(w_loaded, 16)

        @block.gpsimd
        def _(pool):
            pool.memset(headmask[:, :, :], 1.0).then_inc(hm, 1)
            pool.memset(ones3[:, :], 1.0).then_inc(hm, 1)
            pool.wait_ge(hm, 1)
            pool.affine_select(out=headmask[:, :, :], in_=headmask[:, :, :], compare_op=ALU.is_ge, fill=0.0,
                               base=0, pattern=[[-DH, HC], [0, P]], channel_multiplier=1).then_inc(hm, 1)
            pool.wait_ge(hm, 3)
            pool.affine_select(out=headmask[:, :, :], in_=headmask[:, :, :], compare_op=ALU.is_ge, fill=0.0,
                               base=DH - 1, pattern=[[DH, HC], [0, P]], channel_multiplier=-1).then_inc(hm, 1)
            pool.wait_ge(hm, 4)

        @block.tensor
        def _(pe):
            pe.wait_ge(w_loaded, 16 * 10)
            for i in range(4):
                transpose_square(pe, banks[i], raw[:, i], K.ident).then_inc(w_turned, 1)
            pe.wait_ge(w_ready, 5)
            for c in range(DC):
                mm = pe.matmul(banks[4][:, 0:D], bvb[:, c, :], wo[:, c, :], start=c == 0, stop=c == DC - 1)
            mm.then_inc(bias_mm, 1)

        @block.vector
        def _(dve):
            dve.memset(zeros[:, :], 0.0).then_inc(zero_made, 1)
            dve.wait_ge(w_loaded, 16 * 10)
            for c in range(DC):
                cc = dve.tensor_scalar(bvb[:, c, :], K.ones[:, :], bv[:, c:c + 1], None, ALU.mult)
            cc.then_inc(w_ready, 1)
            for i, w in enumerate((wq, wk, wv, wo)):
                dve.wait_ge(w_turned, i + 1)
                dve.tensor_copy(w[:, :, :].rearrange("p c d -> p (c d)"), banks[i][:, :]).then_inc(w_ready, 1)
            dve.wait_ge(bias_mm, 1)
            dve.tensor_tensor(gbias[:, :], banks[4][:, 0:D], bob[:, :], ALU.add).then_inc(w_ready, 1)
            dve.wait_ge(w_ready, 6)
            dve.tensor_scalar(gbias[:, :], gbias[:, :], g, None, ALU.mult).then_inc(w_ready, 1)
            dve.wait_ge(w_ready, 7)

    xin = sb("a_xin", [P, 2, D])
    cin = sb("a_cin", [P, 2, D])
    min_ = sb("a_mask", [P, 2, P], I32)
    xhat = sb("a_xhat", [P, D])
    keep = sb("a_keep", [P, P])
    inv = sb("a_inv", [3, P])
    madd = sb("a_madd", [3, 2, P], BF16)
    ft = sb("a_ft", [P, 2 * D])
    qT = sb("a_qT", [P, 2, DC, P])
    kT = sb("a_kT", [P, DC, P])
    km = sb("a_km", [P, 2, H, P])
    va = sb("a_va", [P, 2, H, DH + 1])
    negm = sb("a_negm", [P, 2, UNIT])
    mx = sb("a_mx", [P, 2, UNIT])
    pr = sb("a_pr", [P, 2, UNIT, P])
    pT = sb("a_pT", [P, 2, UNIT, P])
    rden = sb("a_rden", [P, H])
    co = sb("a_co", [P, D])
    coT = sb("a_coT", [P, D])
    st1, st2 = sb("a_st1", [P, 6]), sb("a_st2", [P, 6])
    mv1, mv2 = sb("a_mv1", [P, 2]), sb("a_mv2", [P, 2])
    ve1, ve2 = sb("a_ve1", [P, 1]), sb("a_ve2", [P, 1])
    rs1, rs2 = sb("a_rs1", [P, 1]), sb("a_rs2", [P, 1])
    t = sb("a_t", [P, D])
    tT = sb("a_tT", [P, D])

    ld = [sem("ld0"), sem("ld1")]
    zeroed = sem("zeroed")
    bn1, mv1s, ve1s, rs1s = sem("bn1"), sem("mv1"), sem("ve1"), sem("rs1")
    bn2, mv2s, ve2s, rs2s, ln2s = sem("bn2"), sem("mv2"), sem("ve2"), sem("rs2"), sem("ln2")
    pre = sem("preadded")
    invs, madds, keeps = sem("inv"), sem("madd"), sem("keep")
    xhs, fts_mm, fts = sem("xhat"), sem("ft_mm"), sem("ft")
    qkmm, vmm = sem("qk_mm"), sem("v_mm")
    qs, ks, vs, kms = sem("q"), sem("k"), sem("v"), sem("km")
    smm, mxs, negs, exps = sem("scores"), sem("max"), sem("negmax"), sem("exp")
    tmm, pTd, pTa = sem("pt_mm"), sem("pt_dve"), sem("pt_act")
    pvs, rdens, cos, cot_mm, cots = sem("pv"), sem("rden"), sem("co"), sem("coT_mm"), sem("coT")
    ymm, xress, ts, tt_mm, tts, lgmm, lgs = (sem("y_mm"), sem("xres"), sem("t"), sem("tT_mm"), sem("tT"),
                                             sem("logit_mm"), sem("logit"))
    ones_set = sem("ones_set")

    xv, cv = K.x, K.ctx
    mask = K.mask.rearrange("b x y s -> (b x y) s")
    scale = DH ** -0.5

    with nc.Block() as block:

        @block.sync
        def _(sp):
            for b, p, h in steps(sp, n):
                if not first(b, 2):
                    sp.wait_ge(xhs, b - 1)
                    sp.wait_ge(pre, b - 1)
                    sp.wait_ge(fts_mm, b - 1)
                    sp.wait_ge(keeps, b - 1)
                    sp.wait_ge(invs, b - 1)
                sp.dma_start(xin[:, p, :], xv[bass.ds(b, 1)].rearrange("a p d -> p (a d)")).then_inc(ld[p], 16)
                sp.dma_start(cin[:, p, :], cv[bass.ds(b, 1)].rearrange("a p d -> p (a d)")).then_inc(ld[p], 16)
                sp.dma_start(min_[:, p, :], mask[bass.ds(b, 1), :].rearrange("a s -> (a s)").partition_broadcast(P)
                             ).then_inc(ld[p], 16)
                if isinstance(b, int) and b == 1:
                    for r in range(0, E * K.cap, 512):
                        rows = min(512, E * K.cap - r)
                        sp.dma_start(K.disp[r:r + rows, :].rearrange("(p k) d -> p (k d)", p=P),
                                     zeros[:, 0:rows * D // P]).then_inc(zeroed, 16)
            sp.wait_ge(zeroed, 16 * (-(-E * K.cap // 512)))

        @block.gpsimd
        def _(pool):
            def front(b, p, h):
                pool.wait_ge(mv1s, b + 1)
                pool.sem_inc(K.passed, 1)
                pool.tensor_scalar(ve1[:, :], mv1[:, 1:2], LN_EPS, 1.0, ALU.add, ALU.mult).then_inc(ve1s, 1)
                pool.wait_ge(ve1s, b + 1)
                if not first(b, 1):
                    pool.wait_ge(xhs, b)
                pool.tensor_tensor(rs1[:, :], ve1[:, :], K.half[:, :], ALU.pow).then_inc(rs1s, 1)
                pool.wait_ge(ld[p], 48 * h + 48)
                pool.tensor_tensor(K.xres[:, bass.ds(b * D, D)], xin[:, p, :], gbias[:, :], ALU.add
                                   ).then_inc(pre, 1)

            def keys(b, p):
                pool.wait_ge(ks, b + 1)
                if not first(b, 2):
                    pool.wait_ge(smm, (b - 1) * NU)
                for c in range(DC):
                    pool.tensor_tensor(km[:, p, c * HC:(c + 1) * HC, :],
                                       kT[:, c, :].unsqueeze(1).broadcast_to([P, HC, P]),
                                       headmask[:, :, :], ALU.mult).then_inc(kms, 1)

            def after(b):
                pool.wait_ge(mv2s, b + 1)
                pool.sem_inc(K.passed, 1)
                pool.tensor_scalar(ve2[:, :], mv2[:, 1:2], LN_EPS, 1.0, ALU.add, ALU.mult).then_inc(ve2s, 1)
                pool.wait_ge(ve2s, b + 1)
                if not first(b, 1):
                    pool.wait_ge(ts, b)
                pool.tensor_tensor(rs2[:, :], ve2[:, :], K.half[:, :], ALU.pow).then_inc(rs2s, 1)
                pool.sem_inc(K.passed, 1)
                pool.tensor_copy(K.ln2[:, bass.ds(b, 1), 0:1].rearrange("p a c -> p (a c)"),
                                 mv2[:, 0:1]).then_inc(ln2s, 1)
                pool.wait_ge(rs2s, b + 1)
                pool.sem_inc(K.passed, 1)
                pool.tensor_copy(K.ln2[:, bass.ds(b, 1), 1:2].rearrange("p a c -> p (a c)"),
                                 rs2[:, :]).then_inc(ln2s, 1)

            front(0, 0, 0)
            keys(0, 0)
            front(1, 1, 0)
            for b, p, h in steps(pool, n):
                if not last(b, n, 1):
                    keys(b + 1, 1 - p)
                if not last(b, n, 2):
                    front(b + 2, p, h + 1)
                if not first(b, 1):
                    after(b - 1)
            after(n - 1)
            pool.wait_ge(ln2s, 2 * n)

        @block.tensor
        def _(pe):
            def turn_inputs(b, p, h):
                pe.wait_ge(xhs, b + 1)
                pe.wait_ge(ld[p], 48 * h + 48)
                if not first(b, 1):
                    pe.wait_ge(vs, b)
                for c in range(DC):
                    pe.transpose(fbank[:, c * P:(c + 1) * P], xhat[:, c * P:(c + 1) * P], K.ident[:, :])
                for c in range(DC):
                    mm = pe.transpose(fbank[:, D + c * P:D + (c + 1) * P], cin[:, p, c * P:(c + 1) * P],
                                      K.ident[:, :])
                mm.then_inc(fts_mm, 1)

            def project_qk(b):
                pe.wait_ge(fts, b + 1)
                if not first(b, 1):
                    pe.wait_ge(qs, b)
                    pe.wait_ge(ks, b)
                for o, (w, src) in enumerate(((wq, 0), (wk, D))):
                    for m in range(DC):
                        for c in range(DC):
                            mm = pe.matmul(qkbank[:, o * D + m * P:o * D + (m + 1) * P],
                                           w[:, c, m * P:(m + 1) * P], ft[:, src + c * P:src + (c + 1) * P],
                                           start=c == 0, stop=c == DC - 1)
                mm.then_inc(qkmm, 1)

            def project_v(b):
                pe.wait_ge(fts, b + 1)
                for c in range(DC):
                    mm = pe.matmul(fbank[:, 0:D], ft[:, D + c * P:D + (c + 1) * P], wv[:, c, :],
                                   start=c == 0, stop=c == DC - 1)
                mm.then_inc(vmm, 1)

            def scores(b, p, u):
                c = u * UNIT // HC
                if u == 0:
                    pe.wait_ge(qs, b + 1)
                    pe.wait_ge(madds, b + 1)
                pe.wait_ge(kms, b * DC + c + 1)
                if u >= 2:
                    pe.wait_ge(exps, b * NU + u - 1)
                elif not first(b, 1):
                    pe.wait_ge(exps, b * NU + u - 1)
                pe.matmul(sbank[u % 2][:, :], ones3[:, :],
                          madd[:, p, :].unsqueeze(1).broadcast_to([3, UNIT, P]), start=True, stop=False)
                pe.matmul(sbank[u % 2][:, :], qT[:, p, c, :], km[:, p, u * UNIT:(u + 1) * UNIT, :],
                          start=False, stop=True).then_inc(smm, 1)

            def turn_probs(b, u):
                pe.wait_ge(exps, b * NU + u + 1)
                if not first(b, 1) or u >= 2:
                    half = 2 * b + u // 2
                    pe.wait_ge(pTd if u % 2 == 0 else pTa, half)
                for j in range(UNIT):
                    mm = pe.transpose(tbank[u % 2][:, j * P:(j + 1) * P], pr[:, u % 2, j, :], K.ident[:, :])
                mm.then_inc(tmm, 1)

            def weigh(b, p, u):
                pe.wait_ge(pTd if u % 2 == 0 else pTa, 2 * b + u // 2 + 1)
                if u == 0:
                    pe.wait_ge(vs, b + 1)
                    if not first(b, 1):
                        pe.wait_ge(cos, b)
                for j in range(UNIT):
                    hh = u * UNIT + j
                    mm = pe.matmul(pvbank[:, hh * (DH + 1):(hh + 1) * (DH + 1)], pT[:, u % 2, j, :],
                                   va[:, p, hh, :], start=True, stop=True)
                mm.then_inc(pvs, 1)

            def turn_context(b):
                pe.wait_ge(cos, b + 1)
                if not first(b, 1):
                    pe.wait_ge(lgs, b)
                for c in range(DC):
                    mm = pe.transpose(bbank[:, c * P:(c + 1) * P], co[:, c * P:(c + 1) * P], K.ident[:, :])
                mm.then_inc(cot_mm, 1)

            def out_project(b):
                pe.wait_ge(cots, b + 1)
                for c in range(DC):
                    mm = pe.matmul(bbank[:, D:2 * D], coT[:, c * P:(c + 1) * P], wo[:, c, :],
                                   start=c == 0, stop=c == DC - 1)
                mm.then_inc(ymm, 1)

            def turn_t(b):
                pe.wait_ge(ts, b + 1)
                for c in range(DC):
                    mm = pe.transpose(bbank[:, D + c * P:D + (c + 1) * P], t[:, c * P:(c + 1) * P],
                                      K.ident[:, :])
                mm.then_inc(tt_mm, 1)

            def route(b):
                pe.wait_ge(tts, b + 1)
                for c in range(DC):
                    mm = pe.matmul(bbank[:, 0:E], tT[:, c * P:(c + 1) * P], wr[:, c, :],
                                   start=c == 0, stop=c == DC - 1)
                mm.then_inc(lgmm, 1)

            turn_inputs(0, 0, 0)
            project_qk(0)
            project_v(0)
            turn_inputs(1, 1, 0)
            scores(0, 0, 0)
            scores(0, 0, 1)
            for b, p, h in steps(pe, n):
                for u in range(NU):
                    if u < 2 or not last(b, n, 1):
                        scores(*two_on(b, p, u))
                    if u == 0 and not last(b, n, 1):
                        project_qk(b + 1)
                    if u == 2 and not first(b, 1):
                        turn_context(b - 1)
                    if u == 3 and not first(b, 1):
                        out_project(b - 1)
                    turn_probs(b, u)
                    if u or not first(b, 1):
                        weigh(*one_back(b, p, u))
                    if u == 0 and not last(b, n, 1):
                        project_v(b + 1)
                    if u == 0 and not first(b, 2):
                        turn_t(b - 2)
                    if u == 1 and not first(b, 2):
                        route(b - 2)
                    if u == 3 and not last(b, n, 2):
                        turn_inputs(b + 2, p, h + 1)
            weigh(n - 1, 1, NU - 1)
            turn_t(n - 2)
            route(n - 2)
            turn_context(n - 1)
            out_project(n - 1)
            turn_t(n - 1)
            route(n - 1)

        @block.scalar
        def _(act):
            def exp_unit(b, u):
                act.wait_ge(negs, b * NU + u + 1)
                if u >= 2 or not first(b, 1):
                    act.wait_ge(tmm, b * NU + u - 1)
                for j in range(UNIT):
                    ex = act.activation(pr[:, u % 2, j, :], sbank[u % 2][:, j * P:(j + 1) * P], ACT.Exp,
                                        bias=negm[:, u % 2, j:j + 1], scale=scale)
                ex.then_inc(exps, 1)

            def inputs_out(b):
                act.wait_ge(fts_mm, b + 1)
                if not first(b, 1):
                    act.wait_ge(vmm, b)
                act.activation(ft[:, :], fbank[:, :], ACT.Copy).then_inc(fts, 1)

            def q_out(b, p):
                act.wait_ge(ks, b + 1)
                if not first(b, 2):
                    act.wait_ge(smm, (b - 1) * NU)
                for c in range(DC):
                    cp = act.activation(qT[:, p, c, :], qkbank[:, c * P:(c + 1) * P], ACT.Identity,
                                        bias=bq[:, c:c + 1])
                cp.then_inc(qs, 1)

            def probs_out(b, u):
                act.wait_ge(tmm, b * NU + u + 1)
                if u >= 2 or not first(b, 1):
                    act.wait_ge(pvs, b * NU + u - 1)
                act.activation(pT[:, u % 2, :, :].rearrange("p a k -> p (a k)"), tbank[u % 2][:, :],
                               ACT.Copy).then_inc(pTa, 1)

            def context_out(b):
                act.wait_ge(cot_mm, b + 1)
                if not first(b, 1):
                    act.wait_ge(ymm, b)
                act.activation(coT[:, :], bbank[:, 0:D], ACT.Copy).then_inc(cots, 1)

            def t_out(b):
                act.wait_ge(tt_mm, b + 1)
                if not first(b, 1):
                    act.wait_ge(lgmm, b)
                act.activation(tT[:, :], bbank[:, D:2 * D], ACT.Copy).then_inc(tts, 1)

            inputs_out(0)
            q_out(0, 0)
            inputs_out(1)
            exp_unit(0, 0)
            exp_unit(0, 1)
            for b, p, h in steps(act, n):
                for u in range(NU):
                    if u == 1 and not last(b, n, 1):
                        q_out(b + 1, 1 - p)
                    if u == 1 and not first(b, 2):
                        t_out(b - 2)
                    if u == 2 and not first(b, 1):
                        context_out(b - 1)
                    if u % 2 == 1:
                        probs_out(b, u)
                    if u < 2 or not last(b, n, 1):
                        b2, _, u2 = two_on(b, p, u)
                        exp_unit(b2, u2)
                    if u == 3 and not last(b, n, 2):
                        inputs_out(b + 2)
            t_out(n - 2)
            context_out(n - 1)
            t_out(n - 1)

        @block.vector
        def _(dve):
            def stats(b, p, h):
                dve.wait_ge(ld[p], 48 * h + 48)
                dve.sem_inc(K.passed, 1)
                dve.bn_stats(st1[:, :], xin[:, p, :]).then_inc(bn1, 1)
                dve.wait_ge(bn1, b + 1)
                if not first(b, 1):
                    dve.wait_ge(ve1s, b)
                dve.sem_inc(K.passed, 1)
                dve.bn_aggr(mv1[:, :], st1[:, :]).then_inc(mv1s, 1)
                dve.tensor_scalar(inv[:, :], min_[0:3, p, :], 0.0, None, ALU.is_equal).then_inc(invs, 1)
                if not first(b, 1):
                    dve.wait_ge(ks, b)
                dve.tensor_scalar(keep[:, :], min_[:, p, :], 0.0, None, ALU.not_equal).then_inc(keeps, 1)
                dve.wait_ge(invs, b + 1)
                if not first(b, 2):
                    dve.wait_ge(smm, (b - 1) * NU)
                dve.tensor_scalar(madd[:, p, :], inv[:, :], parts[:, 0:1], None, ALU.mult).then_inc(madds, 1)

            def normalise_in(b, p):
                dve.wait_ge(rs1s, b + 1)
                if not first(b, 1):
                    dve.wait_ge(fts_mm, b)
                dve.tensor_scalar(xhat[:, :], xin[:, p, :], mv1[:, 0:1], rs1[:, 0:1], ALU.subtract, ALU.mult
                                  ).then_inc(xhs, 1)

            def unit_max(b, u):
                dve.wait_ge(smm, b * NU + u + 1)
                dve.tensor_reduce(mx[:, u % 2, :], sbank[u % 2][:, :].rearrange("p (a k) -> p a k", k=P),
                                  AX.X, ALU.max).then_inc(mxs, 1)
                dve.wait_ge(mxs, b * NU + u + 1)
                if u >= 2 or not first(b, 1):
                    dve.wait_ge(exps, b * NU + u - 1)
                dve.tensor_scalar(negm[:, u % 2, :], mx[:, u % 2, :], -scale, None, ALU.mult).then_inc(negs, 1)

            def probs_out(b, u):
                dve.wait_ge(tmm, b * NU + u + 1)
                if u >= 2 or not first(b, 1):
                    dve.wait_ge(pvs, b * NU + u - 1)
                dve.tensor_copy(pT[:, u % 2, :, :].rearrange("p a k -> p (a k)"), tbank[u % 2][:, :]
                                ).then_inc(pTd, 1)

            def k_out(b):
                dve.wait_ge(qkmm, b + 1)
                if not first(b, 1):
                    dve.wait_ge(kms, b * DC)
                for c in range(DC):
                    cp = dve.scalar_tensor_tensor(kT[:, c, :], qkbank[:, D + c * P:D + (c + 1) * P],
                                                  bk[:, c:c + 1], keep[:, :], ALU.add, ALU.mult)
                cp.then_inc(ks, 1)

            def v_out(b, p):
                dve.wait_ge(vmm, b + 1)
                if not first(b, 2):
                    dve.wait_ge(pvs, (b - 1) * NU)
                dve.tensor_copy(va[:, p, :, 0:DH], fbank[:, 0:D].rearrange("p (h d) -> p h d", d=DH)
                                ).then_inc(vs, 1)

            def context(b):
                dve.wait_ge(pvs, (b + 1) * NU)
                pv = pvbank[:, 0:H * (DH + 1)].rearrange("p (h d) -> p h d", d=DH + 1)
                dve.reciprocal(rden[:, :], pv[:, :, DH]).then_inc(rdens, 1)
                dve.wait_ge(rdens, b + 1)
                if not first(b, 1):
                    dve.wait_ge(cot_mm, b)
                dve.tensor_tensor(co[:, :].rearrange("p (h d) -> p h d", d=DH), pv[:, :, 0:DH],
                                  rden[:, :].unsqueeze(2).broadcast_to([P, H, DH]), ALU.mult).then_inc(cos, 1)

            def residual(b):
                dve.wait_ge(ymm, b + 1)
                dve.wait_ge(pre, b + 1)
                row = K.xres[:, bass.ds(b * D, D)]
                dve.scalar_tensor_tensor(row, bbank[:, D:2 * D], g, row, ALU.mult, ALU.add).then_inc(xress, 1)
                dve.wait_ge(xress, b + 1)
                dve.sem_inc(K.passed, 1)
                dve.bn_stats(st2[:, :], row).then_inc(bn2, 1)
                dve.wait_ge(bn2, b + 1)
                if not first(b, 1):
                    dve.wait_ge(ve2s, b)
                    dve.wait_ge(ln2s, 2 * b)
                dve.sem_inc(K.passed, 1)
                dve.bn_aggr(mv2[:, :], st2[:, :]).then_inc(mv2s, 1)

            def normalise_out(b):
                dve.wait_ge(rs2s, b + 1)
                if not first(b, 1):
                    dve.wait_ge(tt_mm, b)
                dve.tensor_scalar(t[:, :], K.xres[:, bass.ds(b * D, D)], mv2[:, 0:1], rs2[:, 0:1],
                                  ALU.subtract, ALU.mult).then_inc(ts, 1)

            def logits_out(b):
                dve.wait_ge(lgmm, b + 1)
                dve.tensor_copy(K.logits[:, bass.ds(b, 1), :].rearrange("p a e -> p (a e)"), bbank[:, 0:E]
                                ).then_inc(lgs, 1)

            for p in range(2):
                ins = dve.memset(va[:, p, :, DH:DH + 1], 1.0)
            ins.then_inc(ones_set, 1)
            stats(0, 0, 0)
            normalise_in(0, 0)
            k_out(0)
            v_out(0, 0)
            stats(1, 1, 0)
            normalise_in(1, 1)
            unit_max(0, 0)
            unit_max(0, 1)
            for b, p, h in steps(dve, n):
                for u in range(NU):
                    if u == 0 and not first(b, 2):
                        normalise_out(b - 2)
                    if u < 2 or not last(b, n, 1):
                        b2, _, u2 = two_on(b, p, u)
                        unit_max(b2, u2)
                    if u == 0 and not last(b, n, 1):
                        k_out(b + 1)
                    if u % 2 == 0:
                        probs_out(b, u)
                    if u == 0 and not first(b, 1):
                        context(b - 1)
                    if u == 0 and not last(b, n, 1):
                        v_out(b + 1, 1 - p)
                    if u == 1 and not last(b, n, 2):
                        stats(b + 2, p, h + 1)
                    if u == 1 and not first(b, 2):
                        logits_out(b - 2)
                    if u == 2 and not last(b, n, 2):
                        normalise_in(b + 2, p)
                    if u == 3 and not first(b, 1):
                        residual(b - 1)
            context(n - 1)
            normalise_out(n - 2)
            logits_out(n - 2)
            residual(n - 1)
            normalise_out(n - 1)
            logits_out(n - 1)
            dve.wait_ge(lgs, n)


def assign_slots(nc, ctx, K):
    n = K.n
    ne = n * E

    def sb(name, shape, dt=F32):
        return ctx.enter_context(nc.sbuf_tensor("b_" + name, shape, dt))

    def sem(name):
        return new_signal(nc, K, "b_" + name)

    rank = sb("rank", [P, E])
    start = sb("start", [P, E])
    spare = sb("spare", [P, n])
    tri = sb("tri", [P, P], BF16)
    onesb = sb("onesb", [P, P], BF16)
    top = sb("top", [P, n])
    ex = sb("ex", [P, n, E])
    den = sb("den", [P, n])
    pmax = sb("pmax", [P, n])
    eq = sb("eq", [P, n, E])
    hot = sb("hot", [P, n, E])
    hotb = sb("hotb", [P, ne], BF16)
    tot = sb("tot", [P, n, E])
    run = sb("run", [P, n, E])
    pos = sb("pos", [P, n, E])
    mine = sb("mine", [P, n])
    base = sb("base", [P, n])
    kept = sb("kept", [P, n])
    slotf = sb("slotf", [P, n])
    tmp = sb("tmp", [P, n])
    W = min(512, ne)
    nb = ne // W
    within = [ctx.enter_context(nc.psum_tensor(f"b_within{i}", [P, 512], F32)) for i in range(nb)]
    total = [ctx.enter_context(nc.psum_tensor(f"b_total{i}", [P, 512], F32)) for i in range(nb)]
    loaded, consts, shifted, exped, onehot, counted, chain = (sem(x) for x in (
        "loaded", "consts", "shifted", "exped", "onehot", "counted", "chain"))

    with nc.Block() as block:

        @block.sync
        def _(sp):
            sp.dma_start(rank[:, :], K.rank.partition_broadcast(P)).then_inc(loaded, 16)
            sp.dma_start(start[:, :], K.start.partition_broadcast(P)).then_inc(loaded, 16)
            sp.dma_start(spare[:, :], K.spare).then_inc(loaded, 16)

        @block.gpsimd
        def _(pool):
            pool.memset(tri[:, :], 1.0).then_inc(consts, 1)
            pool.memset(onesb[:, :], 1.0).then_inc(consts, 1)
            pool.wait_ge(consts, 1)
            pool.affine_select(out=tri[:, :], in_=tri[:, :], compare_op=ALU.is_ge, fill=0.0, base=0,
                               pattern=[[1, P]], channel_multiplier=-1).then_inc(consts, 1)

        @block.scalar
        def _(act):
            act.wait_ge(shifted, 1)
            act.activation(ex[:, :, :], ex[:, :, :], ACT.Exp).then_inc(exped, 1)

        @block.tensor
        def _(pe):
            pe.wait_ge(consts, 3)
            pe.wait_ge(onehot, 1)
            for i in range(nb):
                pe.matmul(within[i][:, 0:W], tri[:, :], hotb[:, i * W:(i + 1) * W], start=True, stop=True)
                mm = pe.matmul(total[i][:, 0:W], onesb[:, :], hotb[:, i * W:(i + 1) * W], start=True, stop=True)
            mm.then_inc(counted, 1)

        @block.vector
        def _(dve):
            done = [0]

            def link(ins):
                done[0] += 1
                ins.then_inc(chain, 1)
                dve.wait_ge(chain, done[0])

            def over_experts(a):
                return a.unsqueeze(2).broadcast_to([P, n, E])

            def over_rows(a):
                return a.unsqueeze(1).broadcast_to([P, n, E])

            lg = K.logits[:, :, :]
            link(dve.tensor_reduce(top[:, :], lg, AX.X, ALU.max))
            dve.tensor_tensor(ex[:, :, :], lg, over_experts(top[:, :]), ALU.subtract).then_inc(shifted, 1)
            link(dve.tensor_tensor(eq[:, :, :], lg, over_experts(top[:, :]), ALU.is_equal))
            dve.wait_ge(loaded, 48)
            link(dve.tensor_tensor(eq[:, :, :], eq[:, :, :], over_rows(rank[:, :]), ALU.mult))
            link(dve.tensor_reduce(mine[:, :], eq[:, :, :], AX.X, ALU.max))
            link(dve.tensor_tensor(hot[:, :, :], eq[:, :, :], over_experts(mine[:, :]), ALU.is_equal))
            dve.tensor_copy(hotb[:, :], hot[:, :, :].rearrange("p n e -> p (n e)")).then_inc(onehot, 1)
            dve.wait_ge(exped, 1)
            link(dve.tensor_reduce(den[:, :], ex[:, :, :], AX.X, ALU.add))
            link(dve.reciprocal(pmax[:, :], den[:, :]))
            dve.wait_ge(counted, 1)
            totf = tot[:, :, :].rearrange("p n e -> p (n e)")
            for i in range(nb):
                ins = dve.tensor_copy(totf[:, i * W:(i + 1) * W], total[i][:, 0:W])
            link(ins)
            for e in range(E):
                ins = dve.tensor_tensor_scan(run[:, :, e], K.ones[:, 0:n], tot[:, :, e], 0.0, ALU.mult, ALU.add)
            link(ins)
            link(dve.tensor_tensor(run[:, :, :], run[:, :, :], tot[:, :, :], ALU.subtract))
            posf = pos[:, :, :].rearrange("p n e -> p (n e)")
            runf = run[:, :, :].rearrange("p n e -> p (n e)")
            for i in range(nb):
                ins = dve.tensor_tensor(posf[:, i * W:(i + 1) * W], within[i][:, 0:W], runf[:, i * W:(i + 1) * W],
                                        ALU.add)
            link(ins)
            link(dve.tensor_tensor(pos[:, :, :], pos[:, :, :], hot[:, :, :], ALU.mult))
            link(dve.tensor_reduce(mine[:, :], pos[:, :, :], AX.X, ALU.add))
            link(dve.tensor_tensor(hot[:, :, :], hot[:, :, :], over_rows(start[:, :]), ALU.mult))
            link(dve.tensor_reduce(base[:, :], hot[:, :, :], AX.X, ALU.add))
            link(dve.tensor_scalar(kept[:, :], mine[:, :], float(K.cap), None, ALU.is_le))
            link(dve.tensor_tensor(slotf[:, :], base[:, :], mine[:, :], ALU.add))
            link(dve.tensor_scalar(tmp[:, :], slotf[:, :], float(E * K.cap - 1), None, ALU.min))
            link(dve.tensor_copy(K.read[:, :], tmp[:, :]))
            link(dve.tensor_tensor(slotf[:, :], slotf[:, :], spare[:, :], ALU.subtract))
            link(dve.tensor_tensor(slotf[:, :], slotf[:, :], kept[:, :], ALU.mult))
            link(dve.tensor_tensor(slotf[:, :], slotf[:, :], spare[:, :], ALU.add))
            link(dve.tensor_copy(K.slot[:, :], slotf[:, :]))
            g = K.gates[:, 2:3]
            link(dve.scalar_tensor_tensor(K.wexp[:, :], kept[:, :], g, pmax[:, :], ALU.mult, ALU.mult))
            link(dve.tensor_scalar(tmp[:, :], kept[:, :], -1.0, 1.0, ALU.mult, ALU.add))
            link(dve.tensor_scalar(tmp[:, :], tmp[:, :], g, None, ALU.mult))
            link(dve.tensor_tensor(K.wself[:, :], tmp[:, :], K.ln2[:, :, 1], ALU.mult))


def dispatch(nc, ctx, K):
    n = K.n
    t = ctx.enter_context(nc.sbuf_tensor("c_t", [P, 4, D], F32))
    at = ctx.enter_context(nc.sbuf_tensor("c_at", [P, 4], U32))
    ready = new_signal(nc, K, "c_ready")
    sent = [new_signal(nc, K, f"c_sent{p}") for p in range(4)]
    with nc.Block() as block:

        @block.vector
        def _(dve):
            for b, p, h in quads(dve, n):
                if not first(b, 4):
                    dve.wait_ge(sent[p], 16 * h)
                dve.tensor_copy(at[:, p:p + 1], K.slot[:, bass.ds(b, 1)])
                dve.tensor_scalar(t[:, p, :], K.xres[:, bass.ds(b * D, D)],
                                  K.ln2[:, bass.ds(b, 1), 0:1].rearrange("p a c -> p (a c)"),
                                  K.ln2[:, bass.ds(b, 1), 1:2].rearrange("p a c -> p (a c)"),
                                  ALU.subtract, ALU.mult).then_inc(ready, 1)

        @block.gpsimd
        def _(pool):
            for b, p, h in quads(pool, n):
                pool.wait_ge(ready, b + 1)
                pool.sem_inc(K.passed, 1)
                pool.indirect_dma_start(
                    out=K.disp[:, :], out_offset=bass.IndirectOffsetOnAxis(ap=at[:, p:p + 1], axis=0),
                    in_=t[:, p, :], in_offset=None).then_inc(sent[p], 16)
            for p in range(4):
                pool.wait_ge(sent[p], 16 * (n // 4))


def experts(nc, ctx, K):
    G = K.group
    SC = G // P
    ng = K.cap // G
    RING = 4

    def sb(name, shape, dt=F32):
        return ctx.enter_context(nc.sbuf_tensor("d_" + name, shape, dt))

    def psum(name):
        return ctx.enter_context(nc.psum_tensor("d_" + name, [P, 512], F32))

    def sem(name):
        return new_signal(nc, K, "d_" + name)

    w1f, w2f = sb("w1f", [P, DC * FF]), sb("w2f", [P, FC * D])
    w1 = sb("w1", [P, 2, 2, DC * FF], BF16)
    w2 = sb("w2", [P, 2, 2, FC * D], BF16)
    rows = sb("rows", [P, SC, D])
    tT = sb("tT", [P, 2, DC, G], BF16)
    hT = sb("hT", [P, RING, 2, G], BF16)
    ys = sb("ys", [P, SC, D])
    tb = [psum(f"tb{c}") for c in range(DC)]
    hb = [psum(f"hb{i}") for i in range(2)]
    yb = [psum(f"yb{s}") for s in range(SC)]
    wl, wc, wsplit = sem("w_loaded"), sem("w_high"), sem("w_split")
    rl, tmm, th, tl = sem("rows_loaded"), sem("t_mm"), sem("t_high"), sem("t_low")
    hmm, hh, hl, used, ysd, ysa, stored = (sem(x) for x in (
        "h_mm", "h_high", "h_low", "h_used", "y_dve", "y_act", "stored"))

    def groups(eng):
        with eng.Fori(0, E // 2) as j:
            for ep in range(2):
                with eng.Fori(0, ng) as k:
                    yield (2 * j + ep) * ng + k, ep, 2 * j + ep

    with nc.Block() as block:

        @block.sync
        def _(sp):
            sp.dma_start(rows[:, :, :], K.disp[0:G, :].rearrange("(p s) d -> p s d", s=SC)).then_inc(rl, 16)
            with sp.Fori(1, E * ng) as q:
                sp.wait_ge(tmm, q)
                sp.dma_start(rows[:, :, :], K.disp[bass.ds(q * G, G), :].rearrange("(p s) d -> p s d", s=SC)
                             ).then_inc(rl, 16)
            sp.wait_ge(tmm, E * ng)
            sp.dma_start(rows[:, :, :], K.disp[0:G, :].rearrange("(p s) d -> p s d", s=SC)).then_inc(rl, 16)

        @block.gpsimd
        def _(pool):
            def split(e, ep, free):
                pool.dma_start(w1f[:, :].rearrange("p (c f) -> p c f", c=DC),
                               K.W1[bass.ds(e, 1)].rearrange("a (c p) f -> p (a c) f", p=P)).then_inc(wl, 16)
                pool.dma_start(w2f[:, :].rearrange("p (c d) -> p c d", c=FC),
                               K.W2[bass.ds(e, 1)].rearrange("a (c p) d -> p (a c) d", p=P)).then_inc(wl, 16)
                if free:
                    pool.wait_ge(used, RING + (e - 1) * ng * FC)
                pool.wait_ge(wl, 32 * e + 32)
                pool.sem_inc(K.passed, 1)
                pool.tensor_copy(w1[:, ep, 0, :], w1f[:, :]).then_inc(wc, 1)
                pool.sem_inc(K.passed, 1)
                pool.tensor_copy(w2[:, ep, 0, :], w2f[:, :]).then_inc(wc, 1)
                pool.wait_ge(wc, 2 * e + 2)
                pool.tensor_tensor(w1[:, ep, 1, :], w1f[:, :], w1[:, ep, 0, :], ALU.subtract).then_inc(wsplit, 1)
                pool.tensor_tensor(w2[:, ep, 1, :], w2f[:, :], w2[:, ep, 0, :], ALU.subtract).then_inc(wsplit, 1)
                pool.wait_ge(wsplit, 2 * e + 2)

            split(0, 0, False)
            split(1, 1, False)
            with pool.Fori(1, E // 2) as j:
                for ep in range(2):
                    split(2 * j + ep, ep, True)

        @block.tensor
        def _(pe):
            def turn():
                for c in range(DC):
                    for s in range(SC):
                        mm = pe.transpose(tb[c][:, s * P:(s + 1) * P], rows[:, s, c * P:(c + 1) * P],
                                          K.ident[:, :])
                mm.then_inc(tmm, 1)

            def hidden(q, ep, f):
                pe.wait_ge(hl, q * FC + f + 1)
                bank = hb[f % 2]
                k = 0
                for wp, tp in ((0, 0), (0, 1), (1, 0)):
                    for c in range(DC):
                        mm = pe.matmul(bank[:, 0:G], w1[:, ep, wp, c * FF + f * P:c * FF + (f + 1) * P],
                                       tT[:, tp, c, :], start=k == 0, stop=k == 5)
                        k += 1
                mm.then_inc(hmm, 1)

            def back(q, ep, f):
                pe.wait_ge(hl, q * FC + f + 3)
                if f == 0:
                    pe.wait_ge(ysa, q + 1)
                    pe.wait_ge(ysd, q + 1)
                for s in range(SC):
                    for hp, wp in ((0, 0), (0, 1), (1, 0)):
                        mm = pe.matmul(yb[s][:, 0:D], hT[:, f % RING, hp, s * P:(s + 1) * P],
                                       w2[:, ep, wp, f * D:(f + 1) * D],
                                       start=f == 0 and hp == 0 and wp == 0, stop=f == FC - 1 and hp == 1)
                mm.then_inc(used, 1)

            pe.sem_inc(used, RING)
            pe.wait_ge(rl, 16)
            turn()
            for q, ep, e in groups(pe):
                pe.wait_ge(wsplit, 2 * e + 2)
                pe.wait_ge(th, q + 1)
                pe.wait_ge(tl, q + 1)
                for f in range(FC + 2):
                    if f < FC:
                        hidden(q, ep, f)
                    if f >= 2:
                        back(q, ep, f - 2)
                    if f == FC // 2:
                        pe.wait_ge(rl, 16 * q + 32)
                        turn()

        @block.scalar
        def _(act):
            act.sem_inc(ysa, 1)
            act.sem_inc(stored, 16)

            def high():
                for c in range(DC):
                    cp = act.activation(tT[:, 0, c, :], tb[c][:, 0:G], ACT.Copy)
                cp.then_inc(th, 1)

            act.wait_ge(tmm, 1)
            high()
            for q, ep, e in groups(act):
                for f in range(FC):
                    act.wait_ge(hmm, q * FC + f + 1)
                    act.wait_ge(used, q * FC + f + 1)
                    act.activation(hT[:, f % RING, 0, :], hb[f % 2][:, 0:G], ACT.Relu).then_inc(hh, 1)
                act.wait_ge(tmm, q + 2)
                act.wait_ge(hmm, (q + 1) * FC)
                high()
                act.wait_ge(used, RING + (q + 1) * FC)
                act.wait_ge(stored, 16 * q + 16)
                for s in range(0, SC, 2):
                    cp = act.activation(ys[:, s, :], yb[s][:, 0:D], ACT.Copy)
                cp.then_inc(ysa, 1)
                act.wait_ge(ysa, q + 2)
                act.wait_ge(ysd, q + 2)
                act.dma_start(K.eout[bass.ds(q * G, G), :].rearrange("(p s) d -> p s d", s=SC), ys[:, :, :]
                              ).then_inc(stored, 16)
            act.wait_ge(stored, 16 * (E * ng + 1))

        @block.vector
        def _(dve):
            dve.sem_inc(hl, 2)
            dve.sem_inc(ysd, 1)

            def low():
                for c in range(DC):
                    cp = dve.tensor_tensor(tT[:, 1, c, :], tb[c][:, 0:G], tT[:, 0, c, :], ALU.subtract)
                cp.then_inc(tl, 1)

            dve.wait_ge(th, 1)
            low()
            for q, ep, e in groups(dve):
                for f in range(FC):
                    dve.wait_ge(hh, q * FC + f + 1)
                    dve.scalar_tensor_tensor(hT[:, f % RING, 1, :], hb[f % 2][:, 0:G], 0.0, hT[:, f % RING, 0, :],
                                             ALU.max, ALU.subtract).then_inc(hl, 1)
                dve.wait_ge(th, q + 2)
                low()
                dve.wait_ge(used, RING + (q + 1) * FC)
                dve.wait_ge(stored, 16 * q + 16)
                for s in range(1, SC, 2):
                    cp = dve.tensor_copy(ys[:, s, :], yb[s][:, 0:D])
                cp.then_inc(ysd, 1)


def combine_and_correlate(nc, ctx, K):
    n = K.n
    DX = D + 1

    def sb(name, shape, dt=F32):
        return ctx.enter_context(nc.sbuf_tensor("e_" + name, shape, dt))

    def psum(name):
        return ctx.enter_context(nc.psum_tensor("e_" + name, [P, 512], F32))

    def sem(name):
        return new_signal(nc, K, "e_" + name)

    dft = sb("dft", [P, P])
    gm = sb("gm", [P, DC, DX])
    brow = sb("brow", [1, DX])
    dc = sb("dc", [1, P])
    banks = [psum(f"bank{i}") for i in range(8)]
    w_loaded, w_turned, w_ready, g_mm = sem("w_loaded"), sem("w_turned"), sem("w_ready"), sem("g_mm")

    with ExitStack() as prep, nc.Block() as block:
        raw = prep.enter_context(nc.sbuf_tensor("e_raw", [P, 2, DC, D], F32))
        wT = prep.enter_context(nc.sbuf_tensor("e_wT", [P, 2, DC, D], F32))
        bq = prep.enter_context(nc.sbuf_tensor("e_bq", [P, DC], F32))
        bk = prep.enter_context(nc.sbuf_tensor("e_bk", [P, DC], F32))

        @block.sync
        def _(sp):
            for i, w in enumerate((K.Wq1, K.Wk1)):
                sp.dma_start(raw[:, i], w.rearrange("(c p) d -> p c d", p=P)).then_inc(w_loaded, 16)
            sp.dma_start(bq[:, :], K.bq1.rearrange("(c p) -> p c", p=P), allow_slow_non_contiguous=True).then_inc(w_loaded, 16)
            sp.dma_start(bk[:, :], K.bk1.rearrange("(c p) -> p c", p=P), allow_slow_non_contiguous=True).then_inc(w_loaded, 16)
            sp.dma_start(dft[:, :], K.dft).then_inc(w_loaded, 16)

        @block.tensor
        def _(pe):
            pe.wait_ge(w_loaded, 16 * 5)
            for i in range(2):
                mm = transpose_square(pe, banks[i], raw[:, i], K.ident)
            mm.then_inc(w_turned, 1)
            pe.wait_ge(w_ready, 2)
            for m in range(DC):
                for c in range(DC):
                    pe.matmul(banks[2 + m][:, 0:D], wT[:, 0, c, m * P:(m + 1) * P], wT[:, 1, c, :],
                              start=c == 0, stop=c == DC - 1)
            for m in range(DC):
                for c in range(DC):
                    pe.matmul(banks[4 + m][:, 0:1], wT[:, 0, c, m * P:(m + 1) * P], bk[:, c:c + 1],
                              start=c == 0, stop=c == DC - 1)
            for c in range(DC):
                pe.matmul(banks[6][0:1, 0:D], bq[:, c:c + 1], wT[:, 1, c, :], start=c == 0, stop=c == DC - 1)
            for c in range(DC):
                mm = pe.matmul(banks[7][0:1, 0:1], bq[:, c:c + 1], bk[:, c:c + 1], start=c == 0,
                               stop=c == DC - 1)
            mm.then_inc(g_mm, 1)

        @block.vector
        def _(dve):
            dve.memset(dc[:, :], 0.0).then_inc(w_ready, 1)
            dve.wait_ge(w_turned, 1)
            for i in range(2):
                ins = dve.tensor_copy(wT[:, i].rearrange("p c d -> p (c d)"), banks[i][:, :])
            ins.then_inc(w_ready, 1)
            dve.wait_ge(g_mm, 1)
            for m in range(DC):
                dve.tensor_copy(gm[:, m, 0:D], banks[2 + m][:, 0:D])
                dve.tensor_copy(gm[:, m, D:DX], banks[4 + m][:, 0:1])
            dve.tensor_scalar(brow[:, 0:D], banks[6][0:1, 0:D], float(P), None, ALU.mult)
            dve.tensor_scalar(brow[:, D:DX], banks[7][0:1, 0:1], float(P), None, ALU.mult)
            dve.wait_ge(w_ready, 1)
            dve.memset(dc[:, 0:1], 1.0).then_inc(w_ready, 1)
            dve.wait_ge(w_ready, 3)

    at = sb("at", [P, 2], U32)
    eo = sb("eo", [P, 2, D])
    cin = sb("cin", [P, 2, D])
    own = sb("own", [P, D])
    xh = sb("xh", [P, 2, D])
    xfT = sb("xfT", [P, DC * P])
    cf = sb("cf", [P, 2, DX])
    prod = sb("prod", [P, DX])
    pc = sb("pc", [P, 1])
    st, mv, ve, rs = sb("st", [P, 6]), sb("mv", [P, 2, 2]), sb("ve", [P, 1]), sb("rs", [P, 2])
    xb, cb, gb = banks[0:2], banks[2:4], banks[4:6]
    ctl = [sem("ctx0"), sem("ctx1")]
    got = [sem("got0"), sem("got1")]
    ats, owns, sums, xs, bn, mvs, ves, rss, xhs = (sem(x) for x in (
        "at", "own", "sum", "x", "bn", "mv", "ve", "rs", "xhat"))
    xfmm, cfmm, xfs, cfs, gmm, prods, ps, preset = (sem(x) for x in (
        "xf_mm", "cf_mm", "xf", "cf", "g_prod", "prod", "p", "preset"))

    with nc.Block() as block:

        @block.sync
        def _(sp):
            for b, p, h in steps(sp, n):
                if not first(b, 2):
                    sp.wait_ge(cfmm, b - 1)
                sp.dma_start(cin[:, p, :], K.ctx[bass.ds(b, 1)].rearrange("a p d -> p (a d)")
                             ).then_inc(ctl[p], 16)

        @block.gpsimd
        def _(pool):
            def gather(b, p):
                pool.wait_ge(ats, b + 1)
                if not first(b, 2):
                    pool.wait_ge(sums, b - 1)
                pool.sem_inc(K.passed, 1)
                pool.indirect_dma_start(
                    out=eo[:, p, :], out_offset=None, in_=K.eout[:, :],
                    in_offset=bass.IndirectOffsetOnAxis(ap=at[:, p:p + 1], axis=0)).then_inc(got[p], 16)

            def deviation(b, p):
                if not first(b, 1):
                    pool.wait_ge(rss, b)
                pool.wait_ge(mvs, b + 1)
                pool.sem_inc(K.passed, 1)
                pool.tensor_scalar(ve[:, :], mv[:, p, 1:2], LN_EPS, 1.0, ALU.add, ALU.mult).then_inc(ves, 1)
                pool.wait_ge(ves, b + 1)
                if not first(b, 2):
                    pool.wait_ge(xhs, b - 1)
                pool.tensor_tensor(rs[:, p:p + 1], ve[:, :], K.half[:, :], ALU.pow).then_inc(rss, 1)

            gather(0, 0)
            gather(1, 1)
            deviation(0, 0)
            for b, p, h in steps(pool, n):
                if not last(b, n, 2):
                    gather(b + 2, p)
                if not last(b, n, 1):
                    deviation(b + 1, 1 - p)

        @block.tensor
        def _(pe):
            def spectra(b, p, h):
                pe.wait_ge(ctl[p], 16 * h + 16)
                if not first(b, 2):
                    pe.wait_ge(cfs, b - 1)
                pe.matmul(cb[p][:, 0:D], dft[:, :], cin[:, p, :], start=True, stop=True).then_inc(cfmm, 1)
                pe.wait_ge(xhs, b + 1)
                if not first(b, 2):
                    pe.wait_ge(xfs, b - 1)
                for c in range(DC):
                    mm = pe.matmul(xb[p][:, c * P:(c + 1) * P], xh[:, p, c * P:(c + 1) * P], dft[:, :],
                                   start=True, stop=True)
                mm.then_inc(xfmm, 1)

            def product(b, p):
                pe.wait_ge(xfs, b + 1)
                if not first(b, 2):
                    pe.wait_ge(prods, b - 1)
                for c in range(DC):
                    pe.matmul(gb[p][:, 0:DX], xfT[:, c * P:(c + 1) * P], gm[:, c, :], start=c == 0, stop=False)
                pe.matmul(gb[p][:, 0:DX], dc[:, :], brow[:, :], start=False, stop=True).then_inc(gmm, 1)

            for b, p, h in steps(pe, n):
                spectra(b, p, h)
                if not first(b, 1):
                    product(b - 1, 1 - p)
            product(n - 1, 1)

        @block.scalar
        def _(act):
            act.wait_ge(preset, 2)
            for b, p, h in steps(act, n):
                act.wait_ge(cfmm, b + 1)
                if not first(b, 2):
                    act.wait_ge(prods, b - 1)
                act.activation(cf[:, p, 0:D], cb[p][:, 0:D], ACT.Copy).then_inc(cfs, 1)
                act.wait_ge(xfmm, b + 1)
                if not first(b, 1):
                    act.wait_ge(gmm, b)
                act.activation(xfT[:, :], xb[p][:, 0:D], ACT.Copy).then_inc(xfs, 1)

        @block.vector
        def _(dve):
            def row_of(b):
                return K.xres[:, bass.ds(b * D, D)]

            def name_row(b, p):
                dve.tensor_copy(at[:, p:p + 1], K.read[:, bass.ds(b, 1)]).then_inc(ats, 1)

            def add_result(b, p, h):
                row = row_of(b)
                dve.tensor_scalar(own[:, :], row, K.ln2[:, bass.ds(b, 1), 0:1].rearrange("p a c -> p (a c)"),
                                  K.wself[:, bass.ds(b, 1)], ALU.subtract, ALU.mult).then_inc(owns, 1)
                dve.wait_ge(got[p], 16 * h + 16)
                dve.wait_ge(owns, b + 1)
                dve.scalar_tensor_tensor(row, eo[:, p, :], K.wexp[:, bass.ds(b, 1)], row, ALU.mult, ALU.add
                                         ).then_inc(sums, 1)

            def add_own(b):
                row = row_of(b)
                dve.wait_ge(sums, b + 1)
                dve.tensor_tensor(row, row, own[:, :], ALU.add).then_inc(xs, 1)

            def stats(b):
                dve.wait_ge(xs, b + 1)
                if not first(b, 1):
                    dve.wait_ge(mvs, b)
                dve.sem_inc(K.passed, 1)
                dve.bn_stats(st[:, :], row_of(b)).then_inc(bn, 1)

            def aggregate(b, p):
                dve.wait_ge(bn, b + 1)
                if not first(b, 2):
                    dve.wait_ge(ves, b - 1)
                    dve.wait_ge(xhs, b - 1)
                dve.sem_inc(K.passed, 1)
                dve.bn_aggr(mv[:, p, :], st[:, :]).then_inc(mvs, 1)

            def normalise(b, p):
                dve.wait_ge(rss, b + 1)
                if not first(b, 2):
                    dve.wait_ge(xfmm, b - 1)
                dve.tensor_scalar(xh[:, p, :], row_of(b), mv[:, p, 0:1], rs[:, p:p + 1],
                                  ALU.subtract, ALU.mult).then_inc(xhs, 1)

            def reduce(b, p):
                dve.wait_ge(gmm, b + 1)
                dve.wait_ge(cfs, b + 1)
                if not first(b, 1):
                    dve.wait_ge(ps, b)
                dve.tensor_tensor_reduce(prod[:, :], gb[p][:, 0:DX], cf[:, p, :], 1.0, 0.0, ALU.mult, ALU.add,
                                         pc[:, :]).then_inc(prods, 1)

            def keep_sum(b):
                dve.wait_ge(prods, b + 1)
                dve.tensor_copy(K.spec[:, bass.ds(b, 1)], pc[:, :]).then_inc(ps, 1)

            dve.memset(cf[:, :, D:DX], 0.0).then_inc(preset, 1)
            dve.wait_ge(preset, 1)
            dve.memset(cf[0:1, :, D:DX], float(P)).then_inc(preset, 1)
            dve.wait_ge(preset, 2)
            name_row(0, 0)
            name_row(1, 1)
            add_result(0, 0, 0)
            add_own(0)
            stats(0)
            aggregate(0, 0)
            for b, p, h in steps(dve, n):
                if not last(b, n, 2):
                    name_row(b + 2, p)
                if not last(b, n, 1):
                    add_result(b + 1, 1 - p, h + p)
                normalise(b, p)
                if not last(b, n, 1):
                    add_own(b + 1)
                if not first(b, 2):
                    reduce(b - 2, p)
                if not last(b, n, 1):
                    stats(b + 1)
                if not first(b, 2):
                    keep_sum(b - 2)
                if not last(b, n, 1):
                    aggregate(b + 1, 1 - p)
            for b in (n - 2, n - 1):
                reduce(b, b % 2)
                keep_sum(b)
            dve.wait_ge(ps, n)


def pick_delays(nc, ctx, K):
    n = K.n

    def sb(name, shape, dt=F32):
        return ctx.enter_context(nc.sbuf_tensor("f_" + name, shape, dt))

    def sem(name):
        return new_signal(nc, K, "f_" + name)

    idft = sb("idft", [P, P])
    mean = sb("mean", [n, P])
    rest, rest2 = sb("rest", [n, P]), sb("rest2", [n, P])
    top8, next8, ninth = sb("top8", [n, 8]), sb("next8", [n, 8]), sb("ninth", [n, 8])
    ex, kept, den, w, twice = sb("ex", [n, P]), sb("kept", [n, P]), sb("den", [n, 1]), sb("w", [n, P]), sb("twice", [n, 2, P])
    neg = sb("neg", [n, 1])
    bank = ctx.enter_context(nc.psum_tensor("f_bank", [P, 512], F32))
    loaded, mmd, negs, exped, chain, twices, stored = (sem(x) for x in (
        "loaded", "mean_mm", "neg", "exped", "chain", "twice", "stored"))

    with nc.Block() as block:

        @block.sync
        def _(sp):
            sp.dma_start(idft[:, :], K.idft).then_inc(loaded, 16)
            sp.wait_ge(twices, 1)
            sp.dma_start(K.circ, twice[:, :, :].rearrange("n a k -> n (a k)")).then_inc(stored, 16)
            sp.wait_ge(stored, 16)

        @block.tensor
        def _(pe):
            pe.wait_ge(loaded, 16)
            pe.matmul(bank[0:n, 0:P], K.spec[:, 0:n], idft[:, :], start=True, stop=True).then_inc(mmd, 1)

        @block.scalar
        def _(act):
            act.wait_ge(negs, 1)
            act.activation(ex[:, :], mean[:, :], ACT.Exp, bias=neg[:, 0:1]).then_inc(exped, 1)

        @block.vector
        def _(dve):
            done = [0]

            def link(ins):
                done[0] += 1
                ins.then_inc(chain, 1)
                dve.wait_ge(chain, done[0])

            dve.wait_ge(mmd, 1)
            link(dve.tensor_copy(mean[:, :], bank[0:n, 0:P]))
            link(dve.max(top8[:, :], mean[:, :]))
            dve.tensor_scalar(neg[:, :], top8[:, 0:1], -1.0, None, ALU.mult).then_inc(negs, 1)
            link(dve.match_replace(rest[:, :], top8[:, :], mean[:, :], LOWEST))
            link(dve.max(next8[:, :], rest[:, :]))
            link(dve.memset(ninth[:, :], LOWEST))
            link(dve.tensor_copy(ninth[:, 0:1], next8[:, 0:1]))
            link(dve.match_replace(rest2[:, :], ninth[:, :], rest[:, :], LOWEST))
            link(dve.tensor_scalar(kept[:, :], rest2[:, :], 0.5 * LOWEST, None, ALU.is_le))
            dve.wait_ge(exped, 1)
            link(dve.tensor_tensor(ex[:, :], ex[:, :], kept[:, :], ALU.mult))
            link(dve.tensor_reduce(den[:, :], ex[:, :], AX.X, ALU.add))
            link(dve.reciprocal(den[:, :], den[:, :]))
            link(dve.tensor_scalar(w[:, :], ex[:, :], den[:, 0:1], None, ALU.mult))
            for a in range(2):
                ins = dve.tensor_copy(twice[:, a, :], w[:, :])
            ins.then_inc(twices, 1)


def delayed_values(nc, ctx, K):
    n = K.n
    g = K.gates[:, 1:2]

    def sb(name, shape, dt=F32):
        return ctx.enter_context(nc.sbuf_tensor("g_" + name, shape, dt))

    def sem(name):
        return new_signal(nc, K, "g_" + name)

    wvo = sb("wvo", [P, DC, D])
    gbias = sb("gbias", [P, D])
    banks = [ctx.enter_context(nc.psum_tensor(f"g_bank{i}", [P, 512], F32)) for i in range(4)]
    w_loaded, w_turned, w_ready, o_mm = sem("w_loaded"), sem("w_turned"), sem("w_ready"), sem("o_mm")

    with ExitStack() as prep, nc.Block() as block:
        raw = prep.enter_context(nc.sbuf_tensor("g_raw", [P, DC, D], F32))
        wvT = prep.enter_context(nc.sbuf_tensor("g_wvT", [P, DC, D], F32))
        wo = prep.enter_context(nc.sbuf_tensor("g_wo", [P, DC, D], F32))
        bv = prep.enter_context(nc.sbuf_tensor("g_bv", [P, DC], F32))
        bvb = prep.enter_context(nc.sbuf_tensor("g_bvb", [P, DC, P], F32))
        bob = prep.enter_context(nc.sbuf_tensor("g_bob", [P, D], F32))

        @block.sync
        def _(sp):
            sp.dma_start(raw[:, :, :], K.Wv1.rearrange("(c p) d -> p c d", p=P)).then_inc(w_loaded, 16)
            sp.dma_start(wo[:, :, :], K.Wo1.rearrange("(c p) d -> p c d", p=P)).then_inc(w_loaded, 16)
            sp.dma_start(bv[:, :], K.bv1.rearrange("(c p) -> p c", p=P), allow_slow_non_contiguous=True).then_inc(w_loaded, 16)
            sp.dma_start(bob[:, :], K.bo1.partition_broadcast(P)).then_inc(w_loaded, 16)

        @block.tensor
        def _(pe):
            pe.wait_ge(w_loaded, 64)
            transpose_square(pe, banks[0], raw, K.ident).then_inc(w_turned, 1)
            pe.wait_ge(w_ready, 2)
            for m in range(DC):
                for c in range(DC):
                    pe.matmul(banks[1 + m][:, 0:D], wvT[:, c, m * P:(m + 1) * P], wo[:, c, :],
                              start=c == 0, stop=c == DC - 1)
            for c in range(DC):
                mm = pe.matmul(banks[3][:, 0:D], bvb[:, c, :], wo[:, c, :], start=c == 0, stop=c == DC - 1)
            mm.then_inc(o_mm, 1)

        @block.vector
        def _(dve):
            dve.wait_ge(w_loaded, 64)
            for c in range(DC):
                ins = dve.tensor_scalar(bvb[:, c, :], K.ones[:, :], bv[:, c:c + 1], None, ALU.mult)
            ins.then_inc(w_ready, 1)
            dve.wait_ge(w_turned, 1)
            dve.tensor_copy(wvT[:, :, :].rearrange("p c d -> p (c d)"), banks[0][:, :]).then_inc(w_ready, 1)
            dve.wait_ge(o_mm, 1)
            for m in range(DC):
                dve.tensor_copy(wvo[:, m, :], banks[1 + m][:, 0:D])
            dve.tensor_tensor(gbias[:, :], banks[3][:, 0:D], bob[:, :], ALU.add).then_inc(w_ready, 1)
            dve.wait_ge(w_ready, 3)
            dve.tensor_scalar(gbias[:, :], gbias[:, :], g, None, ALU.mult).then_inc(w_ready, 1)
            dve.wait_ge(w_ready, 4)

    cin = sb("cin", [P, 2, D])
    ci = sb("ci", [P, 2, P])
    aT = sb("aT", [P, 2, D])
    abank, ybank = banks[0:2], banks[2:4]
    ld = [sem("ld0"), sem("ld1")]
    amm, aTs, ymm, pre, xs = (sem(x) for x in ("a_mm", "aT", "y_mm", "preadded", "x"))
    circ = K.circ

    with nc.Block() as block:

        @block.sync
        def _(sp):
            for b, p, h in steps(sp, n):
                if not first(b, 2):
                    sp.wait_ge(amm, b - 1)
                sp.dma_start(cin[:, p, :], K.ctx[bass.ds(b, 1)].rearrange("a p d -> p (a d)")
                             ).then_inc(ld[p], 16)
                sp.dma_start(ci[:, p, :], bass.AP(tensor=circ.tensor, offset=b * 2 * P + 1, ap=[[1, P], [1, P]])
                             ).then_inc(ld[p], 16)

        @block.gpsimd
        def _(pool):
            for b, p, h in steps(pool, n):
                row = K.xres[:, bass.ds(b * D, D)]
                pool.tensor_tensor(row, row, gbias[:, :], ALU.add).then_inc(pre, 1)

        @block.tensor
        def _(pe):
            def out(b, p):
                pe.wait_ge(aTs, b + 1)
                if not first(b, 2):
                    pe.wait_ge(xs, b - 1)
                for c in range(DC):
                    mm = pe.matmul(ybank[p][:, 0:D], aT[:, p, c * P:(c + 1) * P], wvo[:, c, :],
                                   start=c == 0, stop=c == DC - 1)
                mm.then_inc(ymm, 1)

            for b, p, h in steps(pe, n):
                pe.wait_ge(ld[p], 32 * h + 32)
                if not first(b, 2):
                    pe.wait_ge(aTs, b - 1)
                for c in range(DC):
                    mm = pe.matmul(abank[p][:, c * P:(c + 1) * P], cin[:, p, c * P:(c + 1) * P], ci[:, p, :],
                                   start=True, stop=True)
                mm.then_inc(amm, 1)
                if not first(b, 1):
                    out(b - 1, 1 - p)
            out(n - 1, 1)

        @block.scalar
        def _(act):
            for b, p, h in steps(act, n):
                act.wait_ge(amm, b + 1)
                if not first(b, 2):
                    act.wait_ge(ymm, b - 1)
                for c in range(DC):
                    last = c * P - 1 if c else None
                    cp = act.activation(aT[:, p, c * P:(c + 1) * P], abank[p][:, (c + 1) * P - 1:last:-1], ACT.Copy)
                cp.then_inc(aTs, 1)

        @block.vector
        def _(dve):
            for b, p, h in steps(dve, n):
                dve.wait_ge(ymm, b + 1)
                dve.wait_ge(pre, b + 1)
                row = K.xres[:, bass.ds(b * D, D)]
                dve.scalar_tensor_tensor(row, ybank[p][:, 0:D], g, row, ALU.mult, ALU.add).then_inc(xs, 1)
            dve.wait_ge(xs, n)


def ternary_ffn(nc, ctx, K):
    n = K.n
    SC = 4
    G = SC * P
    nq = n // SC
    RH, RG = 4, 4
    g = K.gates[:, 3:4]

    def sb(name, shape, dt=F32):
        return ctx.enter_context(nc.sbuf_tensor("h_" + name, shape, dt))

    def sem(name):
        return new_signal(nc, K, "h_" + name)

    wf = sb("wf", [P, DC, FF], BF16)
    wp = sb("wp", [P, FC, D], BF16)
    lnw = sb("lnw", [P, FC])
    u1, gu2 = sb("u1", [P, D]), sb("gu2", [P, D])
    banks = [ctx.enter_context(nc.psum_tensor(f"h_bank{i}", [P, 512], F32)) for i in range(8)]
    loaded, chain, absd, summed, tern, turned, w32s, u_mm, ends = (sem(x) for x in (
        "loaded", "chain", "abs_sums", "summed", "ternary", "turned", "w32", "u_mm", "prepared"))

    with ExitStack() as prep, nc.Block() as block:
        def pb(name, shape):
            return prep.enter_context(nc.sbuf_tensor("h_" + name, shape, F32))

        raw = [pb("rawf", [P, FC * D]), pb("rawp", [P, DC * FF])]
        low, asum, thr, nthr = pb("low", [P, FC * D]), pb("asum", [P, 2]), pb("thr", [P, 2]), pb("nthr", [P, 2])
        wp32 = pb("wp32", [P, FC, D])
        lnb = pb("lnb", [P, FC])
        wide = pb("wide", [P, 2, FC, P])

        @block.sync
        def _(sp):
            sp.dma_start(raw[0][:, :].rearrange("p (c d) -> p c d", c=FC),
                         K.Wfc.rearrange("(c p) d -> p c d", p=P)).then_inc(loaded, 16)
            sp.dma_start(raw[1][:, :].rearrange("p (c f) -> p c f", c=DC),
                         K.Wpr.rearrange("(c p) f -> p c f", p=P)).then_inc(loaded, 16)
            sp.dma_start(lnw[:, :], K.lnw.rearrange("(c p) -> p c", p=P), allow_slow_non_contiguous=True).then_inc(loaded, 16)
            sp.dma_start(lnb[:, :], K.lnb.rearrange("(c p) -> p c", p=P), allow_slow_non_contiguous=True).then_inc(loaded, 16)

        @block.tensor
        def _(pe):
            pe.wait_ge(absd, 2)
            pe.matmul(banks[0][:, 0:2], K.ones[:, :], asum[:, :], start=True, stop=True).then_inc(summed, 1)
            pe.wait_ge(tern, 2)
            for dd in range(DC):
                for c in range(FC):
                    pe.transpose(banks[dd * 2 + c // 4][:, (c % 4) * P:(c % 4 + 1) * P],
                                 raw[0][:, c * D + dd * P:c * D + (dd + 1) * P], K.ident[:, :])
            for c in range(FC):
                for dd in range(DC):
                    at = (c % 2) * D + dd * P
                    mm = pe.transpose(banks[4 + c // 2][:, at:at + P],
                                      raw[1][:, dd * FF + c * P:dd * FF + (c + 1) * P], K.ident[:, :])
            mm.then_inc(turned, 1)
            pe.wait_ge(w32s, 1)
            for k in range(2):
                for c in range(FC):
                    mm = pe.matmul(banks[k][:, 0:D], wide[:, k, c, :], wp32[:, c, :], start=c == 0,
                                   stop=c == FC - 1)
            mm.then_inc(u_mm, 1)

        @block.vector
        def _(dve):
            done = [0]

            def link(ins):
                done[0] += 1
                ins.then_inc(chain, 1)
                dve.wait_ge(chain, done[0])

            dve.wait_ge(loaded, 64)
            for k in range(2):
                dve.tensor_reduce(asum[:, k:k + 1], raw[k][:, :], AX.X, ALU.add,
                                  apply_absolute_value=True).then_inc(absd, 1)
            dve.wait_ge(summed, 1)
            link(dve.tensor_scalar(thr[:, :], banks[0][:, 0:2], 1.0 / (FF * D), 1e-6, ALU.mult, ALU.add))
            link(dve.tensor_scalar(thr[:, :], thr[:, :], 0.5, None, ALU.mult))
            link(dve.tensor_scalar(nthr[:, :], thr[:, :], -1.0, None, ALU.mult))
            for k in range(2):
                link(dve.tensor_scalar(low[:, :], raw[k][:, :], nthr[:, k:k + 1], None, ALU.is_lt))
                ins = dve.scalar_tensor_tensor(raw[k][:, :], raw[k][:, :], thr[:, k:k + 1], low[:, :],
                                               ALU.is_gt, ALU.subtract)
                link(ins)
            dve.sem_inc(tern, 2)
            for c in range(FC):
                dve.tensor_scalar(wide[:, 0, c, :], K.ones[:, :], lnw[:, c:c + 1], None, ALU.mult)
                dve.tensor_scalar(wide[:, 1, c, :], K.ones[:, :], lnb[:, c:c + 1], None, ALU.mult)
            dve.wait_ge(turned, 1)
            for dd in range(DC):
                for c in range(2):
                    dve.tensor_copy(wf[:, dd, c * 512:(c + 1) * 512], banks[dd * 2 + c][:, :])
            for c in range(4):
                dve.tensor_copy(wp[:, 2 * c:2 * c + 2, :].rearrange("p a d -> p (a d)"), banks[4 + c][:, :])
                ins = dve.tensor_copy(wp32[:, 2 * c:2 * c + 2, :].rearrange("p a d -> p (a d)"),
                                      banks[4 + c][:, :])
            ins.then_inc(w32s, 1)
            dve.wait_ge(u_mm, 1)
            dve.tensor_copy(u1[:, :], banks[0][:, 0:D]).then_inc(ends, 1)
            dve.tensor_scalar(gu2[:, :], banks[1][:, 0:D], g, None, ALU.mult).then_inc(ends, 1)
            dve.wait_ge(ends, 2)

    st, mv = sb("st", [P, SC, 6]), sb("mv", [P, SC, 2])
    ve, rs = sb("ve", [P, SC]), sb("rs", [P, SC])
    xh = sb("xh", [P, SC, D])
    xT = sb("xT", [P, 2, 2, DC, G], BF16)
    hf = sb("hf", [P, RG, G])
    hq = sb("hq", [P, RG, G])
    hT = sb("hT", [P, RH, 2, G], BF16)
    s12 = sb("s12", [P, 2, 2, G])
    ysb = sb("ysb", [P, SC, D])
    m12, msq, var, ve2, rs2 = sb("m12", [P, 2 * SC]), sb("msq", [P, SC]), sb("var", [P, SC]), sb("ve2", [P, SC]), sb("rs2", [P, SC])
    ca, cb = sb("ca", [P, SC]), sb("cb", [P, SC])
    osb = sb("osb", [P, SC, D])
    tb, hb, yb = banks[0:2], banks[2:4], banks[4:8]
    (bns, mvs, ves, rss, xhs, tmm, th, tl, hmm, hfs, hqs, hh, hl, used, summed1, summed2, sum_mm, m12s, msqs, vars_, ve2s, rs2s,
     cas, cbs, ys, o1, o2, o3, stored) = (sem(x) for x in (
        "bn", "mv", "ve", "rs", "xhat", "t_mm", "t_high", "t_low", "h_mm", "h", "h_square", "h_high", "h_low",
        "h_used", "h_summed", "h_square_summed", "sum_mm", "means", "mean_square", "variance", "ve2", "rs2", "ca", "cb", "y",
        "out1", "out2", "out3", "stored"))
    outv = K.out.rearrange("(q s) p d -> q p s d", s=SC)

    def y_of(p, s):
        return yb[2 * p + s // 2][:, (s % 2) * D:(s % 2 + 1) * D]

    with nc.Block() as block:

        @block.tensor
        def _(pe):
            def turn(q):
                pe.wait_ge(xhs, q + 1)
                if not first(q, 1):
                    pe.wait_ge(th, q)
                    pe.wait_ge(tl, q)
                if not first(q, 2):
                    pe.wait_ge(m12s, q - 1)
                for c in range(DC):
                    for s in range(SC):
                        mm = pe.transpose(tb[c][:, s * P:(s + 1) * P], xh[:, s, c * P:(c + 1) * P],
                                          K.ident[:, :])
                mm.then_inc(tmm, 1)

            def hidden(q, p, f):
                if f == 0:
                    pe.wait_ge(th, q + 1)
                    pe.wait_ge(tl, q + 1)
                if f >= 2 or not first(q, 1):
                    pe.wait_ge(hfs, q * FC + f - 1)
                k = 0
                for part in range(2):
                    for c in range(DC):
                        mm = pe.matmul(hb[f % 2][:, :], wf[:, c, f * P:(f + 1) * P], xT[:, p, part, c, :],
                                       start=k == 0, stop=k == 3)
                        k += 1
                mm.then_inc(hmm, 1)

            def back(q, p, f):
                pe.wait_ge(hl, q * FC + f + 1)
                if f == 0 and not first(q, 2):
                    pe.wait_ge(ys, q - 1)
                for s in range(SC):
                    for part in range(2):
                        mm = pe.matmul(y_of(p, s), hT[:, f % RH, part, s * P:(s + 1) * P], wp[:, f, :],
                                       start=f == 0 and part == 0 and s % 2 == 0,
                                       stop=f == FC - 1 and part == 1 and s % 2 == 1)
                mm.then_inc(used, 1)

            def sums(q, p):
                pe.wait_ge(summed1, (q + 1) * FC)
                pe.wait_ge(summed2, (q + 1) * FC)
                for k in range(2):
                    for s in range(SC):
                        mm = pe.matmul(tb[0][:, k * SC + s:k * SC + s + 1], s12[:, p, k, s * P:(s + 1) * P],
                                       K.ones[:, 0:1], start=True, stop=True)
                mm.then_inc(sum_mm, 1)

            turn(0)
            for q, p, h in steps(pe, nq):
                for f in range(FC):
                    hidden(q, p, f)
                    if f >= 2:
                        back(q, p, f - 2)
                    elif not first(q, 1):
                        back(q - 1, 1 - p, f + FC - 2)
                    if f == 2 and not first(q, 1):
                        sums(q - 1, 1 - p)
                    if f == 4 and not last(q, nq, 1):
                        turn(q + 1)
            back(nq - 1, 1, FC - 2)
            back(nq - 1, 1, FC - 1)
            sums(nq - 1, 1)

        @block.scalar
        def _(act):
            def high(q, p):
                act.wait_ge(tmm, q + 1)
                if not first(q, 2):
                    act.wait_ge(hmm, (q - 1) * FC)
                for c in range(DC):
                    cp = act.activation(xT[:, p, 0, c, :], tb[c][:, :], ACT.Copy)
                cp.then_inc(th, 1)

            def chunk(q, f):
                act.wait_ge(hmm, q * FC + f + 1)
                if f >= RG or not first(q, 1):
                    act.wait_ge(hl, q * FC + f - RG + 1)
                    act.wait_ge(summed1, q * FC + f - RG + 1)
                    act.wait_ge(summed2, q * FC + f - RG + 1)
                act.activation(hf[:, f % RG, :],
                               hb[f % 2][:, :], ACT.Gelu).then_inc(hfs, 1)
                act.wait_ge(hfs, q * FC + f + 1)
                if f >= RH or not first(q, 1):
                    act.wait_ge(used, q * FC + f - RH + 1)
                act.activation(hT[:, f % RH, 0, :], hf[:, f % RG, :], ACT.Copy, scale=lnw[:, f:f + 1]
                               ).then_inc(hh, 1)
                act.activation(hq[:, f % RG, :], hf[:, f % RG, :], ACT.Square).then_inc(hqs, 1)

            def y_out(q, p):
                act.wait_ge(used, (q + 1) * FC)
                if not first(q, 1):
                    act.wait_ge(o1, SC * q)
                for s in range(SC):
                    cp = act.activation(ysb[:, s, :], y_of(p, s), ACT.Copy)
                cp.then_inc(ys, 1)

            high(0, 0)
            for q, p, h in steps(act, nq):
                for f in range(FC):
                    if f == 6 and not last(q, nq, 1):
                        high(q + 1, 1 - p)
                    chunk(q, f)
                    if f == 2 and not first(q, 1):
                        y_out(q - 1, 1 - p)
            y_out(nq - 1, 1)

        @block.gpsimd
        def _(pool):
            half4 = K.half[:, 0:1].broadcast_to([P, SC])

            def deviation(q):
                pool.wait_ge(mvs, SC * (q + 1))
                pool.sem_inc(K.passed, 1)
                pool.tensor_scalar(ve[:, :], mv[:, :, 1], LN_EPS, 1.0, ALU.add, ALU.mult).then_inc(ves, 1)
                pool.wait_ge(ves, q + 1)
                if not first(q, 1):
                    pool.wait_ge(xhs, q)
                pool.tensor_tensor(rs[:, :], ve[:, :], half4, ALU.pow).then_inc(rss, 1)

            def chunk(q, p, f):
                if f == 0 and not first(q, 2):
                    pool.wait_ge(sum_mm, q - 1)
                pool.wait_ge(hqs, q * FC + f + 1)
                if f == 0:
                    pool.sem_inc(K.passed, 1)
                    pool.tensor_copy(s12[:, p, 1, :], hq[:, f % RG, :]).then_inc(summed2, 1)
                else:
                    pool.wait_ge(summed2, q * FC + f)
                    pool.tensor_tensor(s12[:, p, 1, :], s12[:, p, 1, :], hq[:, f % RG, :], ALU.add
                                       ).then_inc(summed2, 1)

            def deviation2(q):
                pool.wait_ge(vars_, q + 1)
                pool.sem_inc(K.passed, 1)
                pool.tensor_scalar(ve2[:, :], var[:, :], LN_EPS, 1.0, ALU.add, ALU.mult).then_inc(ve2s, 1)
                pool.wait_ge(ve2s, q + 1)
                if not first(q, 1):
                    pool.wait_ge(cas, q)
                pool.tensor_tensor(rs2[:, :], ve2[:, :], half4, ALU.pow).then_inc(rs2s, 1)

            def finish(q):
                for s in range(SC):
                    pool.wait_ge(o2, SC * q + s + 1)
                    pool.tensor_tensor(osb[:, s, :], osb[:, s, :], gu2[:, :], ALU.add).then_inc(o3, 1)

            deviation(0)
            for q, p, h in steps(pool, nq):
                if not last(q, nq, 1):
                    deviation(q + 1)
                for f in range(FC):
                    chunk(q, p, f)
                    if f == 2 and not first(q, 1):
                        deviation2(q - 1)
                    if f == 7 and not first(q, 1):
                        finish(q - 1)
            deviation2(nq - 1)
            finish(nq - 1)

        @block.sync
        def _(sp):
            with sp.Fori(0, nq) as q:
                sp.wait_ge(o3, SC * q + SC)
                sp.dma_start(outv[bass.ds(q, 1)].rearrange("a p s d -> p (a s) d"), osb[:, :, :]
                             ).then_inc(stored, 16)
            sp.wait_ge(stored, 16 * nq)

        @block.vector
        def _(dve):
            def row(q, s):
                return K.xres[:, bass.ds((q * SC + s) * D, D)]

            def stats(q):
                for s in range(SC):
                    dve.sem_inc(K.passed, 1)
                    dve.bn_stats(st[:, s, :], row(q, s)).then_inc(bns, 1)
                if not first(q, 1):
                    dve.wait_ge(ves, q)
                for s in range(SC):
                    dve.wait_ge(bns, SC * q + s + 1)
                    dve.sem_inc(K.passed, 1)
                    dve.bn_aggr(mv[:, s, :], st[:, s, :]).then_inc(mvs, 1)

            def normalise(q):
                dve.wait_ge(rss, q + 1)
                if not first(q, 1):
                    dve.wait_ge(tmm, q)
                for s in range(SC):
                    ins = dve.tensor_scalar(xh[:, s, :], row(q, s), mv[:, s, 0:1], rs[:, s:s + 1],
                                            ALU.subtract, ALU.mult)
                ins.then_inc(xhs, 1)

            def low_part(q, p):
                dve.wait_ge(th, q + 1)
                for c in range(DC):
                    ins = dve.tensor_tensor(xT[:, p, 1, c, :], tb[c][:, :], xT[:, p, 0, c, :], ALU.subtract)
                ins.then_inc(tl, 1)

            def chunk(q, p, f):
                dve.wait_ge(hh, q * FC + f + 1)
                dve.scalar_tensor_tensor(hT[:, f % RH, 1, :], hf[:, f % RG, :], lnw[:, f:f + 1],
                                         hT[:, f % RH, 0, :], ALU.mult, ALU.subtract).then_inc(hl, 1)
                if f == 0:
                    if not first(q, 2):
                        dve.wait_ge(sum_mm, q - 1)
                    dve.tensor_copy(s12[:, p, 0, :], hf[:, f % RG, :]).then_inc(summed1, 1)
                else:
                    dve.wait_ge(summed1, q * FC + f)
                    dve.tensor_tensor(s12[:, p, 0, :], s12[:, p, 0, :], hf[:, f % RG, :], ALU.add
                                      ).then_inc(summed1, 1)

            def moments(q):
                dve.wait_ge(sum_mm, q + 1)
                dve.tensor_scalar(m12[:, :], tb[0][:, 0:2 * SC], 1.0 / FF, None, ALU.mult).then_inc(m12s, 1)
                dve.wait_ge(m12s, q + 1)
                dve.tensor_tensor(msq[:, :], m12[:, 0:SC], m12[:, 0:SC], ALU.mult).then_inc(msqs, 1)
                dve.wait_ge(msqs, q + 1)
                dve.tensor_tensor(var[:, :], m12[:, SC:2 * SC], msq[:, :], ALU.subtract).then_inc(vars_, 1)

            def add(q):
                dve.wait_ge(rs2s, q + 1)
                dve.tensor_scalar(ca[:, :], rs2[:, :], g, None, ALU.mult).then_inc(cas, 1)
                dve.wait_ge(cas, q + 1)
                dve.scalar_tensor_tensor(cb[:, :], ca[:, :], -1.0, m12[:, 0:SC], ALU.mult, ALU.mult
                                         ).then_inc(cbs, 1)
                dve.wait_ge(ys, q + 1)
                dve.wait_ge(cbs, q + 1)
                if not first(q, 1):
                    dve.wait_ge(stored, 16 * q)

            def add_rows(q, rows):
                for s in rows:
                    dve.scalar_tensor_tensor(osb[:, s, :], ysb[:, s, :], ca[:, s:s + 1], row(q, s),
                                             ALU.mult, ALU.add).then_inc(o1, 1)
                for s in rows:
                    dve.wait_ge(o1, SC * q + s + 1)
                    dve.scalar_tensor_tensor(osb[:, s, :], u1[:, :], cb[:, s:s + 1], osb[:, s, :],
                                             ALU.mult, ALU.add).then_inc(o2, 1)

            stats(0)
            normalise(0)
            low_part(0, 0)
            for q, p, h in steps(dve, nq):
                for f in range(FC):
                    if f == 1 and not last(q, nq, 1):
                        stats(q + 1)
                    if f == 3 and not last(q, nq, 1):
                        normalise(q + 1)
                    if f == 3 and not first(q, 1):
                        moments(q - 1)
                    if f == 5 and not first(q, 1):
                        add(q - 1)
                        add_rows(q - 1, (0, 1))
                    if f == 7 and not first(q, 1):
                        add_rows(q - 1, (2, 3))
                    if f == 6 and not last(q, nq, 1):
                        low_part(q + 1, 1 - p)
                    chunk(q, p, f)
            moments(nq - 1)
            add(nq - 1)
            add_rows(nq - 1, range(SC))


def build(nc, K):
    with ExitStack() as ctx:
        setup(nc, ctx, K)
        with ExitStack() as stage:
            cross_attention(nc, stage, K)
            end_stage(nc, K)
        with ExitStack() as stage:
            assign_slots(nc, stage, K)
            end_stage(nc, K)
        with ExitStack() as stage:
            dispatch(nc, stage, K)
            end_stage(nc, K)
        with ExitStack() as stage:
            experts(nc, stage, K)
            end_stage(nc, K)
        K.spec = ctx.enter_context(nc.sbuf_tensor("spec", [P, K.n], F32))
        with ExitStack() as stage:
            combine_and_correlate(nc, stage, K)
            end_stage(nc, K)
        with ExitStack() as stage:
            pick_delays(nc, stage, K)
            end_stage(nc, K)
        with ExitStack() as stage:
            delayed_values(nc, stage, K)
            end_stage(nc, K)
        with ExitStack() as stage:
            ternary_ffn(nc, stage, K)
            end_stage(nc, K)


_NAMES = {
    "x": "x", "ctx_1024": "ctx", "mask_Bx1x1xS2_ik0": "mask", "g_xattn": "g_xattn", "g_ffn": "g_ffn",
    "L0_xattn_Wq": "Wq0", "L0_xattn_bq": "bq0", "L0_xattn_Wk": "Wk0", "L0_xattn_bk": "bk0",
    "L0_xattn_Wv": "Wv0", "L0_xattn_bv": "bv0", "L0_xattn_Wo": "Wo0", "L0_xattn_bo": "bo0",
    "L0_ffn_Wr": "Wr", "L0_ffn_W1": "W1", "L0_ffn_W2": "W2",
    "L1_xattn_Wq": "Wq1", "L1_xattn_bq": "bq1", "L1_xattn_Wk": "Wk1", "L1_xattn_bk": "bk1",
    "L1_xattn_Wv": "Wv1", "L1_xattn_bv": "bv1", "L1_xattn_Wo": "Wo1", "L1_xattn_bo": "bo1",
    "L1_ffn_W_fc": "Wfc", "L1_ffn_ln_w": "lnw", "L1_ffn_ln_b": "lnb", "L1_ffn_W_proj": "Wpr",
}


def _constants(n, cap):
    time = np.arange(P)
    freq = np.concatenate([np.arange(P // 2 + 1), np.arange(1, P // 2)])
    angle = 2 * np.pi * ((time[:, None] * freq[None, :]) % P) / P
    cosine = np.arange(P) <= P // 2
    dft = np.where(cosine[None, :], np.cos(angle), np.sin(angle))
    weight = np.where((freq == 0) | (freq == P // 2), 1.0, 2.0)[:, None] / (P * D)
    return {
        "dft": dft.astype(np.float32),
        "idft": (weight * dft.T).astype(np.float32),
        "mask_parts": np.array(MASK_PARTS, np.float32)[:, None],
        "rank": np.arange(E, 0, -1).astype(np.float32),
        "start": (np.arange(E) * cap - 1).astype(np.float32),
        "spare": (E * cap + np.arange(n)[None, :] * P + np.arange(P)[:, None]).astype(np.float32),
    }


def _program(nc, arrays, n, cap):
    K = Kernel()
    K.n, K.cap = n, cap
    K.group = max(g for g in (128, 256, 384, 512) if cap % g == 0)
    K.signals = []

    def given(*names):
        return [nc.dram_tensor(name, arrays[name].shape, mybir.dt.from_np(arrays[name].dtype),
                               kind="ExternalInput").ap() for name in names]

    K.x, K.ctx, K.mask, K.g_xattn, K.g_ffn = given("x", "ctx", "mask", "g_xattn", "g_ffn")
    K.Wq0, K.Wk0, K.Wv0, K.Wo0 = given("Wq0", "Wk0", "Wv0", "Wo0")
    K.bq0, K.bk0, K.bv0, K.bo0 = given("bq0", "bk0", "bv0", "bo0")
    K.Wr, K.W1, K.W2 = given("Wr", "W1", "W2")
    K.Wq1, K.Wk1, K.Wv1, K.Wo1 = given("Wq1", "Wk1", "Wv1", "Wo1")
    K.bq1, K.bk1, K.bv1, K.bo1 = given("bq1", "bk1", "bv1", "bo1")
    K.Wfc, K.lnw, K.lnb, K.Wpr = given("Wfc", "lnw", "lnb", "Wpr")
    K.dft, K.idft, K.mask_parts = given("dft", "idft", "mask_parts")
    K.rank, K.start, K.spare = given("rank", "start", "spare")
    K.out = nc.dram_tensor("out", (n, P, D), F32, kind="ExternalOutput").ap()
    K.disp = nc.dram_tensor("disp", (E * cap + n * P, D), F32, kind="Internal").ap()
    K.eout = nc.dram_tensor("eout", (E * cap, D), F32, kind="Internal").ap()
    K.circ = nc.dram_tensor("circ", (n, 2 * P), F32, kind="Internal").ap()
    build(nc, K)


def kernel(**inputs):
    import concourse.bacc as _bacc
    from concourse.bass_utils import run_bass_kernel_spmd as _run

    nc = _bacc.Bacc("TRN2", target_bir_lowering=False, num_devices=1)
    arrays = {short: np.ascontiguousarray(inputs[name]) for name, short in _NAMES.items()}
    n = arrays["x"].shape[0]
    cap = int(1.25 * n * P / E)
    arrays.update(_constants(n, cap))
    _program(nc, arrays, n, cap)
    return _run(nc, [arrays], core_ids=[0]).results[0]["out"]
```

```python
from contextlib import ExitStack

import numpy as np

import concourse.bass as bass
from concourse import mybir

F32 = mybir.dt.float32
BF16 = mybir.dt.bfloat16
I32 = mybir.dt.int32
U32 = mybir.dt.uint32
ALU = mybir.AluOpType
ACT = mybir.ActivationFunctionType
AX = mybir.AxisListType

P = 128
D = 256
DC = D // P
H = 16
DH = D // H
HC = H // DC
UNIT = 4
NU = H // UNIT
E = 8
FF = 1024
FC = FF // P
TOPK = 9
LN_EPS = 1e-5
MASK_PARTS = (-998244352.0, -1753088.0, -2560.0)
LOWEST = -3.0e38


def steps(eng, n):
    yield 0, 0, 0
    yield 1, 1, 0
    pairs = 2 if (n - 4) % 4 == 0 else 1
    if n > 4:
        with eng.Fori(0, (n - 4) // (2 * pairs)) as j:
            for i in range(pairs):
                for p in range(2):
                    yield 2 * pairs * j + 2 * i + 2 + p, p, pairs * j + i + 1
    yield n - 2, 0, (n - 2) // 2
    yield n - 1, 1, (n - 2) // 2


def first(b, k):
    return isinstance(b, int) and b < k


def last(b, n, k):
    return isinstance(b, int) and b >= n - k


def two_on(b, p, u):
    return (b, p, u + 2) if u + 2 < NU else (b + 1, 1 - p, u + 2 - NU)


def one_back(b, u):
    return (b, u - 1) if u else (b - 1, NU - 1)


def two_back(b, p, u):
    return (b, p, u - 2) if u >= 2 else (b - 1, 1 - p, u - 2 + NU)


def quads(eng, n):
    for r in range(4):
        yield r, r, 0
    if n > 8:
        with eng.Fori(1, n // 4 - 1) as j:
            for r in range(4):
                yield 4 * j + r, r, j
    for r in range(4):
        yield n - 4 + r, r, n // 4 - 1


class Kernel:
    pass


def new_signal(nc, K, name):
    K.signals.append(nc.alloc_semaphore(name=name))
    return K.signals[-1]


def end_stage(nc, K):
    nc.clear_and_free_semaphores(K.signals)
    nc.all_engine_barrier()
    K.signals = []


def setup(nc, ctx, K):
    def sb(name, shape, dt=F32):
        return ctx.enter_context(nc.sbuf_tensor(name, shape, dt))

    def sem(name):
        return ctx.enter_context(nc.semaphore(name))

    n = K.n
    K.xres = sb("xres", [P, n * D])
    K.ident = sb("ident", [P, P])
    K.ones = sb("ones", [P, P])
    K.gates = sb("gates", [P, 4])
    K.ln2 = sb("ln2", [P, n, 2])
    K.slot = sb("slot", [P, n], U32)
    K.read = sb("read", [P, n], U32)
    K.wexp = sb("wexp", [P, n])
    K.wself = sb("wself", [P, n])
    K.half = sb("half", [P, 1])

    made = sem("const_made")
    loaded = sem("gates_loaded")
    gated = sem("gated")
    K.passed = sem("passed")
    with nc.Block() as block:

        @block.gpsimd
        def _(pool):
            pool.memset(K.ident[:, :], 0.0).then_inc(made, 1)
            pool.wait_ge(made, 1)
            pool.memset(K.ones[:, :], 1.0).then_inc(made, 1)
            pool.memset(K.half[:, :], -0.5).then_inc(made, 1)
            pool.affine_select(out=K.ident[:, :], in_=K.ident[:, :], compare_op=ALU.not_equal, fill=1.0,
                               base=0, pattern=[[-1, P]], channel_multiplier=1).then_inc(made, 1)
            pool.wait_ge(made, 4)

        @block.sync
        def _(sp):
            sp.dma_start(K.gates[:, 0:2], K.g_xattn.partition_broadcast(P)).then_inc(loaded, 16)
            sp.dma_start(K.gates[:, 2:4], K.g_ffn.partition_broadcast(P)).then_inc(loaded, 16)

        @block.scalar
        def _(act):
            act.wait_ge(loaded, 32)
            act.activation(K.gates[:, :], K.gates[:, :], ACT.Tanh).then_inc(gated, 1)
            act.wait_ge(gated, 1)


def transpose_square(pe, bank, rows, ident):
    for ki in range(DC):
        for ko in range(DC):
            mm = pe.transpose(bank[:, ki * D + ko * P:ki * D + (ko + 1) * P],
                              rows[:, ko, ki * P:(ki + 1) * P], ident[:, :])
    return mm


def cross_attention(nc, ctx, K):

    def sb(name, shape, dt=F32):
        return ctx.enter_context(nc.sbuf_tensor(name, shape, dt))

    def psum(name):
        return ctx.enter_context(nc.psum_tensor(name, [P, 512], F32))

    def sem(name):
        return new_signal(nc, K, "a_" + name)

    n = K.n
    g = K.gates[:, 0:1]
    scale = DH ** -0.5
    wq, wk, wv, wo = (sb(f"a_w{c}T", [P, DC, D]) for c in "qkvo")
    wr = sb("a_wr", [P, DC, E])
    bq = sb("a_bq", [P, DC])
    bk = sb("a_bk", [P, DC])
    bv = sb("a_bv", [P, DC])
    gbias = sb("a_gbias", [P, D])
    headmask = sb("a_headmask", [P, HC, P])
    ones3 = sb("a_ones3", [3, P], BF16)
    parts = sb("a_parts", [3, 1])
    ZR = E * K.cap // n
    zeros = sb("a_zeros", [P, 2 * D])

    banks = [psum(f"a_bank{i}") for i in range(8)]
    sbank, tbank, pvbank, fbank, qkbank, bbank = banks[0:2], banks[2:4], banks[4], banks[5], banks[6], banks[7]

    w_loaded = sem("w_loaded")
    w_turned = sem("w_turned")
    w_ready = sem("w_ready")
    bias_mm = sem("bias_mm")
    hm = sem("headmask")
    zero_made = sem("zero_made")

    with ExitStack() as prep, nc.Block() as block:
        raw = prep.enter_context(nc.sbuf_tensor("a_raw", [P, 4, DC, D], F32))
        bvb = prep.enter_context(nc.sbuf_tensor("a_bvb", [P, DC, P], F32))
        bob = prep.enter_context(nc.sbuf_tensor("a_bob", [P, D], F32))

        @block.sync
        def _(sp):
            for i, w in enumerate((K.Wq0, K.Wk0, K.Wv0, K.Wo0)):
                sp.dma_start(raw[:, i], w.rearrange("(c p) d -> p c d", p=P)).then_inc(w_loaded, 16)
            sp.dma_start(wr[:, :, :], K.Wr.rearrange("(c p) e -> p c e", p=P)).then_inc(w_loaded, 16)
            for t, v in ((bq, K.bq0), (bk, K.bk0), (bv, K.bv0)):
                sp.dma_start(t[:, :], v.rearrange("(c p) -> p c", p=P), allow_slow_non_contiguous=True).then_inc(w_loaded, 16)
            sp.dma_start(bob[:, :], K.bo0.partition_broadcast(P)).then_inc(w_loaded, 16)
            sp.dma_start(parts[:, :], K.mask_parts).then_inc(w_loaded, 16)

        @block.gpsimd
        def _(pool):
            pool.memset(headmask[:, :, :], 1.0).then_inc(hm, 1)
            pool.memset(ones3[:, :], 1.0).then_inc(hm, 1)
            pool.wait_ge(hm, 1)
            pool.affine_select(out=headmask[:, :, :], in_=headmask[:, :, :], compare_op=ALU.is_ge, fill=0.0,
                               base=0, pattern=[[-DH, HC], [0, P]], channel_multiplier=1).then_inc(hm, 1)
            pool.wait_ge(hm, 3)
            pool.affine_select(out=headmask[:, :, :], in_=headmask[:, :, :], compare_op=ALU.is_ge, fill=0.0,
                               base=DH - 1, pattern=[[DH, HC], [0, P]], channel_multiplier=-1).then_inc(hm, 1)
            pool.wait_ge(hm, 4)

        @block.tensor
        def _(pe):
            pe.wait_ge(w_loaded, 16 * 10)
            for i in range(4):
                transpose_square(pe, banks[i], raw[:, i], K.ident).then_inc(w_turned, 1)
            pe.wait_ge(w_ready, 5)
            for c in range(DC):
                mm = pe.matmul(banks[4][:, 0:D], bvb[:, c, :], wo[:, c, :], start=c == 0, stop=c == DC - 1)
            mm.then_inc(bias_mm, 1)

        @block.vector
        def _(dve):
            dve.memset(zeros[:, :], 0.0).then_inc(zero_made, 1)
            dve.wait_ge(w_loaded, 16 * 10)
            for c in range(DC):
                cc = dve.tensor_scalar(bvb[:, c, :], K.ones[:, :], bv[:, c:c + 1], None, ALU.mult)
            cc.then_inc(w_ready, 1)
            dve.wait_ge(w_turned, 1)
            dve.tensor_scalar(wq[:, :, :].rearrange("p c d -> p (c d)"), banks[0][:, :], scale, None, ALU.mult)
            dve.tensor_scalar(bq[:, :], bq[:, :], scale, None, ALU.mult).then_inc(w_ready, 1)
            for i, w in enumerate((wk, wv, wo)):
                dve.wait_ge(w_turned, i + 2)
                dve.tensor_copy(w[:, :, :].rearrange("p c d -> p (c d)"), banks[i + 1][:, :]).then_inc(w_ready, 1)
            dve.wait_ge(bias_mm, 1)
            dve.tensor_tensor(gbias[:, :], banks[4][:, 0:D], bob[:, :], ALU.add).then_inc(w_ready, 1)
            dve.wait_ge(w_ready, 6)
            dve.tensor_scalar(gbias[:, :], gbias[:, :], g, None, ALU.mult).then_inc(w_ready, 1)
            dve.wait_ge(w_ready, 7)

    xin = sb("a_xin", [P, 2, D])
    cin = sb("a_cin", [P, 2, D])
    min_ = sb("a_mask", [P, 2, P], I32)
    xhat = sb("a_xhat", [P, D])
    keep = sb("a_keep", [P, P])
    inv = sb("a_inv", [3, P])
    madd = sb("a_madd", [3, 2, P], BF16)
    ft = sb("a_ft", [P, 2 * D])
    qT = sb("a_qT", [P, 2, DC, P])
    kT = sb("a_kT", [P, DC, P])
    km = sb("a_km", [P, 2, H, P])
    va = sb("a_va", [P, 2, H, 2, DH], BF16)
    den = sb("a_den", [P, 2, H])
    negm = sb("a_negm", [P, 2, UNIT])
    pr = sb("a_pr", [P, 2, UNIT, P])
    pT = sb("a_pT", [P, 2, 2, UNIT, P], BF16)
    pvsum = sb("a_pvsum", [P, D])
    rden = sb("a_rden", [P, H])
    co = sb("a_co", [P, D])
    coT = sb("a_coT", [P, D])
    st1, st2 = sb("a_st1", [P, 6]), sb("a_st2", [P, 6])
    mv1, mv2 = sb("a_mv1", [P, 2]), sb("a_mv2", [P, 2])
    ve1, ve2 = sb("a_ve1", [P, 1]), sb("a_ve2", [P, 1])
    rs1, rs2 = sb("a_rs1", [P, 1]), sb("a_rs2", [P, 1])
    t = sb("a_t", [P, D])
    tT = sb("a_tT", [P, D])

    ld = [sem("ld0"), sem("ld1")]
    zeroed = sem("zeroed")
    bn1, mv1s, ve1s, rs1s = sem("bn1"), sem("mv1"), sem("ve1"), sem("rs1")
    bn2, mv2s, ve2s, rs2s, ln2s = sem("bn2"), sem("mv2"), sem("ve2"), sem("rs2"), sem("ln2")
    pre = sem("preadded")
    invs, madds, keeps = sem("inv"), sem("madd"), sem("keep")
    xhs, fts_mm, fts = sem("xhat"), sem("ft_mm"), sem("ft")
    qkmm, vmm = sem("qk_mm"), sem("v_mm")
    qs, ks, vs, kms = sem("q"), sem("k"), sem("v"), sem("km")
    smm, negs, exps = sem("scores"), sem("negmax"), sem("exp")
    tmm, pTd, pTa = sem("pt_mm"), sem("pt_dve"), sem("pt_act")
    pvs, rdens, cos, cot_mm, cots = sem("pv"), sem("rden"), sem("co"), sem("coT_mm"), sem("coT")
    ymm, xress, ts, tt_mm, tts, lgmm, lgs = (sem("y_mm"), sem("xres"), sem("t"), sem("tT_mm"), sem("tT"),
                                             sem("logit_mm"), sem("logit"))
    vhs, pvsums = sem("v_high"), sem("pvsum")

    xv, cv = K.x, K.ctx
    mask = K.mask.rearrange("b x y s -> (b x y) s")

    with nc.Block() as block:

        @block.sync
        def _(sp):
            for b, p, h in steps(sp, n):
                if not first(b, 2):
                    sp.wait_ge(xhs, b - 1)
                    sp.wait_ge(pre, b - 1)
                    sp.wait_ge(fts_mm, b - 1)
                    sp.wait_ge(keeps, b - 1)
                    sp.wait_ge(invs, b - 1)
                sp.dma_start(xin[:, p, :], xv[bass.ds(b, 1)].rearrange("a p d -> p (a d)")).then_inc(ld[p], 16)
                sp.dma_start(cin[:, p, :], cv[bass.ds(b, 1)].rearrange("a p d -> p (a d)")).then_inc(ld[p], 16)
                sp.dma_start(min_[:, p, :], mask[bass.ds(b, 1), :].rearrange("a s -> (a s)").partition_broadcast(P)
                             ).then_inc(ld[p], 16)
                sp.dma_start(K.disp[bass.ds(b * ZR, ZR), :].rearrange("(p k) d -> p (k d)", k=2),
                             zeros[0:ZR // 2, :]).then_inc(zeroed, 16)
            sp.wait_ge(zeroed, 16 * n)

        @block.gpsimd
        def _(pool):
            def front(b, p, h):
                pool.wait_ge(mv1s, b + 1)
                pool.sem_inc(K.passed, 1)
                pool.tensor_scalar(ve1[:, :], mv1[:, 1:2], LN_EPS, 1.0, ALU.add, ALU.mult).then_inc(ve1s, 1)
                pool.wait_ge(ve1s, b + 1)
                if not first(b, 1):
                    pool.wait_ge(xhs, b)
                pool.tensor_tensor(rs1[:, :], ve1[:, :], K.half[:, :], ALU.pow).then_inc(rs1s, 1)
                pool.wait_ge(ld[p], 48 * h + 48)
                pool.tensor_tensor(K.xres[:, bass.ds(b * D, D)], xin[:, p, :], gbias[:, :], ALU.add
                                   ).then_inc(pre, 1)

            def keys(b, p, c):
                pool.wait_ge(ks, b + 1)
                if not first(b, 2):
                    pool.wait_ge(smm, (b - 1) * NU)
                pool.tensor_tensor(km[:, p, c * HC:(c + 1) * HC, :],
                                   kT[:, c, :].unsqueeze(1).broadcast_to([P, HC, P]),
                                   headmask[:, :, :], ALU.mult).then_inc(kms, 1)

            def after(b):
                pool.wait_ge(mv2s, b + 1)
                pool.sem_inc(K.passed, 1)
                pool.tensor_scalar(ve2[:, :], mv2[:, 1:2], LN_EPS, 1.0, ALU.add, ALU.mult).then_inc(ve2s, 1)
                pool.wait_ge(ve2s, b + 1)
                if not first(b, 1):
                    pool.wait_ge(ts, b)
                pool.tensor_tensor(rs2[:, :], ve2[:, :], K.half[:, :], ALU.pow).then_inc(rs2s, 1)
                pool.sem_inc(K.passed, 1)
                pool.tensor_copy(K.ln2[:, bass.ds(b, 1), 0:1].rearrange("p a c -> p (a c)"),
                                 mv2[:, 0:1]).then_inc(ln2s, 1)
                pool.wait_ge(rs2s, b + 1)
                pool.sem_inc(K.passed, 1)
                pool.tensor_copy(K.ln2[:, bass.ds(b, 1), 1:2].rearrange("p a c -> p (a c)"),
                                 rs2[:, :]).then_inc(ln2s, 1)

            front(0, 0, 0)
            keys(0, 0, 0)
            keys(0, 0, 1)
            front(1, 1, 0)
            for b, p, h in steps(pool, n):
                if not last(b, n, 1):
                    keys(b + 1, 1 - p, 0)
                    keys(b + 1, 1 - p, 1)
                if not last(b, n, 2):
                    front(b + 2, p, h + 1)
                if not first(b, 1):
                    after(b - 1)
            after(n - 1)
            pool.wait_ge(ln2s, 2 * n)

        @block.tensor
        def _(pe):
            def turn_inputs(b, p, h):
                pe.wait_ge(xhs, b + 1)
                pe.wait_ge(ld[p], 48 * h + 48)
                if not first(b, 1):
                    pe.wait_ge(vs, b)
                for c in range(DC):
                    pe.transpose(fbank[:, c * P:(c + 1) * P], xhat[:, c * P:(c + 1) * P], K.ident[:, :])
                for c in range(DC):
                    mm = pe.transpose(fbank[:, D + c * P:D + (c + 1) * P], cin[:, p, c * P:(c + 1) * P],
                                      K.ident[:, :])
                mm.then_inc(fts_mm, 1)

            def project_qk(b):
                pe.wait_ge(fts, b + 1)
                if not first(b, 1):
                    pe.wait_ge(qs, b)
                    pe.wait_ge(ks, b)
                for o, (w, src) in enumerate(((wq, 0), (wk, D))):
                    for m in range(DC):
                        for c in range(DC):
                            mm = pe.matmul(qkbank[:, o * D + m * P:o * D + (m + 1) * P],
                                           w[:, c, m * P:(m + 1) * P], ft[:, src + c * P:src + (c + 1) * P],
                                           start=c == 0, stop=c == DC - 1)
                mm.then_inc(qkmm, 1)

            def project_v(b):
                pe.wait_ge(fts, b + 1)
                for c in range(DC):
                    mm = pe.matmul(fbank[:, 0:D], ft[:, D + c * P:D + (c + 1) * P], wv[:, c, :],
                                   start=c == 0, stop=c == DC - 1)
                mm.then_inc(vmm, 1)

            def scores(b, p, u):
                c = u * UNIT // HC
                if u == 0:
                    pe.wait_ge(qs, b + 1)
                    pe.wait_ge(madds, b + 1)
                pe.wait_ge(kms, b * DC + c + 1)
                if u >= 2:
                    pe.wait_ge(exps, b * NU + u - 1)
                elif not first(b, 1):
                    pe.wait_ge(exps, b * NU + u - 1)
                pe.matmul(sbank[u % 2][:, :], ones3[:, :],
                          madd[:, p, :].unsqueeze(1).broadcast_to([3, UNIT, P]), start=True, stop=False)
                pe.matmul(sbank[u % 2][:, :], qT[:, p, c, :], km[:, p, u * UNIT:(u + 1) * UNIT, :],
                          start=False, stop=True).then_inc(smm, 1)

            def turn_probs(b, u):
                pe.wait_ge(exps, b * NU + u + 1)
                if not first(b, 1) or u >= 2:
                    pe.wait_ge(pTd, b * NU + u - 1)
                for j in range(UNIT):
                    mm = pe.transpose(tbank[u % 2][:, j * P:(j + 1) * P], pr[:, u % 2, j, :], K.ident[:, :])
                mm.then_inc(tmm, 1)

            def weigh(b, p, u):
                pe.wait_ge(pTd, b * NU + u + 1)
                if u == 0:
                    pe.wait_ge(vs, b + 1)
                    if not first(b, 1):
                        pe.wait_ge(pvsums, 2 * b)
                for j in range(UNIT):
                    hh = u * UNIT + j
                    pe.matmul(pvbank[:, hh * 2 * DH:(hh + 1) * 2 * DH], pT[:, u % 2, 0, j, :],
                              va[:, p, hh, :, :], start=True, stop=False)
                    mm = pe.matmul(pvbank[:, hh * 2 * DH:hh * 2 * DH + DH], pT[:, u % 2, 1, j, :],
                                   va[:, p, hh, 0, :], start=False, stop=True)
                mm.then_inc(pvs, 1)

            def turn_context(b):
                pe.wait_ge(cos, b + 1)
                if not first(b, 1):
                    pe.wait_ge(lgs, b)
                for c in range(DC):
                    mm = pe.transpose(bbank[:, c * P:(c + 1) * P], co[:, c * P:(c + 1) * P], K.ident[:, :])
                mm.then_inc(cot_mm, 1)

            def out_project(b):
                pe.wait_ge(cots, b + 1)
                for c in range(DC):
                    mm = pe.matmul(bbank[:, D:2 * D], coT[:, c * P:(c + 1) * P], wo[:, c, :],
                                   start=c == 0, stop=c == DC - 1)
                mm.then_inc(ymm, 1)

            def turn_t(b):
                pe.wait_ge(ts, b + 1)
                for c in range(DC):
                    mm = pe.transpose(bbank[:, D + c * P:D + (c + 1) * P], t[:, c * P:(c + 1) * P],
                                      K.ident[:, :])
                mm.then_inc(tt_mm, 1)

            def route(b):
                pe.wait_ge(tts, b + 1)
                for c in range(DC):
                    mm = pe.matmul(bbank[:, 0:E], tT[:, c * P:(c + 1) * P], wr[:, c, :],
                                   start=c == 0, stop=c == DC - 1)
                mm.then_inc(lgmm, 1)

            turn_inputs(0, 0, 0)
            project_qk(0)
            project_v(0)
            turn_inputs(1, 1, 0)
            scores(0, 0, 0)
            scores(0, 0, 1)
            for b, p, h in steps(pe, n):
                for u in range(NU):
                    if u < 2 or not last(b, n, 1):
                        scores(*two_on(b, p, u))
                    if u == 0 and not last(b, n, 1):
                        project_qk(b + 1)
                    if u >= 2 or not first(b, 1):
                        weigh(*two_back(b, p, u))
                    turn_probs(b, u)
                    if u == 1 and not last(b, n, 1):
                        project_v(b + 1)
                    if u == 0 and not first(b, 2):
                        turn_t(b - 2)
                    if u == 1 and not first(b, 2):
                        route(b - 2)
                    if u == 2 and not first(b, 1):
                        turn_context(b - 1)
                    if u == 3 and not first(b, 1):
                        out_project(b - 1)
                    if u == 3 and not last(b, n, 2):
                        turn_inputs(b + 2, p, h + 1)
            weigh(n - 1, 1, NU - 2)
            weigh(n - 1, 1, NU - 1)
            turn_t(n - 2)
            route(n - 2)
            turn_context(n - 1)
            out_project(n - 1)
            turn_t(n - 1)
            route(n - 1)

        @block.scalar
        def _(act):
            def exp_unit(b, p, u):
                act.wait_ge(negs, b * NU + u + 1)
                if u >= 2 or not first(b, 1):
                    act.wait_ge(tmm, b * NU + u - 1)
                if u == 0 and not first(b, 2):
                    act.wait_ge(rdens, b - 1)
                for j in range(UNIT):
                    ex = act.activation(pr[:, u % 2, j, :], sbank[u % 2][:, j * P:(j + 1) * P], ACT.Exp,
                                        bias=negm[:, u % 2, j:j + 1],
                                        accum_out=den[:, p, u * UNIT + j:u * UNIT + j + 1])
                ex.then_inc(exps, 1)

            def inputs_out(b):
                act.wait_ge(fts_mm, b + 1)
                if not first(b, 1):
                    act.wait_ge(vmm, b)
                act.activation(ft[:, :], fbank[:, :], ACT.Copy).then_inc(fts, 1)

            def q_out(b, p):
                act.wait_ge(ks, b + 1)
                if not first(b, 2):
                    act.wait_ge(smm, (b - 1) * NU)
                for c in range(DC):
                    cp = act.activation(qT[:, p, c, :], qkbank[:, c * P:(c + 1) * P], ACT.Identity,
                                        bias=bq[:, c:c + 1])
                cp.then_inc(qs, 1)

            def probs_out(b, u):
                act.wait_ge(tmm, b * NU + u + 1)
                if u >= 2 or not first(b, 1):
                    act.wait_ge(pvs, b * NU + u - 1)
                act.activation(pT[:, u % 2, 0, :, :].rearrange("p a k -> p (a k)"), tbank[u % 2][:, :],
                               ACT.Copy).then_inc(pTa, 1)

            def v_high(b, p):
                act.wait_ge(vmm, b + 1)
                if not first(b, 2):
                    act.wait_ge(pvs, (b - 1) * NU)
                act.activation(va[:, p, :, 0, :], fbank[:, 0:D].rearrange("p (h d) -> p h d", d=DH), ACT.Copy
                               ).then_inc(vhs, 1)

            def context_out(b):
                act.wait_ge(cot_mm, b + 1)
                if not first(b, 1):
                    act.wait_ge(ymm, b)
                act.activation(coT[:, :], bbank[:, 0:D], ACT.Copy).then_inc(cots, 1)

            def t_out(b):
                act.wait_ge(tt_mm, b + 1)
                if not first(b, 1):
                    act.wait_ge(lgmm, b)
                act.activation(tT[:, :], bbank[:, D:2 * D], ACT.Copy).then_inc(tts, 1)

            inputs_out(0)
            q_out(0, 0)
            v_high(0, 0)
            inputs_out(1)
            exp_unit(0, 0, 0)
            exp_unit(0, 0, 1)
            for b, p, h in steps(act, n):
                for u in range(NU):
                    if u == 1 and not first(b, 2):
                        t_out(b - 2)
                    if u or not first(b, 1):
                        probs_out(*one_back(b, u))
                    if u == 1 and not last(b, n, 1):
                        q_out(b + 1, 1 - p)
                    if u == 2 and not last(b, n, 1):
                        v_high(b + 1, 1 - p)
                    if u == 2 and not first(b, 1):
                        context_out(b - 1)
                    if u < 2 or not last(b, n, 1):
                        exp_unit(*two_on(b, p, u))
                    if u == 3 and not last(b, n, 2):
                        inputs_out(b + 2)
            probs_out(n - 1, NU - 1)
            t_out(n - 2)
            context_out(n - 1)
            t_out(n - 1)

        @block.vector
        def _(dve):
            def stats(b, p, h):
                dve.wait_ge(ld[p], 48 * h + 48)
                dve.sem_inc(K.passed, 1)
                dve.bn_stats(st1[:, :], xin[:, p, :]).then_inc(bn1, 1)
                dve.wait_ge(bn1, b + 1)
                if not first(b, 1):
                    dve.wait_ge(ve1s, b)
                dve.sem_inc(K.passed, 1)
                dve.bn_aggr(mv1[:, :], st1[:, :]).then_inc(mv1s, 1)

            def masks(b, p):
                dve.tensor_scalar(inv[:, :], min_[0:3, p, :], 0.0, None, ALU.is_equal).then_inc(invs, 1)
                if not first(b, 1):
                    dve.wait_ge(ks, b)
                dve.tensor_scalar(keep[:, :], min_[:, p, :], 0.0, None, ALU.not_equal).then_inc(keeps, 1)
                dve.wait_ge(invs, b + 1)
                if not first(b, 2):
                    dve.wait_ge(smm, (b - 1) * NU)
                dve.tensor_scalar(madd[:, p, :], inv[:, :], parts[:, 0:1], None, ALU.mult).then_inc(madds, 1)

            def normalise_in(b, p):
                dve.wait_ge(rs1s, b + 1)
                if not first(b, 1):
                    dve.wait_ge(fts_mm, b)
                dve.tensor_scalar(xhat[:, :], xin[:, p, :], mv1[:, 0:1], rs1[:, 0:1], ALU.subtract, ALU.mult
                                  ).then_inc(xhs, 1)

            def unit_max(b, u):
                dve.wait_ge(smm, b * NU + u + 1)
                if u >= 2 or not first(b, 1):
                    dve.wait_ge(exps, b * NU + u - 1)
                dve.tensor_reduce(negm[:, u % 2, :], sbank[u % 2][:, :].rearrange("p (a k) -> p a k", k=P),
                                  AX.X, ALU.max, negate=True).then_inc(negs, 1)

            def probs_out(b, u):
                dve.wait_ge(pTa, b * NU + u + 1)
                dve.tensor_tensor(pT[:, u % 2, 1, :, :].rearrange("p a k -> p (a k)"), tbank[u % 2][:, :],
                                  pT[:, u % 2, 0, :, :].rearrange("p a k -> p (a k)"), ALU.subtract
                                  ).then_inc(pTd, 1)

            def k_out(b):
                dve.wait_ge(qkmm, b + 1)
                if not first(b, 1):
                    dve.wait_ge(kms, b * DC)
                for c in range(DC):
                    cp = dve.scalar_tensor_tensor(kT[:, c, :], qkbank[:, D + c * P:D + (c + 1) * P],
                                                  bk[:, c:c + 1], keep[:, :], ALU.add, ALU.mult)
                cp.then_inc(ks, 1)

            def v_out(b, p):
                dve.wait_ge(vhs, b + 1)
                dve.tensor_tensor(va[:, p, :, 1, :], fbank[:, 0:D].rearrange("p (h d) -> p h d", d=DH),
                                  va[:, p, :, 0, :], ALU.subtract).then_inc(vs, 1)

            def context(b, p):
                dve.wait_ge(exps, (b + 1) * NU)
                dve.reciprocal(rden[:, :], den[:, p, :]).then_inc(rdens, 1)
                dve.wait_ge(pvs, (b + 1) * NU)
                pv = pvbank[:, :].rearrange("p (h a d) -> p h a d", a=2, d=DH)
                sums = pvsum[:, :].rearrange("p (h d) -> p h d", d=DH)
                dve.tensor_copy(sums, pv[:, :, 1, :]).then_inc(pvsums, 1)
                dve.wait_ge(pvsums, 2 * b + 1)
                dve.tensor_tensor(sums, pv[:, :, 0, :], sums, ALU.add).then_inc(pvsums, 1)
                dve.wait_ge(rdens, b + 1)
                dve.wait_ge(pvsums, 2 * b + 2)
                if not first(b, 1):
                    dve.wait_ge(cot_mm, b)
                dve.tensor_tensor(co[:, :].rearrange("p (h d) -> p h d", d=DH), sums,
                                  rden[:, :].unsqueeze(2).broadcast_to([P, H, DH]), ALU.mult).then_inc(cos, 1)

            def residual(b):
                dve.wait_ge(ymm, b + 1)
                dve.wait_ge(pre, b + 1)
                row = K.xres[:, bass.ds(b * D, D)]
                dve.scalar_tensor_tensor(row, bbank[:, D:2 * D], g, row, ALU.mult, ALU.add).then_inc(xress, 1)
                dve.wait_ge(xress, b + 1)
                dve.sem_inc(K.passed, 1)
                dve.bn_stats(st2[:, :], row).then_inc(bn2, 1)
                dve.wait_ge(bn2, b + 1)
                if not first(b, 1):
                    dve.wait_ge(ve2s, b)
                    dve.wait_ge(ln2s, 2 * b)
                dve.sem_inc(K.passed, 1)
                dve.bn_aggr(mv2[:, :], st2[:, :]).then_inc(mv2s, 1)

            def normalise_out(b):
                dve.wait_ge(rs2s, b + 1)
                if not first(b, 1):
                    dve.wait_ge(tt_mm, b)
                dve.tensor_scalar(t[:, :], K.xres[:, bass.ds(b * D, D)], mv2[:, 0:1], rs2[:, 0:1],
                                  ALU.subtract, ALU.mult).then_inc(ts, 1)

            def logits_out(b):
                dve.wait_ge(lgmm, b + 1)
                dve.tensor_copy(K.logits[:, bass.ds(b, 1), :].rearrange("p a e -> p (a e)"), bbank[:, 0:E]
                                ).then_inc(lgs, 1)

            stats(0, 0, 0)
            masks(0, 0)
            normalise_in(0, 0)
            k_out(0)
            v_out(0, 0)
            stats(1, 1, 0)
            masks(1, 1)
            normalise_in(1, 1)
            unit_max(0, 0)
            unit_max(0, 1)
            for b, p, h in steps(dve, n):
                for u in range(NU):
                    if u < 2 or not last(b, n, 1):
                        b2, _, u2 = two_on(b, p, u)
                        unit_max(b2, u2)
                    if u == 0 and not first(b, 2):
                        normalise_out(b - 2)
                    if u == 3 and not last(b, n, 2):
                        normalise_in(b + 2, p)
                    if u or not first(b, 1):
                        probs_out(*one_back(b, u))
                    if u == 0 and not last(b, n, 1):
                        k_out(b + 1)
                    if u == 2 and not last(b, n, 1):
                        v_out(b + 1, 1 - p)
                    if u == 1 and not first(b, 1):
                        context(b - 1, 1 - p)
                    if u == 1 and not first(b, 2):
                        logits_out(b - 2)
                    if u == 0 and not last(b, n, 2):
                        stats(b + 2, p, h + 1)
                    if u == 2 and not last(b, n, 2):
                        masks(b + 2, p)
                    if u == 3 and not first(b, 1):
                        residual(b - 1)
            probs_out(n - 1, NU - 1)
            normalise_out(n - 2)
            logits_out(n - 2)
            context(n - 1, 1)
            residual(n - 1)
            normalise_out(n - 1)
            logits_out(n - 1)
            dve.wait_ge(lgs, n)


def assign_slots(nc, ctx, K):
    n = K.n
    ne = n * E

    def sb(name, shape, dt=F32):
        return ctx.enter_context(nc.sbuf_tensor("b_" + name, shape, dt))

    def sem(name):
        return new_signal(nc, K, "b_" + name)

    rank = sb("rank", [P, E])
    start = sb("start", [P, E])
    spare = sb("spare", [P, n])
    tri = sb("tri", [P, P], BF16)
    onesb = sb("onesb", [P, P], BF16)
    top = sb("top", [P, n])
    ex = sb("ex", [P, n, E])
    den = sb("den", [P, n])
    pmax = sb("pmax", [P, n])
    eq = sb("eq", [P, n, E])
    hot = sb("hot", [P, n, E])
    hotb = sb("hotb", [P, ne], BF16)
    tot = sb("tot", [P, n, E])
    run = sb("run", [P, n, E])
    pos = sb("pos", [P, n, E])
    mine = sb("mine", [P, n])
    base = sb("base", [P, n])
    kept = sb("kept", [P, n])
    slotf = sb("slotf", [P, n])
    tmp = sb("tmp", [P, n])
    W = min(512, ne)
    nb = ne // W
    within = [ctx.enter_context(nc.psum_tensor(f"b_within{i}", [P, 512], F32)) for i in range(nb)]
    total = [ctx.enter_context(nc.psum_tensor(f"b_total{i}", [P, 512], F32)) for i in range(nb)]
    loaded, consts, shifted, exped, onehot, counted, chain = (sem(x) for x in (
        "loaded", "consts", "shifted", "exped", "onehot", "counted", "chain"))

    with nc.Block() as block:

        @block.sync
        def _(sp):
            sp.dma_start(rank[:, :], K.rank.partition_broadcast(P)).then_inc(loaded, 16)
            sp.dma_start(start[:, :], K.start.partition_broadcast(P)).then_inc(loaded, 16)
            sp.dma_start(spare[:, :], K.spare).then_inc(loaded, 16)

        @block.gpsimd
        def _(pool):
            pool.memset(tri[:, :], 1.0).then_inc(consts, 1)
            pool.memset(onesb[:, :], 1.0).then_inc(consts, 1)
            pool.wait_ge(consts, 1)
            pool.affine_select(out=tri[:, :], in_=tri[:, :], compare_op=ALU.is_ge, fill=0.0, base=0,
                               pattern=[[1, P]], channel_multiplier=-1).then_inc(consts, 1)

        @block.scalar
        def _(act):
            act.wait_ge(shifted, 1)
            act.activation(ex[:, :, :], ex[:, :, :], ACT.Exp).then_inc(exped, 1)

        @block.tensor
        def _(pe):
            pe.wait_ge(consts, 3)
            pe.wait_ge(onehot, 1)
            for i in range(nb):
                pe.matmul(within[i][:, 0:W], tri[:, :], hotb[:, i * W:(i + 1) * W], start=True, stop=True)
                mm = pe.matmul(total[i][:, 0:W], onesb[:, :], hotb[:, i * W:(i + 1) * W], start=True, stop=True)
            mm.then_inc(counted, 1)

        @block.vector
        def _(dve):
            done = [0]

            def link(ins):
                done[0] += 1
                ins.then_inc(chain, 1)
                dve.wait_ge(chain, done[0])

            def over_experts(a):
                return a.unsqueeze(2).broadcast_to([P, n, E])

            def over_rows(a):
                return a.unsqueeze(1).broadcast_to([P, n, E])

            lg = K.logits[:, :, :]
            link(dve.tensor_reduce(top[:, :], lg, AX.X, ALU.max))
            dve.tensor_tensor(ex[:, :, :], lg, over_experts(top[:, :]), ALU.subtract).then_inc(shifted, 1)
            link(dve.tensor_tensor(eq[:, :, :], lg, over_experts(top[:, :]), ALU.is_equal))
            dve.wait_ge(loaded, 48)
            link(dve.tensor_tensor(eq[:, :, :], eq[:, :, :], over_rows(rank[:, :]), ALU.mult))
            link(dve.tensor_reduce(mine[:, :], eq[:, :, :], AX.X, ALU.max))
            link(dve.tensor_tensor(hot[:, :, :], eq[:, :, :], over_experts(mine[:, :]), ALU.is_equal))
            dve.tensor_copy(hotb[:, :], hot[:, :, :].rearrange("p n e -> p (n e)")).then_inc(onehot, 1)
            dve.wait_ge(exped, 1)
            link(dve.tensor_reduce(den[:, :], ex[:, :, :], AX.X, ALU.add))
            link(dve.reciprocal(pmax[:, :], den[:, :]))
            dve.wait_ge(counted, 1)
            totf = tot[:, :, :].rearrange("p n e -> p (n e)")
            for i in range(nb):
                ins = dve.tensor_copy(totf[:, i * W:(i + 1) * W], total[i][:, 0:W])
            link(ins)
            for e in range(E):
                ins = dve.tensor_tensor_scan(run[:, :, e], K.ones[:, 0:n], tot[:, :, e], 0.0, ALU.mult, ALU.add)
            link(ins)
            link(dve.tensor_tensor(run[:, :, :], run[:, :, :], tot[:, :, :], ALU.subtract))
            posf = pos[:, :, :].rearrange("p n e -> p (n e)")
            runf = run[:, :, :].rearrange("p n e -> p (n e)")
            for i in range(nb):
                ins = dve.tensor_tensor(posf[:, i * W:(i + 1) * W], within[i][:, 0:W], runf[:, i * W:(i + 1) * W],
                                        ALU.add)
            link(ins)
            link(dve.tensor_tensor(pos[:, :, :], pos[:, :, :], hot[:, :, :], ALU.mult))
            link(dve.tensor_reduce(mine[:, :], pos[:, :, :], AX.X, ALU.add))
            link(dve.tensor_tensor(hot[:, :, :], hot[:, :, :], over_rows(start[:, :]), ALU.mult))
            link(dve.tensor_reduce(base[:, :], hot[:, :, :], AX.X, ALU.add))
            link(dve.tensor_scalar(kept[:, :], mine[:, :], float(K.cap), None, ALU.is_le))
            link(dve.tensor_tensor(slotf[:, :], base[:, :], mine[:, :], ALU.add))
            link(dve.tensor_scalar(tmp[:, :], slotf[:, :], float(E * K.cap - 1), None, ALU.min))
            link(dve.tensor_copy(K.read[:, :], tmp[:, :]))
            link(dve.tensor_tensor(slotf[:, :], slotf[:, :], spare[:, :], ALU.subtract))
            link(dve.tensor_tensor(slotf[:, :], slotf[:, :], kept[:, :], ALU.mult))
            link(dve.tensor_tensor(slotf[:, :], slotf[:, :], spare[:, :], ALU.add))
            link(dve.tensor_copy(K.slot[:, :], slotf[:, :]))
            g = K.gates[:, 2:3]
            link(dve.scalar_tensor_tensor(K.wexp[:, :], kept[:, :], g, pmax[:, :], ALU.mult, ALU.mult))
            link(dve.tensor_scalar(tmp[:, :], kept[:, :], -1.0, 1.0, ALU.mult, ALU.add))
            link(dve.tensor_scalar(tmp[:, :], tmp[:, :], g, None, ALU.mult))
            link(dve.tensor_tensor(K.wself[:, :], tmp[:, :], K.ln2[:, :, 1], ALU.mult))


def expert_weights(nc, ctx, K):
    def sb(name, shape, dt=F32):
        return ctx.enter_context(nc.sbuf_tensor("d_" + name, shape, dt))

    K.staging = sb("staging", [P, FC * D])
    K.w1 = sb("w1", [P, 2, 2, DC * FF], BF16)
    K.w2 = sb("w2", [P, 2, 2, FC * D], BF16)


def load_w1(eng, K, e, to, loaded):
    eng.dma_start(to[:, :].rearrange("p (c f) -> p c f", c=DC),
                  K.W1[bass.ds(e, 1)].rearrange("a (c p) f -> p (a c) f", p=P)).then_inc(loaded, 16)


def load_w2(eng, K, e, to, loaded):
    eng.dma_start(to[:, :].rearrange("p (c d) -> p c d", c=FC),
                  K.W2[bass.ds(e, 1)].rearrange("a (c p) d -> p (a c) d", p=P)).then_inc(loaded, 16)


def ternary_store(nc, ctx, K):
    def sb(name, shape, dt=F32):
        return ctx.enter_context(nc.sbuf_tensor("h_" + name, shape, dt))

    K.wf = sb("wf", [P, DC, FF], BF16)
    K.wp = sb("wp", [P, FC, D], BF16)
    K.lnw_col = sb("lnw", [P, FC])
    K.u1, K.gu2 = sb("u1", [P, D]), sb("gu2", [P, D])


def dispatch(nc, ctx, K):
    n = K.n

    def sb(name, shape, dt=F32):
        return ctx.enter_context(nc.sbuf_tensor("c_" + name, shape, dt))

    def sem(name):
        return new_signal(nc, K, "c_" + name)

    t = sb("t", [P, 4, D])
    at = sb("at", [P, 4], U32)
    shift = sb("shift", [P, n])
    low = sb("low", [P, FC * D], BF16)
    asum, thr, nthr = sb("asum", [P, 2]), sb("thr", [P, 2]), sb("nthr", [P, 2])
    lnb = sb("lnb", [P, FC])
    HF = FC // 2
    scaled = sb("scaled", [P, HF, D])
    raw = [K.staging, sb("raw", [P, DC * FF])]
    wf, wp, lnw = K.wf, K.wp, K.lnw_col
    banks = [ctx.enter_context(nc.psum_tensor(f"c_bank{i}", [P, 512], F32)) for i in range(8)]
    shifted, ready, named = sem("shift"), sem("ready"), sem("named")
    sent = [sem(f"sent{p}") for p in range(4)]
    loaded, chain, absd, summed, tern, turned, scales, u_mm, ends = (sem(x) for x in (
        "loaded", "chain", "abs_sums", "summed", "ternary", "turned", "scaled", "u_mm", "prepared"))
    wl, wc, wsplit = sem("expert_loaded"), sem("expert_high"), sem("expert_split")

    with nc.Block() as block:

        @block.scalar
        def _(act):
            act.wait_ge(shifted, 1)
            for b, p, h in quads(act, n):
                if not first(b, 4):
                    act.wait_ge(sent[p], 16 * h)
                act.activation(at[:, p:p + 1], K.slot[:, bass.ds(b, 1)], ACT.Copy).then_inc(named, 1)
                act.activation(t[:, p, :], K.xres[:, bass.ds(b * D, D)], ACT.Identity,
                               bias=shift[:, bass.ds(b, 1)],
                               scale=K.ln2[:, bass.ds(b, 1), 1:2].rearrange("p a c -> p (a c)")
                               ).then_inc(ready, 1)

        @block.gpsimd
        def _(pool):
            for b, p, h in quads(pool, n):
                pool.wait_ge(named, b + 1)
                pool.wait_ge(ready, b + 1)
                pool.sem_inc(K.passed, 1)
                pool.indirect_dma_start(
                    out=K.disp[:, :], out_offset=bass.IndirectOffsetOnAxis(ap=at[:, p:p + 1], axis=0),
                    in_=t[:, p, :], in_offset=None).then_inc(sent[p], 16)
            for p in range(4):
                pool.wait_ge(sent[p], 16 * (n // 4))

        @block.sync
        def _(sp):
            sp.dma_start(raw[0][:, :].rearrange("p (c d) -> p c d", c=FC),
                         K.Wfc.rearrange("(c p) d -> p c d", p=P)).then_inc(loaded, 16)
            sp.dma_start(raw[1][:, :].rearrange("p (c f) -> p c f", c=DC),
                         K.Wpr.rearrange("(c p) f -> p c f", p=P)).then_inc(loaded, 16)
            sp.dma_start(lnw[:, :], K.lnw.rearrange("(c p) -> p c", p=P), allow_slow_non_contiguous=True).then_inc(loaded, 16)
            sp.dma_start(lnb[:, :], K.lnb.rearrange("(c p) -> p c", p=P), allow_slow_non_contiguous=True).then_inc(loaded, 16)
            sp.wait_ge(turned, 1)
            load_w1(sp, K, 0, raw[0], wl)
            load_w2(sp, K, 0, raw[1], wl)

        @block.tensor
        def _(pe):
            pe.wait_ge(absd, 2)
            pe.matmul(banks[0][:, 0:2], K.ones[:, :], asum[:, :], start=True, stop=True).then_inc(summed, 1)
            pe.wait_ge(tern, 2)
            for dd in range(DC):
                for c in range(FC):
                    pe.transpose(banks[dd * 2 + c // 4][:, (c % 4) * P:(c % 4 + 1) * P],
                                 raw[0][:, c * D + dd * P:c * D + (dd + 1) * P], K.ident[:, :])
            for c in range(FC):
                for dd in range(DC):
                    at_ = (c % 2) * D + dd * P
                    mm = pe.transpose(banks[4 + c // 2][:, at_:at_ + P],
                                      raw[1][:, dd * FF + c * P:dd * FF + (c + 1) * P], K.ident[:, :])
            mm.then_inc(turned, 1)
            for i in range(4):
                pe.wait_ge(scales, i + 1)
                for c in range(HF):
                    mm = pe.matmul(banks[i // 2][:, 0:D], K.ones[:, :], scaled[:, c, :],
                                   start=i % 2 == 0 and c == 0, stop=i % 2 == 1 and c == HF - 1)
                mm.then_inc(u_mm, 1)

        @block.vector
        def _(dve):
            done = [0]

            def link(ins):
                done[0] += 1
                ins.then_inc(chain, 1)
                dve.wait_ge(chain, done[0])

            dve.scalar_tensor_tensor(shift[:, :], K.ln2[:, :, 0], -1.0, K.ln2[:, :, 1], ALU.mult, ALU.mult
                                     ).then_inc(shifted, 1)
            dve.wait_ge(loaded, 64)
            for k in range(2):
                dve.tensor_reduce(asum[:, k:k + 1], raw[k][:, :], AX.X, ALU.add,
                                  apply_absolute_value=True).then_inc(absd, 1)
            dve.wait_ge(summed, 1)
            link(dve.tensor_scalar(thr[:, :], banks[0][:, 0:2], 1.0 / (FF * D), 1e-6, ALU.mult, ALU.add))
            link(dve.tensor_scalar(thr[:, :], thr[:, :], 0.5, None, ALU.mult))
            link(dve.tensor_scalar(nthr[:, :], thr[:, :], -1.0, None, ALU.mult))
            for k in range(2):
                link(dve.tensor_scalar(low[:, :], raw[k][:, :], nthr[:, k:k + 1], None, ALU.is_lt))
                link(dve.scalar_tensor_tensor(raw[k][:, :], raw[k][:, :], thr[:, k:k + 1], low[:, :],
                                              ALU.is_gt, ALU.subtract))
            dve.sem_inc(tern, 2)
            dve.wait_ge(turned, 1)
            for dd in range(DC):
                for c in range(2):
                    dve.tensor_copy(wf[:, dd, c * 512:(c + 1) * 512], banks[dd * 2 + c][:, :])
            for c in range(4):
                dve.tensor_copy(wp[:, 2 * c:2 * c + 2, :].rearrange("p a d -> p (a d)"), banks[4 + c][:, :])
            for i in range(4):
                if i:
                    dve.wait_ge(u_mm, i)
                for j in range(HF):
                    c = (i % 2) * HF + j
                    ins = dve.tensor_scalar(scaled[:, j, :], banks[4 + c // 2][:, (c % 2) * D:(c % 2 + 1) * D],
                                            (lnw, lnb)[i // 2][:, c:c + 1], None, ALU.mult)
                ins.then_inc(scales, 1)
            dve.wait_ge(wl, 32)
            dve.tensor_copy(K.w1[:, 0, 0, :], raw[0][:, :]).then_inc(wc, 1)
            dve.tensor_copy(K.w2[:, 0, 0, :], raw[1][:, :]).then_inc(wc, 1)
            dve.wait_ge(wc, 2)
            dve.tensor_tensor(K.w1[:, 0, 1, :], raw[0][:, :], K.w1[:, 0, 0, :], ALU.subtract).then_inc(wsplit, 1)
            dve.tensor_tensor(K.w2[:, 0, 1, :], raw[1][:, :], K.w2[:, 0, 0, :], ALU.subtract).then_inc(wsplit, 1)
            dve.wait_ge(u_mm, 4)
            dve.tensor_copy(K.u1[:, :], banks[0][:, 0:D]).then_inc(ends, 1)
            dve.tensor_scalar(K.gu2[:, :], banks[1][:, 0:D], K.gates[:, 3:4], None, ALU.mult).then_inc(ends, 1)
            dve.wait_ge(ends, 2)
            dve.wait_ge(wsplit, 2)


def experts(nc, ctx, K):
    G = K.group
    SC = G // P
    ng = K.cap // G
    RING = 4

    def sb(name, shape, dt=F32):
        return ctx.enter_context(nc.sbuf_tensor("d_" + name, shape, dt))

    def psum(name):
        return ctx.enter_context(nc.psum_tensor("d_" + name, [P, 512], F32))

    def sem(name):
        return new_signal(nc, K, "d_" + name)

    staging, w1, w2 = K.staging, K.w1, K.w2
    rows = sb("rows", [P, SC, D])
    tT = sb("tT", [P, 2, DC, G], BF16)
    hT = sb("hT", [P, RING, 2, G], BF16)
    ys = sb("ys", [P, SC, D])
    tb = [psum(f"tb{c}") for c in range(DC)]
    hb = [psum(f"hb{i}") for i in range(2)]
    yb = [psum(f"yb{s}") for s in range(SC)]
    wl, wc, wsplit = sem("w_loaded"), sem("w_high"), sem("w_split")
    rl, tmm, th, tl = sem("rows_loaded"), sem("t_mm"), sem("t_high"), sem("t_low")
    hmm, hh, hl, used, ysd, ysa, stored = (sem(x) for x in (
        "h_mm", "h_high", "h_low", "h_used", "y_dve", "y_act", "stored"))

    def groups(eng):
        with eng.Fori(0, E // 2) as j:
            for ep in range(2):
                with eng.Fori(0, ng) as k:
                    yield (2 * j + ep) * ng + k, ep, 2 * j + ep

    with nc.Block() as block:

        @block.sync
        def _(sp):
            sp.dma_start(rows[:, :, :], K.disp[0:G, :].rearrange("(p s) d -> p s d", s=SC)).then_inc(rl, 16)
            with sp.Fori(1, E * ng) as q:
                sp.wait_ge(tmm, q)
                sp.dma_start(rows[:, :, :], K.disp[bass.ds(q * G, G), :].rearrange("(p s) d -> p s d", s=SC)
                             ).then_inc(rl, 16)
            sp.wait_ge(tmm, E * ng)
            sp.dma_start(rows[:, :, :], K.disp[0:G, :].rearrange("(p s) d -> p s d", s=SC)).then_inc(rl, 16)

        @block.gpsimd
        def _(pool):
            def split(e, ep, free):
                for i, (load, w) in enumerate(((load_w1, w1), (load_w2, w2))):
                    pool.sem_inc(K.passed, 1)
                    load(pool, K, e, staging, wl)
                    if free and i == 0:
                        pool.wait_ge(used, RING + (e - 1) * ng * FC)
                    pool.wait_ge(wl, 32 * e - 16 + 16 * i)
                    pool.sem_inc(K.passed, 1)
                    pool.tensor_copy(w[:, ep, 0, :], staging[:, :]).then_inc(wc, 1)
                    pool.wait_ge(wc, 2 * e - 1 + i)
                    pool.tensor_tensor(w[:, ep, 1, :], staging[:, :], w[:, ep, 0, :], ALU.subtract
                                       ).then_inc(wsplit, 1)
                    pool.wait_ge(wsplit, 2 * e + 1 + i)

            pool.sem_inc(wsplit, 2)
            split(1, 1, False)
            with pool.Fori(1, E // 2) as j:
                for ep in range(2):
                    split(2 * j + ep, ep, True)

        @block.tensor
        def _(pe):
            def turn():
                for c in range(DC):
                    for s in range(SC):
                        mm = pe.transpose(tb[c][:, s * P:(s + 1) * P], rows[:, s, c * P:(c + 1) * P],
                                          K.ident[:, :])
                mm.then_inc(tmm, 1)

            def hidden(q, ep, f):
                pe.wait_ge(hl, q * FC + f + 1)
                bank = hb[f % 2]
                k = 0
                for wp, tp in ((0, 0), (0, 1), (1, 0)):
                    for c in range(DC):
                        mm = pe.matmul(bank[:, 0:G], w1[:, ep, wp, c * FF + f * P:c * FF + (f + 1) * P],
                                       tT[:, tp, c, :], start=k == 0, stop=k == 5)
                        k += 1
                mm.then_inc(hmm, 1)

            def back(q, ep, f):
                pe.wait_ge(hl, q * FC + f + 3)
                if f == 0:
                    pe.wait_ge(ysa, q + 1)
                    pe.wait_ge(ysd, q + 1)
                for s in range(SC):
                    for hp, wp in ((0, 0), (0, 1), (1, 0)):
                        mm = pe.matmul(yb[s][:, 0:D], hT[:, f % RING, hp, s * P:(s + 1) * P],
                                       w2[:, ep, wp, f * D:(f + 1) * D],
                                       start=f == 0 and hp == 0 and wp == 0, stop=f == FC - 1 and hp == 1)
                mm.then_inc(used, 1)

            pe.sem_inc(used, RING)
            pe.wait_ge(rl, 16)
            turn()
            for q, ep, e in groups(pe):
                pe.wait_ge(wsplit, 2 * e + 2)
                pe.wait_ge(th, q + 1)
                pe.wait_ge(tl, q + 1)
                for f in range(FC + 2):
                    if f < FC:
                        hidden(q, ep, f)
                    if f >= 2:
                        back(q, ep, f - 2)
                    if f == FC // 2:
                        pe.wait_ge(rl, 16 * q + 32)
                        turn()

        @block.scalar
        def _(act):
            act.sem_inc(ysa, 1)
            act.sem_inc(stored, 16)

            def high():
                for c in range(DC):
                    cp = act.activation(tT[:, 0, c, :], tb[c][:, 0:G], ACT.Copy)
                cp.then_inc(th, 1)

            act.wait_ge(tmm, 1)
            high()
            for q, ep, e in groups(act):
                for f in range(FC):
                    act.wait_ge(hmm, q * FC + f + 1)
                    act.wait_ge(used, q * FC + f + 1)
                    act.activation(hT[:, f % RING, 0, :], hb[f % 2][:, 0:G], ACT.Relu).then_inc(hh, 1)
                act.wait_ge(tmm, q + 2)
                act.wait_ge(hmm, (q + 1) * FC)
                high()
                act.wait_ge(used, RING + (q + 1) * FC)
                act.wait_ge(stored, 16 * q + 16)
                for s in range(0, SC, 2):
                    cp = act.activation(ys[:, s, :], yb[s][:, 0:D], ACT.Copy)
                cp.then_inc(ysa, 1)
                act.wait_ge(ysa, q + 2)
                act.wait_ge(ysd, q + 2)
                act.dma_start(K.eout[bass.ds(q * G, G), :].rearrange("(p s) d -> p s d", s=SC), ys[:, :, :]
                              ).then_inc(stored, 16)
            act.wait_ge(stored, 16 * (E * ng + 1))

        @block.vector
        def _(dve):
            dve.sem_inc(hl, 2)
            dve.sem_inc(ysd, 1)

            def low():
                for c in range(DC):
                    cp = dve.tensor_tensor(tT[:, 1, c, :], tb[c][:, 0:G], tT[:, 0, c, :], ALU.subtract)
                cp.then_inc(tl, 1)

            dve.wait_ge(th, 1)
            low()
            for q, ep, e in groups(dve):
                for f in range(FC):
                    dve.wait_ge(hh, q * FC + f + 1)
                    dve.scalar_tensor_tensor(hT[:, f % RING, 1, :], hb[f % 2][:, 0:G], 0.0, hT[:, f % RING, 0, :],
                                             ALU.max, ALU.subtract).then_inc(hl, 1)
                dve.wait_ge(th, q + 2)
                low()
                dve.wait_ge(used, RING + (q + 1) * FC)
                dve.wait_ge(stored, 16 * q + 16)
                for s in range(1, SC, 2):
                    cp = dve.tensor_copy(ys[:, s, :], yb[s][:, 0:D])
                cp.then_inc(ysd, 1)


def combine_and_correlate(nc, ctx, K):
    n = K.n
    DX = D + 1

    def sb(name, shape, dt=F32):
        return ctx.enter_context(nc.sbuf_tensor("e_" + name, shape, dt))

    def psum(name):
        return ctx.enter_context(nc.psum_tensor("e_" + name, [P, 512], F32))

    def sem(name):
        return new_signal(nc, K, "e_" + name)

    dft = sb("dft", [P, P])
    gm = sb("gm", [P, DC, DX])
    brow = sb("brow", [3, DX], BF16)
    dc = sb("dc", [3, P], BF16)
    banks = [psum(f"bank{i}") for i in range(8)]
    w_loaded, w_turned, w_ready, g_mm = sem("w_loaded"), sem("w_turned"), sem("w_ready"), sem("g_mm")

    with ExitStack() as prep, nc.Block() as block:
        raw = prep.enter_context(nc.sbuf_tensor("e_raw", [P, 2, DC, D], F32))
        wT = prep.enter_context(nc.sbuf_tensor("e_wT", [P, 2, DC, D], F32))
        bq = prep.enter_context(nc.sbuf_tensor("e_bq", [P, DC], F32))
        bk = prep.enter_context(nc.sbuf_tensor("e_bk", [P, DC], F32))
        rest = prep.enter_context(nc.sbuf_tensor("e_rest", [1, 3, DX], F32))
        part = prep.enter_context(nc.sbuf_tensor("e_part", [1, 3, DX], BF16))
        parts, placed = sem("parts"), sem("parts_placed")

        @block.sync
        def _(sp):
            for i, w in enumerate((K.Wq1, K.Wk1)):
                sp.dma_start(raw[:, i], w.rearrange("(c p) d -> p c d", p=P)).then_inc(w_loaded, 16)
            sp.dma_start(bq[:, :], K.bq1.rearrange("(c p) -> p c", p=P), allow_slow_non_contiguous=True).then_inc(w_loaded, 16)
            sp.dma_start(bk[:, :], K.bk1.rearrange("(c p) -> p c", p=P), allow_slow_non_contiguous=True).then_inc(w_loaded, 16)
            sp.dma_start(dft[:, :], K.dft).then_inc(w_loaded, 16)
            sp.wait_ge(parts, 6)
            for i in range(3):
                sp.dma_start(brow[i:i + 1, :], part[:, i, :]).then_inc(placed, 16)
            sp.wait_ge(placed, 48)

        @block.tensor
        def _(pe):
            pe.wait_ge(w_loaded, 16 * 5)
            for i in range(2):
                mm = transpose_square(pe, banks[i], raw[:, i], K.ident)
            mm.then_inc(w_turned, 1)
            pe.wait_ge(w_ready, 2)
            for m in range(DC):
                for c in range(DC):
                    pe.matmul(banks[2 + m][:, 0:D], wT[:, 0, c, m * P:(m + 1) * P], wT[:, 1, c, :],
                              start=c == 0, stop=c == DC - 1)
            for m in range(DC):
                for c in range(DC):
                    pe.matmul(banks[4 + m][:, 0:1], wT[:, 0, c, m * P:(m + 1) * P], bk[:, c:c + 1],
                              start=c == 0, stop=c == DC - 1)
            for c in range(DC):
                pe.matmul(banks[6][0:1, 0:D], bq[:, c:c + 1], wT[:, 1, c, :], start=c == 0, stop=c == DC - 1)
            for c in range(DC):
                mm = pe.matmul(banks[7][0:1, 0:1], bq[:, c:c + 1], bk[:, c:c + 1], start=c == 0,
                               stop=c == DC - 1)
            mm.then_inc(g_mm, 1)

        @block.vector
        def _(dve):
            dve.memset(dc[:, :], 0.0).then_inc(w_ready, 1)
            dve.wait_ge(w_turned, 1)
            for i in range(2):
                ins = dve.tensor_copy(wT[:, i].rearrange("p c d -> p (c d)"), banks[i][:, :])
            ins.then_inc(w_ready, 1)
            dve.wait_ge(g_mm, 1)
            for m in range(DC):
                dve.tensor_copy(gm[:, m, 0:D], banks[2 + m][:, 0:D])
                dve.tensor_copy(gm[:, m, D:DX], banks[4 + m][:, 0:1])
            dve.tensor_scalar(rest[:, 0, 0:D], banks[6][0:1, 0:D], float(P), None, ALU.mult)
            dve.tensor_scalar(rest[:, 0, D:DX], banks[7][0:1, 0:1], float(P), None, ALU.mult).then_inc(parts, 1)
            for i in range(3):
                dve.wait_ge(parts, 2 * i + 1)
                dve.tensor_copy(part[:, i, :], rest[:, i, :]).then_inc(parts, 1)
                if i < 2:
                    dve.wait_ge(parts, 2 * i + 2)
                    dve.tensor_tensor(rest[:, i + 1, :], rest[:, i, :], part[:, i, :], ALU.subtract
                                      ).then_inc(parts, 1)
            dve.wait_ge(w_ready, 1)
            dve.memset(dc[:, 0:1], 1.0).then_inc(w_ready, 1)
            dve.wait_ge(w_ready, 3)

    AHEAD = 4
    at = sb("at", [P, AHEAD], U32)
    eo = sb("eo", [P, AHEAD, D])
    cin = sb("cin", [P, 2, D])
    u = sb("u", [P, 2, D])
    grow = sb("grow", [P, n])
    shift = sb("shift", [P, n])
    xh = sb("xh", [P, 2, D])
    xfT = sb("xfT", [P, DC * P])
    cf = sb("cf", [P, 2, DX])
    prod = sb("prod", [P, DX])
    pc = sb("pc", [P, 1])
    st, mv, ve, rs = sb("st", [P, 6]), sb("mv", [P, 2, 2]), sb("ve", [P, 1]), sb("rs", [P, 2])
    xb, cb, gb = banks[0:2], banks[2:4], banks[4:6]
    ctl = [sem("ctx0"), sem("ctx1")]
    got = [sem(f"got{r}") for r in range(AHEAD)]
    ats, factors, us, xs, bn, mvs, ves, rss, xhs = (sem(x) for x in (
        "at", "factors", "u", "x", "bn", "mv", "ve", "rs", "xhat"))
    xfmm, cfmm, xfs, cfs, gmm, prods, ps, preset = (sem(x) for x in (
        "xf_mm", "cf_mm", "xf", "cf", "g_prod", "prod", "p", "preset"))

    with nc.Block() as block:

        @block.sync
        def _(sp):
            for b, p, h in steps(sp, n):
                if not first(b, 2):
                    sp.wait_ge(cfmm, b - 1)
                sp.dma_start(cin[:, p, :], K.ctx[bass.ds(b, 1)].rearrange("a p d -> p (a d)")
                             ).then_inc(ctl[p], 16)

        @block.gpsimd
        def _(pool):
            def gather(b, r):
                pool.wait_ge(ats, b + 1)
                if not first(b, AHEAD):
                    pool.wait_ge(us, b - AHEAD + 1)
                pool.sem_inc(K.passed, 1)
                pool.indirect_dma_start(
                    out=eo[:, r, :], out_offset=None, in_=K.eout[:, :],
                    in_offset=bass.IndirectOffsetOnAxis(ap=at[:, r:r + 1], axis=0)).then_inc(got[r], 16)

            def deviation(b, p):
                if not first(b, 1):
                    pool.wait_ge(rss, b)
                pool.wait_ge(mvs, b + 1)
                pool.sem_inc(K.passed, 1)
                pool.tensor_scalar(ve[:, :], mv[:, p, 1:2], LN_EPS, 1.0, ALU.add, ALU.mult).then_inc(ves, 1)
                pool.wait_ge(ves, b + 1)
                if not first(b, 2):
                    pool.wait_ge(xhs, b - 1)
                pool.tensor_tensor(rs[:, p:p + 1], ve[:, :], K.half[:, :], ALU.pow).then_inc(rss, 1)

            for r in range(AHEAD):
                gather(r, r)
            deviation(0, 0)
            for b, r, h in quads(pool, n):
                if not last(b, n, 1):
                    deviation(b + 1, (r + 1) % 2)
                if not last(b, n, AHEAD):
                    gather(b + AHEAD, r)

        @block.tensor
        def _(pe):
            def spectra(b, p, h):
                pe.wait_ge(ctl[p], 16 * h + 16)
                if not first(b, 2):
                    pe.wait_ge(cfs, b - 1)
                pe.matmul(cb[p][:, 0:D], dft[:, :], cin[:, p, :], start=True, stop=True).then_inc(cfmm, 1)
                if not first(b, 1):
                    product(b - 1, 1 - p)
                pe.wait_ge(xhs, b + 1)
                if not first(b, 2):
                    pe.wait_ge(xfs, b - 1)
                for c in range(DC):
                    mm = pe.matmul(xb[p][:, c * P:(c + 1) * P], xh[:, p, c * P:(c + 1) * P], dft[:, :],
                                   start=True, stop=True)
                mm.then_inc(xfmm, 1)

            def product(b, p):
                pe.wait_ge(xfs, b + 1)
                if not first(b, 2):
                    pe.wait_ge(prods, b - 1)
                for c in range(DC):
                    pe.matmul(gb[p][:, 0:DX], xfT[:, c * P:(c + 1) * P], gm[:, c, :], start=c == 0, stop=False)
                pe.matmul(gb[p][:, 0:DX], dc[:, :], brow[:, :], start=False, stop=True).then_inc(gmm, 1)

            for b, p, h in steps(pe, n):
                spectra(b, p, h)
            product(n - 1, 1)

        @block.scalar
        def _(act):
            def weigh(b, r, h):
                act.wait_ge(got[r], 16 * h + 16)
                if not first(b, 2):
                    act.wait_ge(xs, b - 1)
                act.activation(u[:, r % 2, :], eo[:, r, :], ACT.Identity, bias=shift[:, bass.ds(b, 1)],
                               scale=K.wexp[:, bass.ds(b, 1)]).then_inc(us, 1)

            act.wait_ge(factors, 2)
            act.wait_ge(preset, 2)
            weigh(0, 0, 0)
            weigh(1, 1, 0)
            for b, r, h in quads(act, n):
                p = r % 2
                if not last(b, n, 2):
                    weigh(b + 2, (r + 2) % AHEAD, h + (r + 2) // AHEAD)
                act.wait_ge(cfmm, b + 1)
                if not first(b, 2):
                    act.wait_ge(prods, b - 1)
                act.activation(cf[:, p, 0:D], cb[p][:, 0:D], ACT.Copy).then_inc(cfs, 1)
                act.wait_ge(xfmm, b + 1)
                if not first(b, 1):
                    act.wait_ge(gmm, b)
                act.activation(xfT[:, :], xb[p][:, 0:D], ACT.Copy).then_inc(xfs, 1)

        @block.vector
        def _(dve):
            def row_of(b):
                return K.xres[:, bass.ds(b * D, D)]

            def name_row(b, r):
                dve.tensor_copy(at[:, r:r + 1], K.read[:, bass.ds(b, 1)]).then_inc(ats, 1)

            def update(b, p):
                dve.wait_ge(us, b + 1)
                dve.scalar_tensor_tensor(row_of(b), row_of(b), grow[:, bass.ds(b, 1)], u[:, p, :], ALU.mult, ALU.add
                                         ).then_inc(xs, 1)

            def stats(b):
                dve.wait_ge(xs, b + 1)
                if not first(b, 1):
                    dve.wait_ge(mvs, b)
                dve.sem_inc(K.passed, 1)
                dve.bn_stats(st[:, :], row_of(b)).then_inc(bn, 1)

            def aggregate(b, p):
                dve.wait_ge(bn, b + 1)
                if not first(b, 2):
                    dve.wait_ge(ves, b - 1)
                    dve.wait_ge(xhs, b - 1)
                dve.sem_inc(K.passed, 1)
                dve.bn_aggr(mv[:, p, :], st[:, :]).then_inc(mvs, 1)

            def normalise(b, p):
                dve.wait_ge(rss, b + 1)
                if not first(b, 2):
                    dve.wait_ge(xfmm, b - 1)
                dve.tensor_scalar(xh[:, p, :], row_of(b), mv[:, p, 0:1], rs[:, p:p + 1],
                                  ALU.subtract, ALU.mult).then_inc(xhs, 1)

            def reduce(b, p):
                dve.wait_ge(gmm, b + 1)
                dve.wait_ge(cfs, b + 1)
                if not first(b, 1):
                    dve.wait_ge(ps, b)
                dve.tensor_tensor_reduce(prod[:, :], gb[p][:, 0:DX], cf[:, p, :], 1.0, 0.0, ALU.mult, ALU.add,
                                         pc[:, :]).then_inc(prods, 1)

            def keep_sum(b):
                dve.wait_ge(prods, b + 1)
                dve.tensor_copy(K.spec[:, bass.ds(b, 1)], pc[:, :]).then_inc(ps, 1)

            dve.memset(cf[:, :, D:DX], 0.0).then_inc(preset, 1)
            dve.wait_ge(preset, 1)
            dve.memset(cf[0:1, :, D:DX], float(P)).then_inc(preset, 1)
            dve.wait_ge(preset, 2)
            dve.tensor_scalar(grow[:, :], K.wself[:, :], 1.0, None, ALU.add).then_inc(factors, 1)
            dve.scalar_tensor_tensor(shift[:, :], K.ln2[:, :, 0], -1.0, K.wself[:, :], ALU.mult, ALU.mult
                                     ).then_inc(factors, 1)
            for r in range(AHEAD):
                name_row(r, r)
            dve.wait_ge(factors, 2)
            update(0, 0)
            stats(0)
            aggregate(0, 0)
            for b, r, h in quads(dve, n):
                p = r % 2
                if not last(b, n, AHEAD):
                    name_row(b + AHEAD, r)
                if not last(b, n, 1):
                    update(b + 1, 1 - p)
                if not first(b, 2):
                    reduce(b - 2, p)
                normalise(b, p)
                if not last(b, n, 1):
                    stats(b + 1)
                if not first(b, 2):
                    keep_sum(b - 2)
                if not last(b, n, 1):
                    aggregate(b + 1, 1 - p)
            for b in (n - 2, n - 1):
                reduce(b, b % 2)
                keep_sum(b)
            dve.wait_ge(ps, n)


def pick_delays(nc, ctx, K):
    n = K.n

    def sb(name, shape, dt=F32):
        return ctx.enter_context(nc.sbuf_tensor("f_" + name, shape, dt))

    def sem(name):
        return new_signal(nc, K, "f_" + name)

    idft = sb("idft", [P, P])
    mean = sb("mean", [n, P])
    rest, rest2 = sb("rest", [n, P]), sb("rest2", [n, P])
    top8, next8, ninth = sb("top8", [n, 8]), sb("next8", [n, 8]), sb("ninth", [n, 8])
    ex, kept, den, w, twice = sb("ex", [n, P]), sb("kept", [n, P]), sb("den", [n, 1]), sb("w", [n, P]), sb("twice", [n, 2, P])
    neg = sb("neg", [n, 1])
    bank = ctx.enter_context(nc.psum_tensor("f_bank", [P, 512], F32))
    loaded, mmd, negs, exped, chain, twices, stored = (sem(x) for x in (
        "loaded", "mean_mm", "neg", "exped", "chain", "twice", "stored"))

    with nc.Block() as block:

        @block.sync
        def _(sp):
            sp.dma_start(idft[:, :], K.idft).then_inc(loaded, 16)
            sp.wait_ge(twices, 1)
            sp.dma_start(K.circ, twice[:, :, :].rearrange("n a k -> n (a k)")).then_inc(stored, 16)
            sp.wait_ge(stored, 16)

        @block.tensor
        def _(pe):
            pe.wait_ge(loaded, 16)
            pe.matmul(bank[0:n, 0:P], K.spec[:, 0:n], idft[:, :], start=True, stop=True).then_inc(mmd, 1)

        @block.scalar
        def _(act):
            act.wait_ge(negs, 1)
            act.activation(ex[:, :], mean[:, :], ACT.Exp, bias=neg[:, 0:1]).then_inc(exped, 1)

        @block.vector
        def _(dve):
            done = [0]

            def link(ins):
                done[0] += 1
                ins.then_inc(chain, 1)
                dve.wait_ge(chain, done[0])

            dve.wait_ge(mmd, 1)
            link(dve.tensor_copy(mean[:, :], bank[0:n, 0:P]))
            link(dve.max(top8[:, :], mean[:, :]))
            dve.tensor_scalar(neg[:, :], top8[:, 0:1], -1.0, None, ALU.mult).then_inc(negs, 1)
            link(dve.match_replace(rest[:, :], top8[:, :], mean[:, :], LOWEST))
            link(dve.max(next8[:, :], rest[:, :]))
            link(dve.memset(ninth[:, :], LOWEST))
            link(dve.tensor_copy(ninth[:, 0:1], next8[:, 0:1]))
            link(dve.match_replace(rest2[:, :], ninth[:, :], rest[:, :], LOWEST))
            link(dve.tensor_scalar(kept[:, :], rest2[:, :], 0.5 * LOWEST, None, ALU.is_le))
            dve.wait_ge(exped, 1)
            link(dve.tensor_tensor(ex[:, :], ex[:, :], kept[:, :], ALU.mult))
            link(dve.tensor_reduce(den[:, :], ex[:, :], AX.X, ALU.add))
            link(dve.reciprocal(den[:, :], den[:, :]))
            link(dve.tensor_scalar(w[:, :], ex[:, :], den[:, 0:1], None, ALU.mult))
            for a in range(2):
                ins = dve.tensor_copy(twice[:, a, :], w[:, :])
            ins.then_inc(twices, 1)


def delayed_values(nc, ctx, K):
    n = K.n
    g = K.gates[:, 1:2]

    def sb(name, shape, dt=F32):
        return ctx.enter_context(nc.sbuf_tensor("g_" + name, shape, dt))

    def sem(name):
        return new_signal(nc, K, "g_" + name)

    wvo = sb("wvo", [P, DC, D])
    gbias = sb("gbias", [P, D])
    banks = [ctx.enter_context(nc.psum_tensor(f"g_bank{i}", [P, 512], F32)) for i in range(4)]
    w_loaded, w_turned, w_ready, o_mm = sem("w_loaded"), sem("w_turned"), sem("w_ready"), sem("o_mm")

    with ExitStack() as prep, nc.Block() as block:
        raw = prep.enter_context(nc.sbuf_tensor("g_raw", [P, DC, D], F32))
        wvT = prep.enter_context(nc.sbuf_tensor("g_wvT", [P, DC, D], F32))
        wo = prep.enter_context(nc.sbuf_tensor("g_wo", [P, DC, D], F32))
        bv = prep.enter_context(nc.sbuf_tensor("g_bv", [P, DC], F32))
        bvb = prep.enter_context(nc.sbuf_tensor("g_bvb", [P, DC, P], F32))
        bob = prep.enter_context(nc.sbuf_tensor("g_bob", [P, D], F32))

        @block.sync
        def _(sp):
            sp.dma_start(raw[:, :, :], K.Wv1.rearrange("(c p) d -> p c d", p=P)).then_inc(w_loaded, 16)
            sp.dma_start(wo[:, :, :], K.Wo1.rearrange("(c p) d -> p c d", p=P)).then_inc(w_loaded, 16)
            sp.dma_start(bv[:, :], K.bv1.rearrange("(c p) -> p c", p=P), allow_slow_non_contiguous=True).then_inc(w_loaded, 16)
            sp.dma_start(bob[:, :], K.bo1.partition_broadcast(P)).then_inc(w_loaded, 16)

        @block.tensor
        def _(pe):
            pe.wait_ge(w_loaded, 64)
            transpose_square(pe, banks[0], raw, K.ident).then_inc(w_turned, 1)
            pe.wait_ge(w_ready, 2)
            for m in range(DC):
                for c in range(DC):
                    pe.matmul(banks[1 + m][:, 0:D], wvT[:, c, m * P:(m + 1) * P], wo[:, c, :],
                              start=c == 0, stop=c == DC - 1)
            for c in range(DC):
                mm = pe.matmul(banks[3][:, 0:D], bvb[:, c, :], wo[:, c, :], start=c == 0, stop=c == DC - 1)
            mm.then_inc(o_mm, 1)

        @block.vector
        def _(dve):
            dve.wait_ge(w_loaded, 64)
            for c in range(DC):
                ins = dve.tensor_scalar(bvb[:, c, :], K.ones[:, :], bv[:, c:c + 1], None, ALU.mult)
            ins.then_inc(w_ready, 1)
            dve.wait_ge(w_turned, 1)
            dve.tensor_copy(wvT[:, :, :].rearrange("p c d -> p (c d)"), banks[0][:, :]).then_inc(w_ready, 1)
            dve.wait_ge(o_mm, 1)
            for m in range(DC):
                dve.tensor_copy(wvo[:, m, :], banks[1 + m][:, 0:D])
            dve.tensor_tensor(gbias[:, :], banks[3][:, 0:D], bob[:, :], ALU.add).then_inc(w_ready, 1)
            dve.wait_ge(w_ready, 3)
            dve.tensor_scalar(gbias[:, :], gbias[:, :], g, None, ALU.mult).then_inc(w_ready, 1)
            dve.wait_ge(w_ready, 4)

    cin = sb("cin", [P, 4, D])
    ci = sb("ci", [P, 4, P])
    aT = sb("aT", [P, 2, D])
    abank, ybank = banks[0:2], banks[2:4]
    ld = [sem(f"ld{r}") for r in range(4)]
    amm, aTs, ymm, pre, xs = (sem(x) for x in ("a_mm", "aT", "y_mm", "preadded", "x"))
    circ = K.circ

    with nc.Block() as block:

        @block.sync
        def _(sp):
            for b, r, h in quads(sp, n):
                if not first(b, 4):
                    sp.wait_ge(amm, b - 3)
                sp.dma_start(cin[:, r, :], K.ctx[bass.ds(b, 1)].rearrange("a p d -> p (a d)")
                             ).then_inc(ld[r], 16)
                sp.dma_start(ci[:, r, :], bass.AP(tensor=circ.tensor, offset=b * 2 * P + 1, ap=[[1, P], [1, P]])
                             ).then_inc(ld[r], 16)

        @block.gpsimd
        def _(pool):
            for b, p, h in steps(pool, n):
                row = K.xres[:, bass.ds(b * D, D)]
                pool.tensor_tensor(row, row, gbias[:, :], ALU.add).then_inc(pre, 1)

        @block.tensor
        def _(pe):
            def out(b, p):
                pe.wait_ge(aTs, b + 1)
                if not first(b, 2):
                    pe.wait_ge(xs, b - 1)
                for c in range(DC):
                    mm = pe.matmul(ybank[p][:, 0:D], aT[:, p, c * P:(c + 1) * P], wvo[:, c, :],
                                   start=c == 0, stop=c == DC - 1)
                mm.then_inc(ymm, 1)

            for b, r, h in quads(pe, n):
                p = r % 2
                pe.wait_ge(ld[r], 32 * h + 32)
                if not first(b, 2):
                    pe.wait_ge(aTs, b - 1)
                for c in range(DC):
                    mm = pe.matmul(abank[p][:, c * P:(c + 1) * P], cin[:, r, c * P:(c + 1) * P], ci[:, r, :],
                                   start=True, stop=True)
                mm.then_inc(amm, 1)
                if not first(b, 1):
                    out(b - 1, 1 - p)
            out(n - 1, 1)

        @block.scalar
        def _(act):
            for b, p, h in steps(act, n):
                act.wait_ge(amm, b + 1)
                if not first(b, 2):
                    act.wait_ge(ymm, b - 1)
                for c in range(DC):
                    last = c * P - 1 if c else None
                    cp = act.activation(aT[:, p, c * P:(c + 1) * P], abank[p][:, (c + 1) * P - 1:last:-1], ACT.Copy)
                cp.then_inc(aTs, 1)

        @block.vector
        def _(dve):
            for b, p, h in steps(dve, n):
                dve.wait_ge(ymm, b + 1)
                dve.wait_ge(pre, b + 1)
                row = K.xres[:, bass.ds(b * D, D)]
                dve.scalar_tensor_tensor(row, ybank[p][:, 0:D], g, row, ALU.mult, ALU.add).then_inc(xs, 1)
            dve.wait_ge(xs, n)


def ternary_ffn(nc, ctx, K):
    n = K.n
    SC = 4
    G = SC * P
    nq = n // SC
    RH, RG = 4, 4
    LAG = 3
    g = K.gates[:, 3:4]

    def sb(name, shape, dt=F32):
        return ctx.enter_context(nc.sbuf_tensor("h_" + name, shape, dt))

    def sem(name):
        return new_signal(nc, K, "h_" + name)

    wf, wp, lnw, u1, gu2 = K.wf, K.wp, K.lnw_col, K.u1, K.gu2
    banks = [ctx.enter_context(nc.psum_tensor(f"h_bank{i}", [P, 512], F32)) for i in range(8)]
    st, mv = sb("st", [P, SC, 6]), sb("mv", [P, SC, 2])
    ve, rs = sb("ve", [P, SC]), sb("rs", [P, SC])
    xh = sb("xh", [P, SC, D])
    xT = sb("xT", [P, 2, 2, DC, G], BF16)
    hf = sb("hf", [P, RG, G])
    hq = sb("hq", [P, RG, G])
    hT = sb("hT", [P, RH, 2, G], BF16)
    s12 = sb("s12", [P, 2, 2, G])
    ysb = sb("ysb", [P, SC, D])
    m12, msq, var, ve2, rs2 = sb("m12", [P, 2 * SC]), sb("msq", [P, SC]), sb("var", [P, SC]), sb("ve2", [P, SC]), sb("rs2", [P, SC])
    ca, cb = sb("ca", [P, SC]), sb("cb", [P, SC])
    osb = sb("osb", [P, SC, D])
    tb, hb, yb = banks[0:2], banks[2:4], banks[4:8]
    (bns, mvs, ves, rss, xhs, tmm, th, tl, hmm, hfs, hqs, hh, hl, used, summed1, summed2, sum_mm, m12s, msqs, vars_, ve2s, rs2s,
     cas, cbs, ys, o1, o2, o3, stored) = (sem(x) for x in (
        "bn", "mv", "ve", "rs", "xhat", "t_mm", "t_high", "t_low", "h_mm", "h", "h_square", "h_high", "h_low",
        "h_used", "h_summed", "h_square_summed", "sum_mm", "means", "mean_square", "variance", "ve2", "rs2", "ca", "cb", "y",
        "out1", "out2", "out3", "stored"))
    outv = K.out.rearrange("(q s) p d -> q p s d", s=SC)

    def y_of(p, s):
        return yb[2 * p + s // 2][:, (s % 2) * D:(s % 2 + 1) * D]

    with nc.Block() as block:

        @block.tensor
        def _(pe):
            def turn(q):
                pe.wait_ge(xhs, q + 1)
                if not first(q, 1):
                    pe.wait_ge(th, q)
                    pe.wait_ge(tl, q)
                if not first(q, 2):
                    pe.wait_ge(m12s, q - 1)
                for c in range(DC):
                    for s in range(SC):
                        mm = pe.transpose(tb[c][:, s * P:(s + 1) * P], xh[:, s, c * P:(c + 1) * P],
                                          K.ident[:, :])
                mm.then_inc(tmm, 1)

            def hidden(q, p, f):
                if f == 0:
                    pe.wait_ge(th, q + 1)
                    pe.wait_ge(tl, q + 1)
                if f >= 2 or not first(q, 1):
                    pe.wait_ge(hfs, q * FC + f - 1)
                k = 0
                for part in range(2):
                    for c in range(DC):
                        mm = pe.matmul(hb[f % 2][:, :], wf[:, c, f * P:(f + 1) * P], xT[:, p, part, c, :],
                                       start=k == 0, stop=k == 3)
                        k += 1
                mm.then_inc(hmm, 1)

            def back(q, p, f):
                pe.wait_ge(hl, q * FC + f + 1)
                if f == 0 and not first(q, 2):
                    pe.wait_ge(ys, q - 1)
                for s in range(SC):
                    for part in range(2):
                        mm = pe.matmul(y_of(p, s), hT[:, f % RH, part, s * P:(s + 1) * P], wp[:, f, :],
                                       start=f == 0 and part == 0 and s % 2 == 0,
                                       stop=f == FC - 1 and part == 1 and s % 2 == 1)
                mm.then_inc(used, 1)

            def sums(q, p):
                pe.wait_ge(summed1, (q + 1) * FC)
                pe.wait_ge(summed2, (q + 1) * FC)
                for k in range(2):
                    for s in range(SC):
                        mm = pe.matmul(tb[0][:, k * SC + s:k * SC + s + 1], s12[:, p, k, s * P:(s + 1) * P],
                                       K.ones[:, 0:1], start=True, stop=True)
                mm.then_inc(sum_mm, 1)

            turn(0)
            for q, p, h in steps(pe, nq):
                for f in range(FC):
                    hidden(q, p, f)
                    if f >= LAG:
                        back(q, p, f - LAG)
                    elif not first(q, 1):
                        back(q - 1, 1 - p, f + FC - LAG)
                    if f == 2 and not first(q, 1):
                        sums(q - 1, 1 - p)
                    if f == 4 and not last(q, nq, 1):
                        turn(q + 1)
            for f in range(FC - LAG, FC):
                back(nq - 1, 1, f)
            sums(nq - 1, 1)

        @block.scalar
        def _(act):
            def high(q, p):
                act.wait_ge(tmm, q + 1)
                if not first(q, 2):
                    act.wait_ge(hmm, (q - 1) * FC)
                for c in range(DC):
                    cp = act.activation(xT[:, p, 0, c, :], tb[c][:, :], ACT.Copy)
                cp.then_inc(th, 1)

            def chunk(q, f):
                act.wait_ge(hmm, q * FC + f + 1)
                if f >= RG or not first(q, 1):
                    act.wait_ge(hl, q * FC + f - RG + 1)
                    act.wait_ge(summed1, q * FC + f - RG + 1)
                    act.wait_ge(summed2, q * FC + f - RG + 1)
                act.activation(hf[:, f % RG, :],
                               hb[f % 2][:, :], ACT.Gelu).then_inc(hfs, 1)
                act.wait_ge(hfs, q * FC + f + 1)
                if f >= RH or not first(q, 1):
                    act.wait_ge(used, q * FC + f - RH + 1)
                act.activation(hT[:, f % RH, 0, :], hf[:, f % RG, :], ACT.Copy, scale=lnw[:, f:f + 1]
                               ).then_inc(hh, 1)
                act.activation(hq[:, f % RG, :], hf[:, f % RG, :], ACT.Square).then_inc(hqs, 1)

            def y_out(q, p):
                act.wait_ge(used, (q + 1) * FC)
                if not first(q, 1):
                    act.wait_ge(o1, SC * q)
                for s in range(SC):
                    cp = act.activation(ysb[:, s, :], y_of(p, s), ACT.Copy)
                cp.then_inc(ys, 1)

            high(0, 0)
            for q, p, h in steps(act, nq):
                for f in range(FC):
                    if f == 6 and not last(q, nq, 1):
                        high(q + 1, 1 - p)
                    chunk(q, f)
                    if f == 2 and not first(q, 1):
                        y_out(q - 1, 1 - p)
            y_out(nq - 1, 1)

        @block.gpsimd
        def _(pool):
            half4 = K.half[:, 0:1].broadcast_to([P, SC])

            def deviation(q):
                pool.wait_ge(mvs, SC * (q + 1))
                pool.sem_inc(K.passed, 1)
                pool.tensor_scalar(ve[:, :], mv[:, :, 1], LN_EPS, 1.0, ALU.add, ALU.mult).then_inc(ves, 1)
                pool.wait_ge(ves, q + 1)
                if not first(q, 1):
                    pool.wait_ge(xhs, q)
                pool.tensor_tensor(rs[:, :], ve[:, :], half4, ALU.pow).then_inc(rss, 1)

            def chunk(q, p, f):
                if f == 0:
                    return
                if f == 1 and not first(q, 2):
                    pool.wait_ge(sum_mm, q - 1)
                pool.wait_ge(hqs, q * FC + f + 1)
                if f > 1:
                    pool.wait_ge(summed2, q * FC + f)
                pool.tensor_tensor(s12[:, p, 1, :], hq[:, 0, :] if f == 1 else s12[:, p, 1, :],
                                   hq[:, f % RG, :], ALU.add).then_inc(summed2, 2 if f == 1 else 1)

            def deviation2(q):
                pool.wait_ge(vars_, q + 1)
                pool.sem_inc(K.passed, 1)
                pool.tensor_scalar(ve2[:, :], var[:, :], LN_EPS, 1.0, ALU.add, ALU.mult).then_inc(ve2s, 1)
                pool.wait_ge(ve2s, q + 1)
                if not first(q, 1):
                    pool.wait_ge(cas, q)
                pool.tensor_tensor(rs2[:, :], ve2[:, :], half4, ALU.pow).then_inc(rs2s, 1)

            def finish(q):
                for s in range(SC):
                    pool.wait_ge(o2, SC * q + s + 1)
                    pool.tensor_tensor(osb[:, s, :], osb[:, s, :], gu2[:, :], ALU.add).then_inc(o3, 1)

            deviation(0)
            for q, p, h in steps(pool, nq):
                if not last(q, nq, 1):
                    deviation(q + 1)
                for f in range(FC):
                    chunk(q, p, f)
                    if f == 2 and not first(q, 1):
                        deviation2(q - 1)
                    if f == 7 and not first(q, 1):
                        finish(q - 1)
            deviation2(nq - 1)
            finish(nq - 1)

        @block.sync
        def _(sp):
            with sp.Fori(0, nq) as q:
                sp.wait_ge(o3, SC * q + SC)
                sp.dma_start(outv[bass.ds(q, 1)].rearrange("a p s d -> p (a s) d"), osb[:, :, :]
                             ).then_inc(stored, 16)
            sp.wait_ge(stored, 16 * nq)

        @block.vector
        def _(dve):
            def row(q, s):
                return K.xres[:, bass.ds((q * SC + s) * D, D)]

            def stats(q):
                for s in range(SC):
                    dve.sem_inc(K.passed, 1)
                    dve.bn_stats(st[:, s, :], row(q, s)).then_inc(bns, 1)
                if not first(q, 1):
                    dve.wait_ge(ves, q)
                for s in range(SC):
                    dve.wait_ge(bns, SC * q + s + 1)
                    dve.sem_inc(K.passed, 1)
                    dve.bn_aggr(mv[:, s, :], st[:, s, :]).then_inc(mvs, 1)

            def normalise(q):
                dve.wait_ge(rss, q + 1)
                if not first(q, 1):
                    dve.wait_ge(tmm, q)
                for s in range(SC):
                    ins = dve.tensor_scalar(xh[:, s, :], row(q, s), mv[:, s, 0:1], rs[:, s:s + 1],
                                            ALU.subtract, ALU.mult)
                ins.then_inc(xhs, 1)

            def low_part(q, p):
                dve.wait_ge(th, q + 1)
                for c in range(DC):
                    ins = dve.tensor_tensor(xT[:, p, 1, c, :], tb[c][:, :], xT[:, p, 0, c, :], ALU.subtract)
                ins.then_inc(tl, 1)

            def chunk(q, p, f):
                dve.wait_ge(hh, q * FC + f + 1)
                dve.scalar_tensor_tensor(hT[:, f % RH, 1, :], hf[:, f % RG, :], lnw[:, f:f + 1],
                                         hT[:, f % RH, 0, :], ALU.mult, ALU.subtract).then_inc(hl, 1)
                if f == 0:
                    return
                if f == 1 and not first(q, 2):
                    dve.wait_ge(sum_mm, q - 1)
                if f > 1:
                    dve.wait_ge(summed1, q * FC + f)
                dve.tensor_tensor(s12[:, p, 0, :], hf[:, 0, :] if f == 1 else s12[:, p, 0, :],
                                  hf[:, f % RG, :], ALU.add).then_inc(summed1, 2 if f == 1 else 1)

            def moments(q):
                dve.wait_ge(sum_mm, q + 1)
                dve.tensor_scalar(m12[:, :], tb[0][:, 0:2 * SC], 1.0 / FF, None, ALU.mult).then_inc(m12s, 1)
                dve.wait_ge(m12s, q + 1)
                dve.tensor_tensor(msq[:, :], m12[:, 0:SC], m12[:, 0:SC], ALU.mult).then_inc(msqs, 1)
                dve.wait_ge(msqs, q + 1)
                dve.tensor_tensor(var[:, :], m12[:, SC:2 * SC], msq[:, :], ALU.subtract).then_inc(vars_, 1)

            def add(q):
                dve.wait_ge(rs2s, q + 1)
                dve.tensor_scalar(ca[:, :], rs2[:, :], g, None, ALU.mult).then_inc(cas, 1)
                dve.wait_ge(cas, q + 1)
                dve.scalar_tensor_tensor(cb[:, :], ca[:, :], -1.0, m12[:, 0:SC], ALU.mult, ALU.mult
                                         ).then_inc(cbs, 1)
                dve.wait_ge(ys, q + 1)
                dve.wait_ge(cbs, q + 1)
                if not first(q, 1):
                    dve.wait_ge(stored, 16 * q)

            def add_rows(q, rows):
                for s in rows:
                    dve.scalar_tensor_tensor(osb[:, s, :], ysb[:, s, :], ca[:, s:s + 1], row(q, s),
                                             ALU.mult, ALU.add).then_inc(o1, 1)
                for s in rows:
                    dve.wait_ge(o1, SC * q + s + 1)
                    dve.scalar_tensor_tensor(osb[:, s, :], u1[:, :], cb[:, s:s + 1], osb[:, s, :],
                                             ALU.mult, ALU.add).then_inc(o2, 1)

            stats(0)
            normalise(0)
            low_part(0, 0)
            for q, p, h in steps(dve, nq):
                for f in range(FC):
                    if f == 1 and not last(q, nq, 1):
                        stats(q + 1)
                    if f == 3 and not last(q, nq, 1):
                        normalise(q + 1)
                    if f == 3 and not first(q, 1):
                        moments(q - 1)
                    if f == 5 and not first(q, 1):
                        add(q - 1)
                        add_rows(q - 1, (0, 1))
                    if f == 7 and not first(q, 1):
                        add_rows(q - 1, (2, 3))
                    if f == 6 and not last(q, nq, 1):
                        low_part(q + 1, 1 - p)
                    chunk(q, p, f)
            moments(nq - 1)
            add(nq - 1)
            add_rows(nq - 1, range(SC))


def build(nc, K):
    with ExitStack() as ctx:
        setup(nc, ctx, K)
        with ExitStack() as routing:
            K.logits = routing.enter_context(nc.sbuf_tensor("logits", [P, K.n, E], F32))
            with ExitStack() as stage:
                cross_attention(nc, stage, K)
                end_stage(nc, K)
            with ExitStack() as stage:
                assign_slots(nc, stage, K)
                end_stage(nc, K)
        ternary_store(nc, ctx, K)
        with ExitStack() as weights:
            expert_weights(nc, weights, K)
            with ExitStack() as stage:
                dispatch(nc, stage, K)
                end_stage(nc, K)
            with ExitStack() as stage:
                experts(nc, stage, K)
                end_stage(nc, K)
        K.spec = ctx.enter_context(nc.sbuf_tensor("spec", [P, K.n], F32))
        with ExitStack() as stage:
            combine_and_correlate(nc, stage, K)
            end_stage(nc, K)
        with ExitStack() as stage:
            pick_delays(nc, stage, K)
            end_stage(nc, K)
        with ExitStack() as stage:
            delayed_values(nc, stage, K)
            end_stage(nc, K)
        with ExitStack() as stage:
            ternary_ffn(nc, stage, K)
            end_stage(nc, K)


_NAMES = {
    "x": "x", "ctx_1024": "ctx", "mask_Bx1x1xS2_ik0": "mask", "g_xattn": "g_xattn", "g_ffn": "g_ffn",
    "L0_xattn_Wq": "Wq0", "L0_xattn_bq": "bq0", "L0_xattn_Wk": "Wk0", "L0_xattn_bk": "bk0",
    "L0_xattn_Wv": "Wv0", "L0_xattn_bv": "bv0", "L0_xattn_Wo": "Wo0", "L0_xattn_bo": "bo0",
    "L0_ffn_Wr": "Wr", "L0_ffn_W1": "W1", "L0_ffn_W2": "W2",
    "L1_xattn_Wq": "Wq1", "L1_xattn_bq": "bq1", "L1_xattn_Wk": "Wk1", "L1_xattn_bk": "bk1",
    "L1_xattn_Wv": "Wv1", "L1_xattn_bv": "bv1", "L1_xattn_Wo": "Wo1", "L1_xattn_bo": "bo1",
    "L1_ffn_W_fc": "Wfc", "L1_ffn_ln_w": "lnw", "L1_ffn_ln_b": "lnb", "L1_ffn_W_proj": "Wpr",
}


def _constants(n, cap):
    time = np.arange(P)
    freq = np.concatenate([np.arange(P // 2 + 1), np.arange(1, P // 2)])
    angle = 2 * np.pi * ((time[:, None] * freq[None, :]) % P) / P
    cosine = np.arange(P) <= P // 2
    dft = np.where(cosine[None, :], np.cos(angle), np.sin(angle))
    weight = np.where((freq == 0) | (freq == P // 2), 1.0, 2.0)[:, None] / (P * D)
    return {
        "dft": dft.astype(np.float32),
        "idft": (weight * dft.T).astype(np.float32),
        "mask_parts": np.array(MASK_PARTS, np.float32)[:, None],
        "rank": np.arange(E, 0, -1).astype(np.float32),
        "start": (np.arange(E) * cap - 1).astype(np.float32),
        "spare": (E * cap + np.arange(n)[None, :] * P + np.arange(P)[:, None]).astype(np.float32),
    }


def _program(nc, arrays, n, cap):
    K = Kernel()
    K.n, K.cap = n, cap
    K.group = max(g for g in (128, 256, 384, 512) if cap % g == 0)
    K.signals = []

    def given(*names):
        return [nc.dram_tensor(name, arrays[name].shape, mybir.dt.from_np(arrays[name].dtype),
                               kind="ExternalInput").ap() for name in names]

    K.x, K.ctx, K.mask, K.g_xattn, K.g_ffn = given("x", "ctx", "mask", "g_xattn", "g_ffn")
    K.Wq0, K.Wk0, K.Wv0, K.Wo0 = given("Wq0", "Wk0", "Wv0", "Wo0")
    K.bq0, K.bk0, K.bv0, K.bo0 = given("bq0", "bk0", "bv0", "bo0")
    K.Wr, K.W1, K.W2 = given("Wr", "W1", "W2")
    K.Wq1, K.Wk1, K.Wv1, K.Wo1 = given("Wq1", "Wk1", "Wv1", "Wo1")
    K.bq1, K.bk1, K.bv1, K.bo1 = given("bq1", "bk1", "bv1", "bo1")
    K.Wfc, K.lnw, K.lnb, K.Wpr = given("Wfc", "lnw", "lnb", "Wpr")
    K.dft, K.idft, K.mask_parts = given("dft", "idft", "mask_parts")
    K.rank, K.start, K.spare = given("rank", "start", "spare")
    K.out = nc.dram_tensor("out", (n, P, D), F32, kind="ExternalOutput").ap()
    K.disp = nc.dram_tensor("disp", (E * cap + n * P, D), F32, kind="Internal").ap()
    K.eout = nc.dram_tensor("eout", (E * cap, D), F32, kind="Internal").ap()
    K.circ = nc.dram_tensor("circ", (n, 2 * P), F32, kind="Internal").ap()
    build(nc, K)


def kernel(**inputs):
    import concourse.bacc as _bacc
    from concourse.bass_utils import run_bass_kernel_spmd as _run

    nc = _bacc.Bacc("TRN2", target_bir_lowering=False, num_devices=1)
    arrays = {short: np.ascontiguousarray(inputs[name]) for name, short in _NAMES.items()}
    n = arrays["x"].shape[0]
    cap = int(1.25 * n * P / E)
    arrays.update(_constants(n, cap))
    _program(nc, arrays, n, cap)
    return _run(nc, [arrays], core_ids=[0]).results[0]["out"]
```
